# Optimizing a Trainium2 kernel written in Bass

```python
import numpy as np
import jax
import jax.numpy as jnp

def _softmax(x, axis=-1):
    return jax.nn.softmax(x, axis=axis)

def _gelu(x):
    return jax.nn.gelu(x, approximate=True)

def _silu(x):
    return jax.nn.silu(x)

def _sigmoid(x):
    return jax.nn.sigmoid(x)

def _layernorm(x, axis=-1, eps=1e-05):
    m = jnp.mean(x, axis=axis, keepdims=True)
    v = jnp.var(x, axis=axis, keepdims=True)
    return (x - m) / jnp.sqrt(v + eps)

def _scatter_add(tgt, idx, src, axis=0):
    return tgt.at[idx].add(src)

def _segment_sum(src, seg, n):
    return jax.ops.segment_sum(src, seg, n)
kernel_name = 'mk_metaformer_d2_conv_nhwc128_r4_13f1d5'

def setup_inputs(seed: int=0):
    np.random.seed(seed)
    _w = jnp.asarray

    def _rec_inputs():
        import jax
        import jax.numpy as jnp
        _gk = jax.random.key(seed)
        x = -0.000125 + 0.9999 * jax.random.normal(jax.random.fold_in(_gk, 1), (1, 128, 128, 32), jnp.float32)
        return x
    x = _rec_inputs()

    def _L0_conv_setup():
        import jax, jax.numpy as jnp
        import numpy as np
        EPS = 1e-05

        def _layernorm(x, w, b):
            mu = jnp.mean(x, axis=-1, keepdims=True)
            var = jnp.mean(jnp.square(x - mu), axis=-1, keepdims=True)
            return (x - mu) * jax.lax.rsqrt(var + EPS) * w + b
        key = jax.random.key(seed)
        ks = jax.random.split(key, 8)
        B, N, D = (1, 128, 32)
        x = jax.random.normal(ks[0], (B, N, N, D), dtype=jnp.float32)
        mask = jnp.round(jax.random.uniform(ks[1], (B, N, N), dtype=jnp.float32) * 0.6 + 0.4)
        ln1_w = jnp.ones((D,), jnp.float32)
        ln1_b = jnp.zeros((D,), jnp.float32)
        ln2_w = jnp.ones((D // 2,), jnp.float32)
        ln2_b = jnp.zeros((D // 2,), jnp.float32)
        sd = 1.0 / np.sqrt(D)
        pi_w = jax.random.normal(ks[2], (D, D), jnp.float32) * sd
        pi_b = jnp.zeros((D,), jnp.float32)
        gi_w = jax.random.normal(ks[3], (D, D), jnp.float32) * sd
        gi_b = jnp.ones((D,), jnp.float32)
        sd2 = 1.0 / np.sqrt(D // 2)
        po_w = jax.random.normal(ks[4], (D // 2, D), jnp.float32) * sd2
        po_b = jnp.zeros((D,), jnp.float32)
        go_w = jax.random.normal(ks[5], (D // 2, D), jnp.float32) * sd2
        go_b = jnp.ones((D,), jnp.float32)
        return {'x': x, 'mask': mask, 'ln1_w': ln1_w, 'ln1_b': ln1_b, 'pi_w': pi_w, 'pi_b': pi_b, 'gi_w': gi_w, 'gi_b': gi_b, 'ln2_w': ln2_w, 'ln2_b': ln2_b, 'po_w': po_w, 'po_b': po_b, 'go_w': go_w, 'go_b': go_b}
    _L0_conv_all = _L0_conv_setup()
    _L0_conv_in = {k: v for k, v in _L0_conv_all.items() if k in ('mask', 'ln1_w', 'ln1_b', 'pi_w', 'pi_b', 'gi_w', 'gi_b', 'ln2_w', 'ln2_b', 'po_w', 'po_b', 'go_w', 'go_b')}
    del _L0_conv_all

    def _L0_ffn_setup():
        import jax, jax.numpy as jnp
        import numpy as np
        BN_EPS = 1e-05
        key = jax.random.key(seed)
        k1, k2, k3 = jax.random.split(key, 3)
        B, T, I, H = (16, 512, 32, 32)
        x = jax.random.normal(k1, (B, T, I), dtype=jnp.float32)
        W = jax.random.normal(k2, (H, I), dtype=jnp.float32) * (1.0 / np.sqrt(I))
        V = jnp.linalg.qr(jax.random.normal(k3, (H, H), dtype=jnp.float32))[0]
        gamma = jnp.ones((H,), dtype=jnp.float32)
        beta = jnp.zeros((H,), dtype=jnp.float32)
        return {'x': x, 'W': W, 'V': V, 'gamma': gamma, 'beta': beta}
    _L0_ffn_all = _L0_ffn_setup()
    _L0_ffn_in = {k: v for k, v in _L0_ffn_all.items() if k in ('W', 'V', 'gamma', 'beta')}
    del _L0_ffn_all

    def _L1_conv_setup():
        import jax, jax.numpy as jnp
        import numpy as np
        EPS = 1e-05

        def _layer_norm(x, w, b):
            mu = jnp.mean(x, axis=-1, keepdims=True)
            var = jnp.var(x, axis=-1, keepdims=True)
            return (x - mu) * jax.lax.rsqrt(var + EPS) * w + b
        key = jax.random.key(seed)
        ks = jax.random.split(key, 8)
        B, N, CZ, CH = (1, 128, 32, 32)
        s = 0.02
        return {'z': jax.random.normal(ks[0], (B, N, N, CZ), dtype=jnp.float32), 'mask': jnp.ones((B, N, N), dtype=jnp.float32), 'ln_in_w': jnp.ones((CZ,), jnp.float32), 'ln_in_b': jnp.zeros((CZ,), jnp.float32), 'w_ap': jax.random.normal(ks[1], (CZ, CH), jnp.float32) * s, 'b_ap': jnp.zeros((CH,), jnp.float32), 'w_ag': jax.random.normal(ks[2], (CZ, CH), jnp.float32) * s, 'b_ag': jnp.ones((CH,), jnp.float32), 'w_bp': jax.random.normal(ks[3], (CZ, CH), jnp.float32) * s, 'b_bp': jnp.zeros((CH,), jnp.float32), 'w_bg': jax.random.normal(ks[4], (CZ, CH), jnp.float32) * s, 'b_bg': jnp.ones((CH,), jnp.float32), 'ln_out_w': jnp.ones((CH,), jnp.float32), 'ln_out_b': jnp.zeros((CH,), jnp.float32), 'w_z': jax.random.normal(ks[5], (CH, CZ), jnp.float32) * s, 'b_z': jnp.zeros((CZ,), jnp.float32), 'w_g': jax.random.normal(ks[6], (CZ, CZ), jnp.float32) * s, 'b_g': jnp.ones((CZ,), jnp.float32)}
    _L1_conv_all = _L1_conv_setup()
    _L1_conv_in = {k: v for k, v in _L1_conv_all.items() if k in ('mask', 'ln_in_w', 'ln_in_b', 'w_ap', 'b_ap', 'w_ag', 'b_ag', 'w_bp', 'b_bp', 'w_bg', 'b_bg', 'ln_out_w', 'ln_out_b', 'w_z', 'b_z', 'w_g', 'b_g')}
    del _L1_conv_all

    def _L1_ffn_setup():
        import jax, jax.numpy as jnp
        import numpy as np
        B, N, D, C, E, K = (8, 2048, 32, 32, 8, 2)
        key = jax.random.key(seed)
        k0, k1, k2 = jax.random.split(key, 3)
        x = jax.random.normal(k0, (B, N, D), dtype=jnp.float32)
        router_w = jax.random.normal(k1, (D, E), dtype=jnp.float32) * 0.05
        router_b = jnp.zeros((E,), dtype=jnp.float32)
        expert_w = jax.random.normal(k2, (E, D, C), dtype=jnp.float32) * (1.0 / np.sqrt(D))
        expert_b = jnp.zeros((E, C), dtype=jnp.float32)
        return {'x': x, 'router_w': router_w, 'router_b': router_b, 'expert_w': expert_w, 'expert_b': expert_b}
    _L1_ffn_all = _L1_ffn_setup()
    _L1_ffn_in = {k: v for k, v in _L1_ffn_all.items() if k in ('router_w', 'router_b', 'expert_w', 'expert_b')}
    del _L1_ffn_all
    return {'x': x, 'L0_conv_mask': _L0_conv_in['mask'], 'L0_conv_ln1_w': _L0_conv_in['ln1_w'], 'L0_conv_ln1_b': _L0_conv_in['ln1_b'], 'L0_conv_pi_w': _L0_conv_in['pi_w'], 'L0_conv_pi_b': _L0_conv_in['pi_b'], 'L0_conv_gi_w': _L0_conv_in['gi_w'], 'L0_conv_gi_b': _L0_conv_in['gi_b'], 'L0_conv_ln2_w': _L0_conv_in['ln2_w'], 'L0_conv_ln2_b': _L0_conv_in['ln2_b'], 'L0_conv_po_w': _L0_conv_in['po_w'], 'L0_conv_po_b': _L0_conv_in['po_b'], 'L0_conv_go_w': _L0_conv_in['go_w'], 'L0_conv_go_b': _L0_conv_in['go_b'], 'L0_ffn_W': _L0_ffn_in['W'], 'L0_ffn_V': _L0_ffn_in['V'], 'L0_ffn_gamma': _L0_ffn_in['gamma'], 'L0_ffn_beta': _L0_ffn_in['beta'], 'L1_conv_mask': _L1_conv_in['mask'], 'L1_conv_ln_in_w': _L1_conv_in['ln_in_w'], 'L1_conv_ln_in_b': _L1_conv_in['ln_in_b'], 'L1_conv_w_ap': _L1_conv_in['w_ap'], 'L1_conv_b_ap': _L1_conv_in['b_ap'], 'L1_conv_w_ag': _L1_conv_in['w_ag'], 'L1_conv_b_ag': _L1_conv_in['b_ag'], 'L1_conv_w_bp': _L1_conv_in['w_bp'], 'L1_conv_b_bp': _L1_conv_in['b_bp'], 'L1_conv_w_bg': _L1_conv_in['w_bg'], 'L1_conv_b_bg': _L1_conv_in['b_bg'], 'L1_conv_ln_out_w': _L1_conv_in['ln_out_w'], 'L1_conv_ln_out_b': _L1_conv_in['ln_out_b'], 'L1_conv_w_z': _L1_conv_in['w_z'], 'L1_conv_b_z': _L1_conv_in['b_z'], 'L1_conv_w_g': _L1_conv_in['w_g'], 'L1_conv_b_g': _L1_conv_in['b_g'], 'L1_ffn_router_w': _L1_ffn_in['router_w'], 'L1_ffn_router_b': _L1_ffn_in['router_b'], 'L1_ffn_expert_w': _L1_ffn_in['expert_w'], 'L1_ffn_expert_b': _L1_ffn_in['expert_b']}

def reference(x, L0_conv_mask, L0_conv_ln1_w, L0_conv_ln1_b, L0_conv_pi_w, L0_conv_pi_b, L0_conv_gi_w, L0_conv_gi_b, L0_conv_ln2_w, L0_conv_ln2_b, L0_conv_po_w, L0_conv_po_b, L0_conv_go_w, L0_conv_go_b, L0_ffn_W, L0_ffn_V, L0_ffn_gamma, L0_ffn_beta, L1_conv_mask, L1_conv_ln_in_w, L1_conv_ln_in_b, L1_conv_w_ap, L1_conv_b_ap, L1_conv_w_ag, L1_conv_b_ag, L1_conv_w_bp, L1_conv_b_bp, L1_conv_w_bg, L1_conv_b_bg, L1_conv_ln_out_w, L1_conv_ln_out_b, L1_conv_w_z, L1_conv_b_z, L1_conv_w_g, L1_conv_b_g, L1_ffn_router_w, L1_ffn_router_b, L1_ffn_expert_w, L1_ffn_expert_b):
    import jax
    import jax.numpy as jnp

    def _L0_conv_ref(x, mask, ln1_w, ln1_b, pi_w, pi_b, gi_w, gi_b, ln2_w, ln2_b, po_w, po_b, go_w, go_b):
        import jax, jax.numpy as jnp
        import numpy as np
        EPS = 1e-05

        def _layernorm(x, w, b):
            mu = jnp.mean(x, axis=-1, keepdims=True)
            var = jnp.mean(jnp.square(x - mu), axis=-1, keepdims=True)
            return (x - mu) * jax.lax.rsqrt(var + EPS) * w + b
        h = _layernorm(x, ln1_w, ln1_b)
        pi_out = h @ pi_w + pi_b
        gi_logits = h @ gi_w + gi_b
        g = pi_out * jax.nn.sigmoid(gi_logits) * mask[..., None]
        a1, b1, a2, b2 = jnp.split(g, 4, axis=-1)
        x1 = jnp.einsum('bikd,bjkd->bijd', a1, b1)
        x2 = jnp.einsum('bkid,bkjd->bijd', a2, b2)
        t = jnp.concatenate([x1, x2], axis=-1)
        t = _layernorm(t, ln2_w, ln2_b)
        po_out = t @ po_w + po_b
        go_logits = t @ go_w + go_b
        return po_out * jax.nn.sigmoid(go_logits) * mask[..., None]

    def _L0_ffn_ref(x, W, V, gamma, beta):
        import jax, jax.numpy as jnp
        import numpy as np
        BN_EPS = 1e-05
        B, T, H = (x.shape[0], x.shape[1], W.shape[0])
        Wx = jnp.einsum('bti,hi->bth', x, W)
        flat = Wx.reshape(B * T, H)
        mean = jnp.mean(flat, axis=0)
        var = jnp.var(flat, axis=0)
        Wx = ((flat - mean) * jax.lax.rsqrt(var + BN_EPS) * gamma + beta).reshape(B, T, H)
        Vt = V.T

        def step(yt, wx_t):
            yt = jax.nn.sigmoid(wx_t + yt @ Vt)
            return (yt, yt)
        y0 = jnp.zeros((B, H), dtype=Wx.dtype)
        _, ys = jax.lax.scan(step, y0, jnp.swapaxes(Wx, 0, 1))
        return jnp.swapaxes(ys, 0, 1)

    def _L1_conv_ref(z, mask, ln_in_w, ln_in_b, w_ap, b_ap, w_ag, b_ag, w_bp, b_bp, w_bg, b_bg, ln_out_w, ln_out_b, w_z, b_z, w_g, b_g):
        import jax, jax.numpy as jnp
        import numpy as np
        EPS = 1e-05

        def _layer_norm(x, w, b):
            mu = jnp.mean(x, axis=-1, keepdims=True)
            var = jnp.var(x, axis=-1, keepdims=True)
            return (x - mu) * jax.lax.rsqrt(var + EPS) * w + b
        m = mask[..., None]
        zn = _layer_norm(z, ln_in_w, ln_in_b)
        a = m * jax.nn.sigmoid(zn @ w_ag + b_ag) * (zn @ w_ap + b_ap)
        b = m * jax.nn.sigmoid(zn @ w_bg + b_bg) * (zn @ w_bp + b_bp)
        p = jnp.einsum('bikc,bjkc->bijc', a, b)
        x = _layer_norm(p, ln_out_w, ln_out_b) @ w_z + b_z
        g = jax.nn.sigmoid(zn @ w_g + b_g)
        return x * g

    def _L1_ffn_ref(x, router_w, router_b, expert_w, expert_b):
        import jax, jax.numpy as jnp
        import numpy as np
        B, N, D, C, E, K = (8, 2048, 32, 32, 8, 2)
        router_probs = jax.nn.softmax(x @ router_w + router_b, axis=-1)
        top_p, top_i = jax.lax.top_k(router_probs, K)
        top_p = top_p / jnp.sum(top_p, axis=-1, keepdims=True)
        expert_out = jnp.einsum('bnd,edc->bnec', x, expert_w) + expert_b
        gathered = jnp.take_along_axis(expert_out, top_i[..., None], axis=2)
        return jnp.einsum('bnk,bnkc->bnc', top_p, gathered)

    def _gn(v, G=32, eps=1e-05):
        B_, H_, W_, C_ = v.shape
        g = v.reshape(B_, H_, W_, G, C_ // G)
        m = jnp.mean(g, axis=(1, 2, 4), keepdims=True)
        s = jnp.var(g, axis=(1, 2, 4), keepdims=True)
        return ((g - m) / jnp.sqrt(s + eps)).reshape(v.shape)

    def _ln_c(v, eps=1e-06):
        m = jnp.mean(v, axis=-1, keepdims=True)
        s = jnp.var(v, axis=-1, keepdims=True)
        return (v - m) / jnp.sqrt(s + eps)

    def _ln_t(v, eps=1e-05):
        m = jnp.mean(v, axis=-1, keepdims=True)
        s = jnp.var(v, axis=-1, keepdims=True)
        return (v - m) / jnp.sqrt(s + eps)

    def _to_tokens(v):
        B_, H_, W_, C_ = v.shape
        return v.reshape(B_, H_ * W_, C_)

    def _from_tokens(t, like):
        return t.reshape(like.shape)
    x = x + _L0_conv_ref(_ln_c(x), L0_conv_mask, L0_conv_ln1_w, L0_conv_ln1_b, L0_conv_pi_w, L0_conv_pi_b, L0_conv_gi_w, L0_conv_gi_b, L0_conv_ln2_w, L0_conv_ln2_b, L0_conv_po_w, L0_conv_po_b, L0_conv_go_w, L0_conv_go_b)
    t = _to_tokens(x)
    t = t + _L0_ffn_ref(_ln_t(t), L0_ffn_W, L0_ffn_V, L0_ffn_gamma, L0_ffn_beta)
    x = _from_tokens(t, x)
    x = x + _L1_conv_ref(_ln_c(x), L1_conv_mask, L1_conv_ln_in_w, L1_conv_ln_in_b, L1_conv_w_ap, L1_conv_b_ap, L1_conv_w_ag, L1_conv_b_ag, L1_conv_w_bp, L1_conv_b_bp, L1_conv_w_bg, L1_conv_b_bg, L1_conv_ln_out_w, L1_conv_ln_out_b, L1_conv_w_z, L1_conv_b_z, L1_conv_w_g, L1_conv_b_g)
    t = _to_tokens(x)
    t = t + _L1_ffn_ref(_ln_t(t), L1_ffn_router_w, L1_ffn_router_b, L1_ffn_expert_w, L1_ffn_expert_b)
    x = _from_tokens(t, x)
    return x

_drawn_inputs = setup_inputs


def setup_inputs(seed=0):
    import zlib

    import numpy as np

    out = dict(_drawn_inputs(seed))
    spreads = {'L0_conv_ln1_w': (1.0, 0.2),
     'L0_conv_ln1_b': (0.0, 0.1),
     'L0_conv_pi_b': (0.0, 0.1),
     'L0_conv_gi_b': (1.0, 0.2),
     'L0_conv_ln2_w': (1.0, 0.2),
     'L0_conv_ln2_b': (0.0, 0.1),
     'L0_conv_po_b': (0.0, 0.1),
     'L0_conv_go_b': (1.0, 0.2),
     'L0_ffn_gamma': (1.0, 0.2),
     'L0_ffn_beta': (0.0, 0.1),
     'L1_conv_ln_in_w': (1.0, 0.6),
     'L1_conv_ln_in_b': (0.0, 0.1),
     'L1_conv_b_ap': (0.0, 0.1),
     'L1_conv_b_ag': (1.0, 0.6),
     'L1_conv_b_bp': (0.0, 0.1),
     'L1_conv_b_bg': (1.0, 0.6),
     'L1_conv_ln_out_w': (1.0, 0.2),
     'L1_conv_ln_out_b': (0.0, 0.1),
     'L1_conv_b_z': (0.0, 0.1),
     'L1_conv_b_g': (1.0, 0.6),
     'L1_ffn_router_b': (0.0, 0.1),
     'L1_ffn_expert_b': (0.0, 0.1)}
    factors = {'L1_conv_w_ag': 4.686, 'L1_conv_w_bg': 5.508, 'L1_conv_w_g': 3.034}
    for name, (base, spread) in spreads.items():
        noise = np.random.default_rng([zlib.crc32(name.encode()), seed]).standard_normal(out[name].shape)
        drawn = base * np.exp(spread * noise) if base else spread * noise
        out[name] = jnp.asarray(drawn.astype(out[name].dtype))
    for name, factor in factors.items():
        out[name] = (out[name] * factor).astype(out[name].dtype)
    return out
```

```python
from contextlib import ExitStack

import concourse.bass as bass
from concourse import mybir

ALU = mybir.AluOpType
ACT = mybir.ActivationFunctionType
AX = mybir.AxisListType
F32 = mybir.dt.float32
BF16 = mybir.dt.bfloat16
I32 = mybir.dt.int32

P = 128
C = 32
D2 = C // 2
S = P // C
TILES = P // S
GROUP = 4
GROUPS = TILES // GROUP
BANK = 512
EXPERTS = 8
CHUNK = 16
NCHUNKS = P * P // CHUNK
EPS_LN = 1e-5
EPS_C = 1e-6
SAME = 2.0 ** -22

RAW = {"A": (0, 64), "C": (64, 192), "G": (192, 224), "Z": (224, 256), "R": (256, 264),
       "E": (264, 520), "W": (520, 552), "V": (552, 584), "gamma": (584, 585), "beta": (585, 586)}
NRAW = 586
LN_OF = {"A": 0, "C": 1, "G": 1, "Z": 2, "R": None, "E": None}


def build(nc, a, out):
    ctx = ExitStack()
    with ctx:
        def sb(name, shape, dt=F32):
            return ctx.enter_context(nc.sbuf_tensor(name, shape, dt))

        def sem(name):
            return ctx.enter_context(nc.semaphore(name))

        x = sb("x", [P, P, C])
        centred = sb("centred", [P, P * C])
        squares = sb("squares", [P, P * C])
        gated = sb("gated", [P, 2 * C, P])
        gated_t = sb("gated_t", [P, 2 * C, P])
        prod = sb("prod", [P, C * P])
        out_gate = sb("out_gate", [P, P, C])
        xn = sb("xn", [P, 2, GROUP, P])
        xt = sb("xt", [P, 2, GROUP, P])
        sg = sb("sg", [P, 2, BANK])
        mask_a = sb("mask_a", [P, P])
        mask_c = sb("mask_c", [P, P])
        sums = sb("sums", [P, P])
        mean = sb("mean", [P, P])
        var = sb("var", [P, P])
        sd = sb("sd", [P, P])
        rstd = sb("rstd", [P, P])
        newton = sb("newton", [P, P])
        rstd2 = sb("rstd2", [P, P])
        x_cm = gated[:, 0:C, :]
        y_cm = gated_t[:, 0:C, :]
        ends = sb("ends", [P, 2 * P + 1])
        xd = gated[:, 0:C, :]
        ident = sb("ident", [P, P])
        blk4 = sb("blk4", [P, S])
        blk8 = sb("blk8", [P, 2 * S])
        rep32 = sb("rep32", [C, P])
        rep16 = sb("rep16", [D2, P])
        avg4 = sb("avg4", [P, P])
        raw = sb("raw", [C + 1, NRAW])
        raw_s = sb("raw_s", [C, NRAW])
        raw_o = sb("raw_o", [D2 + 1, 2 * C])
        raw_os = sb("raw_os", [D2, 2 * C])
        lnv = sb("lnv", [C, 8])
        lhs_b = sb("lhs_b", [C + 1, 5, P])
        w_a = sb("w_a", [P, 2, S, C])
        w_o = sb("w_o", [P, 2, 2 * S, C])
        w_c = sb("w_c", [P, 2, S, 2 * C])
        w_g = sb("w_g", [P, S, C])
        w_z = sb("w_z", [P, S, C])
        w_r = sb("w_r", [P, S, EXPERTS])
        w_e = sb("w_e", [P, S, EXPERTS * C])
        w_b = sb("w_b", [P, S, C])
        v_b = sb("v_b", [P, S, C])
        w_bt = sb("w_bt", [P, P])
        w_bs = sb("w_bs", [P, P])
        v_t = sb("v_t", [P, P])
        v_next = sb("v_next", [P, P])
        v_wrap = sb("v_wrap", [P, P])
        gb = sb("gb", [P, 2])
        ones_b = sb("ones_b", [P, P], BF16)
        NB = {"A": BANK, "O": BANK, "C": BANK, "G": BANK, "Z": BANK, "R": BANK, "E": 2 * BANK}
        bias = {k: sb(f"bias_{k}", [P, n], BF16) for k, n in NB.items()}
        b_full = prod[:, 0:2 * BANK]
        b_hi = sb("b_hi", [P, 2 * BANK], BF16)
        b_rest = prod[:, 2 * BANK:4 * BANK]
        b_mid = sb("b_mid", [P, 2 * BANK], BF16)
        b_rest2 = prod[:, 4 * BANK:6 * BANK]
        bst = sb("bst", [P, GROUPS, 6])
        mv = sb("mv", [P, 2])
        bn = sb("bn", [P, 12])
        diag = sb("diag", [P, P])
        dif = sb("dif", [P, 2 * P])
        dmax = sb("dmax", [P, 1])
        flag = sb("flag", [1, 2], F32)
        flag_i = sb("flag_i", [1, 1], I32)
        E8 = EXPERTS
        rank = sb("rank", [P, E8])
        lg, pr, eq, sel1, sel2, wgt = (
            gated_t[:, 8 * n:8 * n + 8, :].rearrange("p a b -> p (a b)").rearrange("p (j e) -> p j e", e=E8)
            for n in range(6))
        red = sb("red", [P, 8, P])
        mixed = prod[:, 0:2 * S * E8 * C].rearrange("p (b s e c) -> p b s e c", b=2, s=S, e=E8)

        ps = ctx.enter_context(nc.psum_tensor("ps", [P, 8 * BANK], F32))

        def bank(b, n=1):
            return ps[:, b * BANK:(b + n) * BANK]

        ld_x = [sem(f"ld_x{n}") for n in range(4)]
        ld_m = sem("ld_m")
        ld_w = sem("ld_w")
        stored = sem("stored")
        pool_const = sem("pool_const")
        consts = sem("consts")
        w_dve = sem("w_dve")
        w_pe = sem("w_pe")
        dve_step = sem("dve_step")

        halved = sem("halved")
        weighed = sem("weighed")
        bn_pe = sem("bn_pe")
        bn_dve = sem("bn_dve")
        e_turn = sem("e_turn")
        e_copy_a = sem("e_copy_a")
        e_copy_v = sem("e_copy_v")
        e_prod = sem("e_prod")
        f_turn = sem("f_turn")
        f_copy_a = sem("f_copy_a")
        f_copy_v = sem("f_copy_v")
        f_prod = sem("f_prod")
        f_kept = sem("f_kept")
        s_step = [sem(f"s_step{st}") for st in range(2)]
        s_state = [sem(f"s_state{st}") for st in range(2)]
        r_step = [sem(f"r_step{st}") for st in range(2)]
        r_state = [sem(f"r_state{st}") for st in range(2)]
        ends_kept = sem("ends_kept")
        ends_again = sem("ends_again")
        flag_turned = sem("flag_turned")
        flag_set = sem("flag_set")
        y_turn = sem("y_turn")
        y_added = sem("y_added")
        d_logits = sem("d_logits")
        d_shift = sem("d_shift")
        d_exp = sem("d_exp")
        y_final = sem("y_final")
        halves = sem("halves")
        gate_ready = sem("gate_ready")
        gate_kept = sem("gate_kept")
        bn_act = sem("bn_act")
        bn_done = sem("bn_done")
        bn_var = sem("bn_var")

        block = ctx.enter_context(nc.Block())
        steps = [0]

        def chain(eng, ins):
            steps[0] += 1
            ins.then_inc(dve_step, 1)
            eng.wait_ge(dve_step, steps[0])

        class Norm:
            def __init__(self, name, chans, scale, eps):
                self.chans, self.scale, self.eps = chans, scale, eps
                self.meaned = sem(name + "_meaned")
                self.centred = sem(name + "_centred")
                self.squared = sem(name + "_squared")
                self.varied = sem(name + "_varied")
                self.rooted = sem(name + "_rooted")
                self.done = sem(name + "_done")

        QUARTERS = 4
        QT = P // QUARTERS

        def tok(t, q, chans):
            v = t.rearrange("p (j c) -> p j c", c=chans)
            return v[:, q * QT:(q + 1) * QT, :]

        def bcast(v, n):
            return v.unsqueeze(2).to_broadcast([P, v.shape[1], n])

        def norm_dve(dve, nm, src, ready, centre=False):
            cbuf = centred[:, 0:P * nm.chans]
            sbuf = squares[:, 0:P * nm.chans]

            def second(q):
                dve.wait_ge(nm.squared, q + 1)
                dve.tensor_reduce(var[:, q * QT:(q + 1) * QT], tok(sbuf, q, nm.chans), AX.X,
                                  ALU.add).then_inc(nm.varied, 1)

            for q in range(QUARTERS):
                ready(q)
                cols = slice(q * QT, (q + 1) * QT)
                chain(dve, dve.tensor_reduce(sums[:, cols], src(q), AX.X, ALU.add))
                ins = dve.tensor_scalar(mean[:, cols], sums[:, cols], 1.0 / nm.chans, None, ALU.mult)
                ins.then_inc(nm.meaned, 1)
                if centre:
                    dve.wait_ge(nm.meaned, q + 1)
                    dve.tensor_tensor(tok(cbuf, q, nm.chans), src(q), bcast(mean[:, cols], nm.chans),
                                      ALU.subtract).then_inc(nm.centred, 1)
                if q:
                    second(q - 1)
            second(QUARTERS - 1)
            dve.wait_ge(nm.varied, QUARTERS)
            dve.tensor_scalar(sd[:, :], var[:, :], nm.scale / nm.chans, nm.eps, ALU.mult,
                              ALU.add).then_inc(nm.varied, 1)
            dve.wait_ge(nm.rooted, 1)
            chain(dve, dve.reciprocal(rstd2[:, :], var[:, :]))
            chain(dve, dve.tensor_tensor(newton[:, :], rstd2[:, :], rstd2[:, :], ALU.mult))
            chain(dve, dve.scalar_tensor_tensor(newton[:, :], newton[:, :], -0.5, sd[:, :], ALU.mult, ALU.mult))
            dve.scalar_tensor_tensor(rstd[:, :], newton[:, :], 1.5, rstd2[:, :], ALU.add,
                                     ALU.mult).then_inc(nm.done, 1)
            dve.wait_ge(nm.done, 1)

        def norm_pool(pool, nm, src):
            cbuf = centred[:, 0:P * nm.chans]
            for q in range(QUARTERS):
                pool.wait_ge(nm.meaned, q + 1)
                pool.tensor_tensor(tok(cbuf, q, nm.chans), src(q),
                                   bcast(mean[:, q * QT:(q + 1) * QT], nm.chans),
                                   ALU.subtract).then_inc(nm.centred, 1)

        def norm_act(act, nm):
            n = QT * nm.chans
            for q in range(QUARTERS):
                act.wait_ge(nm.centred, q + 1)
                act.activation(squares[:, q * n:(q + 1) * n], centred[:, q * n:(q + 1) * n],
                               ACT.Square).then_inc(nm.squared, 1)
            act.wait_ge(nm.varied, QUARTERS + 1)
            act.activation(var[:, :], sd[:, :], ACT.Sqrt).then_inc(nm.rooted, 1)

        both = dict(scale=1.0 + EPS_LN, eps=EPS_LN * EPS_C)
        n_a = Norm("na", C, **both)
        n_o = Norm("no", D2, 1.0, EPS_LN)
        n_b = Norm("nb", C, 1.0, EPS_LN)
        n_c = Norm("nc", C, **both)
        n_z = Norm("nz", C, 1.0, EPS_LN)
        n_d = Norm("nd", C, 1.0, EPS_LN)

        def x_q(q):
            return x[:, q * QT:(q + 1) * QT, :]

        def prod_q(q):
            return prod[:, :].rearrange("p (c j) -> p j c", j=P)[:, q * QT:(q + 1) * QT, :]

        class Proj:
            def __init__(self, name):
                self.scaled = sem(name + "_scaled")
                self.turned = sem(name + "_turned")
                self.copied = sem(name + "_copied")
                self.projected = sem(name + "_projected")
                self.gates = sem(name + "_gates")
                self.masked = sem(name + "_masked")
                self.used = sem(name + "_used")
                self.added = sem(name + "_added")

        p_a, p_o, p_b, p_c, p_z, p_d = (Proj(n) for n in ("pa", "po", "pb", "pc", "pz", "pd"))

        def groups(eng, head, tail, last=True):
            head(0, 0, True)
            head(1, 1, True)
            tail(0, 0, True)
            with eng.Fori(1, GROUPS // 2) as it:
                head(2 * it, 0, False)
                tail(2 * it - 1, 1, False)
                head(2 * it + 1, 1, False)
                tail(2 * it, 0, False)
            tail(GROUPS - 1, 1, False)

        def groups_ahead(eng, head, tail):
            head(0, 0, True)
            head(1, 1, True)
            for g in (2, 3):
                head(g, g % 2, False)
                tail(g - 2, g % 2, True)
            with eng.Fori(2, GROUPS // 2) as it:
                head(2 * it, 0, False)
                tail(2 * it - 2, 0, False)
                head(2 * it + 1, 1, False)
                tail(2 * it - 1, 1, False)
            tail(GROUPS - 2, 0, False)
            tail(GROUPS - 1, 1, False)

        def nothing(g, s, early):
            pass

        def scale_group(dve, pj, width):
            ntok = 16

            def f(g, s, early):
                if not early:
                    dve.wait_ge(pj.turned, g - 1)
                src = centred[:, 0:P * width].rearrange("p (g t c) -> p g t c", t=ntok, c=width)
                r = rstd[:, :].rearrange("p (g t) -> p g t", t=ntok)
                dst = xn[:, s, :, :].rearrange("p a b -> p (a b)")[:, 0:ntok * width]
                rg = r[:, bass.ds(g, 1), :].rearrange("p a t -> p (a t)")
                dve.tensor_tensor(dst.rearrange("p (t c) -> p t c", c=width),
                                  src[:, bass.ds(g, 1), :, :].rearrange("p a t c -> p (a t) c"),
                                  bcast(rg, width), ALU.mult).then_inc(pj.scaled, 1)
            return f

        def turn_group(pe, pj, tiles=GROUP):
            def f(g, s, early):
                pe.wait_ge(pj.scaled, g + 1)
                if not early:
                    pe.wait_ge(pj.copied, g - 1)
                for t in range(tiles):
                    ins = pe.transpose(bank(s)[:, t * P:(t + 1) * P], xn[:, s, t, :], ident[:, :])
                ins.then_inc(pj.turned, 1)
            return f

        def copy_group(act, pj, tiles=GROUP):
            def f(g, s, early):
                act.wait_ge(pj.turned, g + 1)
                if not early:
                    act.wait_ge(pj.projected, g - 1)
                act.activation(xt[:, s, 0:tiles, :].rearrange("p a b -> p (a b)"),
                               bank(s)[:, 0:tiles * P], ACT.Copy).then_inc(pj.copied, 1)
            return f

        @block.sync
        def _(sp):
            for q in range(QUARTERS):
                sp.dma_start(x_q(q), a["x"][0, :, q * QT:(q + 1) * QT, :]).then_inc(ld_x[q], 16)
            sp.dma_start(mask_a[:, :], a["L0_conv_mask"][0]).then_inc(ld_m, 16)
            sp.dma_start(mask_c[:, :], a["L1_conv_mask"][0]).then_inc(ld_m, 16)
            for g in range(GROUPS):
                sp.wait_ge(p_d.added, 4 * (g + 1))
                sp.dma_start(out[0, :, 16 * g:16 * g + 16, :], x[:, 16 * g:16 * g + 16, :]).then_inc(stored, 16)
            sp.wait_ge(stored, 16 * GROUPS)

        n_small = [0]

        def small(eng, dst, src):
            n_small[0] += 1
            eng.dma_start(dst, src).then_inc(ld_w, 16)

        def row(v):
            return v.rearrange("(a n) -> a n", a=1)

        def col(v):
            return v.rearrange("(n a) -> n a", a=1)

        @block.gpsimd
        def _(pool):
            k = [0]

            def then(ins):
                k[0] += 1
                ins.then_inc(pool_const, 1)
                pool.wait_ge(pool_const, k[0])

            then(pool.memset(ident[:, :], 0.0))
            then(pool.affine_select(out=ident[:, :], in_=ident[:, :], compare_op=ALU.not_equal, fill=1.0,
                                    base=0, pattern=[[-1, P]], channel_multiplier=1))
            for t, w in ((rep32, C), (rep16, D2)):
                n = P // w
                then(pool.memset(t[:, :], 0.0))
                then(pool.affine_select(out=t[:, :].rearrange("p (a b) -> p a b", b=w),
                                        in_=t[:, :].rearrange("p (a b) -> p a b", b=w),
                                        compare_op=ALU.not_equal, fill=1.0, base=0,
                                        pattern=[[0, n], [-1, w]], channel_multiplier=1))
            for t, w in ((blk4, C), (blk8, D2)):
                n = P // w
                then(pool.memset(t[:, :], 1.0))
                then(pool.affine_select(out=t[:, :], in_=t[:, :], compare_op=ALU.is_ge, fill=0.0, base=0,
                                        pattern=[[-w, n]], channel_multiplier=1))
                then(pool.affine_select(out=t[:, :], in_=t[:, :], compare_op=ALU.is_ge, fill=0.0, base=w - 1,
                                        pattern=[[w, n]], channel_multiplier=-1))
            then(pool.memset(avg4[:, :], 0.0))
            v = avg4[:, :].rearrange("p (a b) -> p a b", b=C)
            for d in range(-S + 1, S):
                then(pool.affine_select(out=v, in_=v, compare_op=ALU.not_equal, fill=1.0 / S, base=-C * d,
                                        pattern=[[-C, S], [-1, C]], channel_multiplier=1))
            for e in range(EXPERTS):
                then(pool.memset(rank[:, e:e + 1], float(EXPERTS - e)))
            then(pool.memset(ones_b[:, :], 1.0))
            then(pool.memset(v_next[:, :], 0.0))
            then(pool.memset(v_wrap[:, :], 0.0))
            then(pool.memset(ends[:, :], 0.0))
            then(pool.memset(lhs_b[:, :, :], 0.0))
            then(pool.memset(lhs_b[C:C + 1, :, :], 1.0))
            for t in bias.values():
                then(pool.memset(t[:, :], 0.0))
            pool.memset(raw[C:C + 1, :], 0.0).then_inc(consts, 1)

            norm_pool(pool, n_a, x_q)
            pool.wait_ge(ld_m, 32)

            def mask_it(pj, msk, n, half=1):
                def f(g, s, early):
                    pool.wait_ge(pj.gates, g + 1)
                    m = msk[:, :].rearrange("p (g t) -> p g t", t=16)[:, bass.ds(g, 1), :]
                    v = sg[:, s, :].rearrange("p (t o) -> p t o", o=n)
                    pool.tensor_tensor(v, v, bcast(m.rearrange("p a t -> p (a t)"), n),
                                       ALU.mult).then_inc(pj.masked, 1)
                return f

            groups(pool, mask_it(p_a, mask_a, C), nothing)

            def add_out(pj):
                def f(g, s, early):
                    pool.wait_ge(pj.used, g + 1)
                    v = x[:, :, :].rearrange("p (g t) c -> p g (t c)", t=16)[:, bass.ds(g, 1), :]
                    v = v.rearrange("p a n -> p (a n)")
                    pool.tensor_tensor(v, v, sg[:, s, :], ALU.add).then_inc(pj.added, 1)
                return f

            groups(pool, mask_it(p_o, mask_a, C), add_out(p_o))

            norm_pool(pool, n_b, x_q)

            norm_pool(pool, n_c, x_q)

            def mask_c_half(h):
                def f(g, s, early):
                    pool.wait_ge(p_c.gates, 2 * g + h + 1)
                    m = mask_c[:, :].rearrange("p (g t) -> p g t", t=8)[:, bass.ds(2 * g + h, 1), :]
                    v = sg[:, h, :].rearrange("p (t o) -> p t o", o=2 * C)
                    pool.tensor_tensor(v, v, bcast(m.rearrange("p a t -> p (a t)"), 2 * C),
                                       ALU.mult).then_inc(p_c.masked, 1)
                return f

            def mask_both(g, s, early):
                mask_c_half(0)(g, s, early)
                mask_c_half(1)(g, s, early)

            groups(pool, mask_both, nothing)
            norm_pool(pool, n_z, prod_q)
            groups(pool, add_out(p_z), nothing)

            norm_pool(pool, n_d, x_q)

            def reduce_experts(u, s):
                pool.wait_ge(p_d.used, u + 1)
                m = mixed[:, s, :, :, :]
                n = EXPERTS // 2
                for lvl in range(2):
                    n //= 2
                    pool.tensor_tensor(m[:, :, 0:n, :], m[:, :, 0:n, :], m[:, :, n:2 * n, :],
                                       ALU.add).then_inc(halved, 1)
                    pool.wait_ge(halved, 2 * u + lvl + 1)
                v = x[:, :, :].rearrange("p (u t) c -> p u t c", t=S)[:, bass.ds(u, 1), :, :]
                v = v.rearrange("p a t c -> p (a t) c")
                pool.tensor_tensor(v, v, m[:, :, 0, :], ALU.add).then_inc(p_d.added, 1)

            with pool.Fori(0, TILES // 2) as it:
                reduce_experts(2 * it, 0)
                reduce_experts(2 * it + 1, 1)


        def flat(t, J):
            return t[:, bass.ds(J, 1), :].rearrange("p a i -> p (a i)") if not isinstance(J, int) else t[:, J, :]

        def sweep_pe(pe, stepped, state, base):
            def summed(st, k, b):
                return bank(2 + 2 * st + b)[:, 0:P]

            def step(st, k, b):
                J = CHUNK * st + k
                pe.matmul(summed(st, k, b), w_bs[:, :], flat(x_cm, J), start=True, stop=False,
                          skip_group_check=True)
                pe.wait_ge(state[st], base + k)
                pe.matmul(summed(st, k, b), v_t[:, :], flat(y_cm, J - 1), start=False, stop=True,
                          skip_group_check=True).then_inc(stepped[st], 1)

            pe.matmul(summed(0, 0, 0), w_bs[:, :], x_cm[:, 0, :], start=True, stop=False,
                      skip_group_check=True)
            pe.matmul(summed(0, 0, 0), v_next[:, :], ends[:, 1:P + 1], start=False, stop=False,
                      skip_group_check=True)
            pe.matmul(summed(0, 0, 0), v_wrap[:, :], ends[:, 0:P], start=False, stop=True,
                      skip_group_check=True).then_inc(stepped[0], 1)
            pe.matmul(summed(1, 0, 0), w_bs[:, :], x_cm[:, CHUNK, :], start=True, stop=False,
                      skip_group_check=True)
            pe.matmul(summed(1, 0, 0), v_t[:, :], ends[:, P + 1:2 * P + 1], start=False, stop=True,
                      skip_group_check=True).then_inc(stepped[1], 1)
            step(0, 1, 1)
            step(1, 1, 1)
            with pe.Fori(1, CHUNK // 2) as it:
                for b in range(2):
                    for st in range(2):
                        step(st, 2 * it + b, b)

        def sweep_act(act, stepped, state, base):
            with act.Fori(0, CHUNK // 2) as it:
                for b in range(2):
                    for st in range(2):
                        act.wait_ge(stepped[st], base + 2 * it + b + 1)
                        act.activation(flat(y_cm, CHUNK * st + 2 * it + b), bank(2 + 2 * st + b)[:, 0:P],
                                       ACT.Sigmoid, bias=bn[:, 9:10]).then_inc(state[st], 1)

        def keep_ends(dve, signal):
            dve.tensor_copy(ends[:, 1:P + 1], y_cm[:, 2 * CHUNK - 1, :])
            dve.tensor_copy(ends[:, P + 1:2 * P + 1], y_cm[:, CHUNK - 1, :]).then_inc(signal, 1)

        @block.tensor
        def _(pe):
            pe.wait_ge(consts, 1)
            pe.wait_ge(w_dve, 1)
            pe.matmul(bank(0), rep32[:, :], raw_s[:, 0:BANK], start=True, stop=True)
            pe.matmul(bank(1)[:, 0:NRAW - BANK], rep32[:, :], raw_s[:, BANK:NRAW], start=True, stop=True)
            pe.matmul(bank(2)[:, 0:2 * C], rep16[:, :], raw_os[:, :], start=True, stop=True)
            for n, key in enumerate(("A", "C", "G", "Z", "R", "E")):
                lo, hi = RAW[key]
                ln = LN_OF[key]
                b = 3 if key != "E" else 4
                at = lo % BANK if key != "E" else 0
                pe.matmul(bank(b)[:, at:at + hi - lo], lhs_b[:, 4 if ln is None else ln, :], raw[:, lo:hi],
                          start=True, stop=True, skip_group_check=True)
            pe.matmul(bank(2)[:, 64:64 + 2 * C], lhs_b[0:D2 + 1, 3, :], raw_o[:, :], start=True,
                      stop=True, skip_group_check=True).then_inc(w_pe, 1)
            pe.wait_ge(w_dve, 2)
            pe.transpose(bank(5)[:, 0:P], w_b[:, :, :].rearrange("p s c -> p (s c)"), ident[:, :])
            pe.transpose(bank(5)[:, P:2 * P], v_b[:, :, :].rearrange("p s c -> p (s c)"),
                         ident[:, :]).then_inc(w_pe, 1)
            pe.wait_ge(w_dve, 3)

            def project(pj, key, mms, per, used_gap):
                def f(g, s, early):
                    pe.wait_ge(pj.copied, g + 1)
                    if not early:
                        pe.wait_ge(pj.used, g - 1)
                    for h in range(2):
                        b = bank(2 + 2 * s + h)
                        pe.matmul(b, ones_b[:, :], bias[key][:, :], start=True, stop=False,
                                  skip_group_check=True)
                        for t in range(per):
                            n = BANK // per
                            ins = pe.matmul(b[:, t * n:(t + 1) * n], xt[:, s, per * h + t, :], mms,
                                            start=False, stop=(t == per - 1), skip_group_check=True)
                    ins.then_inc(pj.projected, 1)
                return f

            groups(pe, turn_group(pe, p_a), project(p_a, "A", w_a[:, :, :, :].rearrange("p h s c -> p (h s c)"), 2, 0))
            pe.wait_ge(p_a.used, GROUPS)
            for q in range(4):
                for t in range(4):
                    ins = pe.transpose(bank(q)[:, t * P:(t + 1) * P], gated[:, 4 * q + t, :], ident[:, :])
                ins.then_inc(e_turn, 1)
            for d in range(8):
                b = bank(6 + d // 4)
                ins = pe.matmul(b[:, (d % 4) * P:(d % 4 + 1) * P], gated[:, 16 + d, :], gated[:, 24 + d, :],
                                start=True, stop=True, skip_group_check=True)
            pe.wait_ge(e_copy_a, 2)
            pe.wait_ge(e_copy_v, 2)
            for d in range(8):
                b = bank(4 + d // 4)
                ins = pe.matmul(b[:, (d % 4) * P:(d % 4 + 1) * P], gated_t[:, d, :], gated_t[:, 8 + d, :],
                                start=True, stop=True, skip_group_check=True)
            ins.then_inc(e_prod, 1)
            groups(pe, turn_group(pe, p_o, 2), project(p_o, "O", w_o[:, :, :, :].rearrange("p h s c -> p (h s c)"), 1, 0))

            def wx(g, s, early):
                pe.wait_ge(p_b.copied, g + 1)
                if not early:
                    pe.wait_ge(p_b.used, g - 1)
                v = x_cm.rearrange("p (g t) i -> p g (t i)", t=GROUP)[:, bass.ds(g, 1), :]
                pe.matmul(bank(2 + s), w_bt[:, :], v.rearrange("p a n -> p (a n)"), start=True,
                          stop=True).then_inc(p_b.projected, 1)

            groups(pe, turn_group(pe, p_b), wx)
            pe.wait_ge(bn_dve, 1)
            pe.matmul(bank(4)[:, 0:1], avg4[:, :], mv[:, 0:1], start=True, stop=True).then_inc(bn_pe, 1)
            pe.wait_ge(bn_dve, 2)
            pe.matmul(bank(4)[:, 0:1], avg4[:, :], bn[:, 2:3], start=True, stop=True).then_inc(bn_pe, 1)
            pe.wait_ge(bn_dve, 3)
            pe.matmul(bank(4)[:, 0:P], w_b[:, :, :].rearrange("p s c -> p (s c)"), diag[:, :],
                      start=True, stop=True).then_inc(bn_pe, 1)
            pe.wait_ge(bn_dve, 4)

            sweep_pe(pe, s_step, s_state, 0)
            pe.wait_ge(ends_kept, 1)
            sweep_pe(pe, s_step, s_state, CHUNK)
            pe.wait_ge(ends_kept, 2)
            pe.transpose(bank(6)[0:1, 0:P], dmax[:, :], ident[:, :]).then_inc(flag_turned, 1)
            pe.wait_ge(flag_set, 1)
            again = pe.value_load(flag_i[0:1, 0:1], min_val=0, max_val=1)
            with pe.If(again > 0):
                with pe.Fori(0, NCHUNKS - 2) as n:
                    pe.wait_ge(ends_again, n + 1)
                    sweep_pe(pe, r_step, r_state, n * CHUNK)
            pe.wait_ge(y_final, 1)
            for g in range(GROUPS):
                if g >= 4:
                    pe.wait_ge(y_added, g - 3)
                for t in range(4):
                    ins = pe.transpose(bank(4 + g % 4)[:, t * P:(t + 1) * P], y_cm[:, 4 * g + t, :], ident[:, :])
                ins.then_inc(y_turn, 1)

            def project_c(g, s, early):
                pe.wait_ge(p_c.copied, g + 1)
                pe.matmul(bank(6 + s), ones_b[:, :], bias["G"][:, :], start=True, stop=False,
                          skip_group_check=True)
                for t in range(GROUP):
                    ins = pe.matmul(bank(6 + s)[:, t * P:(t + 1) * P], xt[:, s, t, :],
                                    w_g[:, :, :].rearrange("p s c -> p (s c)"), start=False,
                                    stop=(t == 3), skip_group_check=True)
                ins.then_inc(gate_ready, 1)
                for h in range(2):
                    if not (early and s == 0):
                        pe.wait_ge(p_c.used, 2 * g + h - 1)
                    for t in range(2):
                        b = bank(2 + 2 * h + t)
                        pe.matmul(b, ones_b[:, :], bias["C"][:, :], start=True, stop=False,
                                  skip_group_check=True)
                        ins = pe.matmul(b, xt[:, s, 2 * h + t, :],
                                        w_c[:, :, :, :].rearrange("p h s c -> p (h s c)"),
                                        start=False, stop=True, skip_group_check=True)
                    ins.then_inc(halves, 1)
            groups(pe, turn_group(pe, p_c), project_c)
            pe.wait_ge(p_c.used, 2 * GROUPS)
            def c_products(q):
                b = bank(4 + q % 2)
                pe.wait_ge(f_copy_a, q + 1)
                pe.wait_ge(f_copy_v, q + 1)
                if q >= 2:
                    pe.wait_ge(f_kept, q - 1)
                for t in range(4):
                    ins = pe.matmul(b[:, t * P:(t + 1) * P], gated_t[:, 4 * q + t, :],
                                    gated_t[:, C + 4 * q + t, :], start=True, stop=True, skip_group_check=True)
                ins.then_inc(f_prod, 1)

            for q in range(8):
                if q >= 2:
                    pe.wait_ge(f_copy_a, q - 1)
                    pe.wait_ge(f_copy_v, q - 1)
                for t in range(4):
                    pe.transpose(bank(q % 2)[:, t * P:(t + 1) * P], gated[:, 4 * q + t, :], ident[:, :])
                for t in range(4):
                    ins = pe.transpose(bank(2 + q % 2)[:, t * P:(t + 1) * P], gated[:, C + 4 * q + t, :],
                                       ident[:, :])
                ins.then_inc(f_turn, 1)
                if q:
                    c_products(q - 1)
            c_products(7)

            def project_z(g, s, early):
                pe.wait_ge(p_z.copied, g + 1)
                if not early:
                    pe.wait_ge(p_z.used, g - 1)
                pe.matmul(bank(2 + s), ones_b[:, :], bias["Z"][:, :], start=True, stop=False,
                          skip_group_check=True)
                for t in range(GROUP):
                    ins = pe.matmul(bank(2 + s)[:, t * P:(t + 1) * P], xt[:, s, t, :],
                                    w_z[:, :, :].rearrange("p s c -> p (s c)"), start=False,
                                    stop=(t == 3), skip_group_check=True)
                ins.then_inc(p_z.projected, 1)

            groups(pe, turn_group(pe, p_z), project_z)

            pe.wait_ge(p_z.used, GROUPS)
            for b in range(2):
                pe.matmul(bank(2 + b), ones_b[:, :], bias["R"][:, :], start=True, stop=False,
                          skip_group_check=True)

            def router(g):
                pe.wait_ge(p_d.copied, g + 1)
                for t in range(GROUP):
                    u = GROUP * g + t
                    b = bank(2 + u // 16)
                    n = S * EXPERTS
                    ins = pe.matmul(b[:, (u % 16) * n:(u % 16 + 1) * n], xd[:, u, :],
                                    w_r[:, :, :].rearrange("p s e -> p (s e)"), start=False, stop=True,
                                    skip_group_check=True)
                if g == GROUPS - 1:
                    ins.then_inc(d_logits, 1)

            turn = turn_group(pe, p_d)
            for g in range(GROUPS):
                turn(g, g % 2, g < 2)
                if g:
                    router(g - 1)
            router(GROUPS - 1)
            for u in range(TILES):
                s = u % 2
                if u >= 2:
                    pe.wait_ge(weighed, u - 1)
                for h in range(2):
                    b = bank(4 + 2 * s + h)
                    pe.matmul(b, ones_b[:, :], bias["E"][:, h * BANK:(h + 1) * BANK], start=True, stop=False,
                              skip_group_check=True)
                    ins = pe.matmul(b, xd[:, u, :],
                                    w_e[:, :, :].rearrange("p s n -> p (s n)")[:, h * BANK:(h + 1) * BANK],
                                    start=False, stop=True, skip_group_check=True)
                ins.then_inc(p_d.projected, 1)


        @block.scalar
        def _(act):
            small(act, raw[0:C, 0:C], a["L0_conv_pi_w"])
            small(act, raw[0:C, C:2 * C], a["L0_conv_gi_w"])
            for n, k in enumerate(("w_ag", "w_bg", "w_ap", "w_bp", "w_g", "w_z")):
                small(act, raw[0:C, 64 + 32 * n:96 + 32 * n], a["L1_conv_" + k])
            small(act, raw[0:C, 256:264], a["L1_ffn_router_w"])
            small(act, raw[0:C, 264:520].rearrange("d (e c) -> d e c", e=EXPERTS),
                  a["L1_ffn_expert_w"].rearrange("e d c -> d e c"))
            small(act, raw[0:C, 520:552], a["L0_ffn_W"])
            small(act, raw[0:C, 552:584], a["L0_ffn_V"])
            small(act, raw[0:C, 584:585], col(a["L0_ffn_gamma"]))
            small(act, raw[0:C, 585:586], col(a["L0_ffn_beta"]))
            small(act, raw_o[0:D2, 0:C], a["L0_conv_po_w"])
            small(act, raw_o[0:D2, C:2 * C], a["L0_conv_go_w"])
            small(act, raw_o[D2:D2 + 1, 0:C], row(a["L0_conv_po_b"]))
            small(act, raw_o[D2:D2 + 1, C:2 * C], row(a["L0_conv_go_b"]))
            for n, k in enumerate(("L0_conv_ln1_", "L1_conv_ln_in_", "L1_conv_ln_out_")):
                small(act, lnv[:, 2 * n:2 * n + 1], col(a[k + "w"]))
                small(act, lnv[:, 2 * n + 1:2 * n + 2], col(a[k + "b"]))
            small(act, lnv[0:D2, 6:7], col(a["L0_conv_ln2_w"]))
            small(act, lnv[0:D2, 7:8], col(a["L0_conv_ln2_b"]))
            act.wait_ge(consts, 1)
            small(act, raw[C:C + 1, 0:C], row(a["L0_conv_pi_b"]))
            small(act, raw[C:C + 1, C:2 * C], row(a["L0_conv_gi_b"]))
            for n, k in enumerate(("b_ag", "b_bg", "b_ap", "b_bp", "b_g", "b_z")):
                small(act, raw[C:C + 1, 64 + 32 * n:96 + 32 * n], row(a["L1_conv_" + k]))
            small(act, raw[C:C + 1, 256:264], row(a["L1_ffn_router_b"]))
            small(act, raw[C:C + 1, 264:520], row(a["L1_ffn_expert_b"].rearrange("e c -> (e c)")))

            def gates(pj, nbank):
                def f(g, s, early):
                    act.wait_ge(pj.projected, g + 1)
                    if not early:
                        act.wait_ge(gates_free[pj], g - 1)
                    v = bank(2 + 2 * s, 2).rearrange("p (t h n) -> p t h n", h=2, n=nbank)[:, :, 1, :]
                    act.activation(sg[:, s, :].rearrange("p (t n) -> p t n", n=nbank), v,
                                   ACT.Sigmoid).then_inc(pj.gates, 1)
                return f

            gates_free = {p_a: p_a.used, p_o: p_o.added}

            norm_act(act, n_a)
            groups(act, copy_group(act, p_a), gates(p_a, P))
            for n, q in enumerate((0, 2)):
                act.wait_ge(e_turn, q + 1)
                act.activation(gated_t[:, 4 * q:4 * q + 4, :].rearrange("p a b -> p (a b)"), bank(q),
                               ACT.Copy).then_inc(e_copy_a, 1)
            norm_act(act, n_o)
            groups(act, copy_group(act, p_o, 2), gates(p_o, 2 * P))

            norm_act(act, n_b)

            def copy_b(g, s, early):
                act.wait_ge(p_b.turned, g + 1)
                v = x_cm.rearrange("p (g t) i -> p g (t i)", t=GROUP)[:, bass.ds(g, 1), :]
                act.activation(v.rearrange("p a n -> p (a n)"), bank(s), ACT.Copy).then_inc(p_b.copied, 1)

            groups(act, copy_b, nothing)
            act.wait_ge(bn_var, 1)
            act.activation(bn[:, 4:5], bn[:, 3:4], ACT.Sqrt).then_inc(bn_act, 1)
            act.wait_ge(bn_done, 1)
            sweep_act(act, s_step, s_state, 0)
            act.wait_ge(ends_kept, 1)
            sweep_act(act, s_step, s_state, CHUNK)
            act.wait_ge(flag_set, 1)
            again = act.value_load(flag_i[0:1, 0:1], min_val=0, max_val=1)
            with act.If(again > 0):
                with act.Fori(0, NCHUNKS - 2) as n:
                    act.wait_ge(ends_again, n + 1)
                    sweep_act(act, r_step, r_state, n * CHUNK)
            act.drain().then_inc(y_final, 1)

            norm_act(act, n_c)

            def copy_c(g, s, early):
                act.wait_ge(p_c.turned, g + 1)
                if not early:
                    act.wait_ge(halves, 2 * g - 2)
                act.activation(xt[:, s, :, :].rearrange("p a b -> p (a b)"), bank(s),
                               ACT.Copy).then_inc(p_c.copied, 1)

            def gates_c(g, s, early):
                act.wait_ge(gate_ready, g + 1)
                v = out_gate[:, :, :].rearrange("p (g t) c -> p g (t c)", t=16)[:, bass.ds(g, 1), :]
                act.activation(v.rearrange("p a n -> p (a n)"), bank(6 + s), ACT.Sigmoid)\
                   .then_inc(gate_kept, 1)
                for h in range(2):
                    act.wait_ge(halves, 2 * g + h + 1)
                    if not (early and s == 0):
                        act.wait_ge(p_c.used, 2 * g + h - 1)
                    v = bank(2 + 2 * h, 2).rearrange("p (t h n) -> p t h n", h=2, n=2 * P)[:, :, 0, :]
                    act.activation(sg[:, h, :].rearrange("p (t n) -> p t n", n=2 * P), v,
                                   ACT.Sigmoid).then_inc(p_c.gates, 1)

            groups(act, copy_c, gates_c)

            def keep(q):
                act.wait_ge(f_prod, q + 1)
                act.activation(prod[:, 4 * P * q:4 * P * (q + 1)], bank(4 + q % 2),
                               ACT.Copy).then_inc(f_kept, 1)

            for q in range(8):
                act.wait_ge(f_turn, q + 1)
                act.activation(gated_t[:, 4 * q:4 * q + 4, :].rearrange("p a b -> p (a b)"), bank(q % 2),
                               ACT.Copy).then_inc(f_copy_a, 1)
                if q:
                    keep(q - 1)
            keep(7)
            norm_act(act, n_z)
            groups(act, copy_group(act, p_z), nothing)

            norm_act(act, n_d)

            def copy_d(g, s, early):
                act.wait_ge(p_d.turned, g + 1)
                v = xd.rearrange("p (g t) i -> p g (t i)", t=GROUP)[:, bass.ds(g, 1), :]
                act.activation(v.rearrange("p a n -> p (a n)"), bank(s), ACT.Copy).then_inc(p_d.copied, 1)

            groups(act, copy_d, nothing)
            act.wait_ge(d_shift, 1)
            act.activation(pr[:, :, :], lg[:, :, :], ACT.Exp).then_inc(d_exp, 1)


        @block.vector
        def _(dve):
            dve.wait_ge(consts, 1)
            dve.wait_ge(ld_w, 16 * n_small[0])
            chain(dve, dve.tensor_copy(raw_s[:, :], raw[0:C, :]))
            for lo, hi, n in ((0, 64, 0), (64, 224, 1), (224, 256, 2)):
                dve.tensor_scalar(raw_s[:, lo:hi], raw[0:C, lo:hi], lnv[:, 2 * n:2 * n + 1], None, ALU.mult)
                dve.tensor_copy(lhs_b[0:C, n, :], lnv[:, 2 * n + 1:2 * n + 2].to_broadcast([C, P]))
            chain(dve, dve.memset(lhs_b[0:D2 + 1, 3, :], 1.0))
            dve.tensor_copy(lhs_b[0:D2, 3, :], lnv[0:D2, 7:8].to_broadcast([D2, P]))
            dve.tensor_scalar(raw_os[:, :], raw_o[0:D2, :], lnv[0:D2, 6:7], None, ALU.mult).then_inc(w_dve, 1)
            dve.wait_ge(w_pe, 1)

            def block_diag(dst, src, heads, blk, nb, cols):
                for h in range(heads):
                    d = dst[:, h, :, :] if heads > 1 else dst[:, :, :]
                    dve.tensor_tensor(d, src[:, h * cols:(h + 1) * cols].unsqueeze(1).to_broadcast([P, nb, cols]),
                                      blk[:, :].unsqueeze(2).to_broadcast([P, nb, cols]), ALU.mult)

            pr_w = ps[:, 0:NRAW]
            block_diag(w_a, pr_w[:, 0:64], 2, blk4, S, C)
            block_diag(w_c, pr_w[:, 64:192], 2, blk4, S, 2 * C)
            block_diag(w_g, pr_w[:, 192:224], 1, blk4, S, C)
            block_diag(w_z, pr_w[:, 224:256], 1, blk4, S, C)
            block_diag(w_r, pr_w[:, 256:264], 1, blk4, S, EXPERTS)
            block_diag(w_e, pr_w[:, 264:520], 1, blk4, S, EXPERTS * C)
            block_diag(w_b, pr_w[:, 520:552], 1, blk4, S, C)
            block_diag(v_b, pr_w[:, 552:584], 1, blk4, S, C)
            block_diag(w_o, bank(2)[:, 0:2 * C], 2, blk8, 2 * S, C)
            dve.tensor_copy(gb[:, :], pr_w[:, 584:586]).then_inc(w_dve, 1)

            def split_bias(key, src, reps):
                n = NB[key]
                inner = src.shape[-1]
                if len(reps) == 2:
                    t, s = reps
                    for h in range(2):
                        v = b_full[:, 0:n].rearrange("p (t h s o) -> p t h s o", t=t, h=2, s=s)
                        w = inner // 2
                        for tt in range(t):
                            ins = dve.tensor_copy(v[:, tt, h, :, :],
                                                  src[:, h * w:(h + 1) * w].unsqueeze(1).to_broadcast([P, s, w]))
                    chain(dve, ins)
                else:
                    r = n // inner
                    chain(dve, dve.tensor_copy(b_full[:, 0:n].rearrange("p (r o) -> p r o", o=inner),
                                               src.unsqueeze(1).to_broadcast([P, r, inner])))
                chain(dve, dve.tensor_copy(b_hi[:, 0:n], b_full[:, 0:n]))
                chain(dve, dve.tensor_tensor(b_rest[:, 0:n], b_full[:, 0:n], b_hi[:, 0:n], ALU.subtract))
                chain(dve, dve.tensor_copy(b_mid[:, 0:n], b_rest[:, 0:n]))
                chain(dve, dve.tensor_tensor(b_rest2[:, 0:n], b_rest[:, 0:n], b_mid[:, 0:n], ALU.subtract))
                dve.tensor_copy(bias[key][0:1, :], b_hi[0:1, 0:n])
                dve.tensor_copy(bias[key][32:33, :], b_mid[32:33, 0:n])
                chain(dve, dve.tensor_copy(bias[key][64:65, :], b_rest2[64:65, 0:n]))

            split_bias("A", bank(3)[:, 0:64], (2, S))
            split_bias("O", bank(2)[:, 64:128], (1, 2 * S))
            split_bias("C", bank(3)[:, 64:192], (1, S))
            split_bias("G", bank(3)[:, 192:224], ())
            split_bias("Z", bank(3)[:, 224:256], ())
            split_bias("R", bank(3)[:, 256:264], ())
            split_bias("E", bank(4)[:, 0:256], ())
            dve.wait_ge(w_pe, 2)
            dve.tensor_copy(w_bt[:, :], bank(5)[:, 0:P])
            dve.tensor_copy(v_t[:, :], bank(5)[:, P:2 * P])
            dve.tensor_copy(v_next[:, C:P], bank(5)[:, P:2 * P - C])
            dve.tensor_copy(v_wrap[P - C:P, 0:C], bank(5)[P - C:P, 2 * P - C:2 * P]).then_inc(w_dve, 1)

            norm_dve(dve, n_a, x_q, lambda q: dve.wait_ge(ld_x[q], 16))

            def gate_a(g, s, early):
                dve.wait_ge(p_a.masked, g + 1)
                v = bank(2 + 2 * s, 2).rearrange("p (u h s o) -> p u h s o", u=4, h=2, s=S)[:, :, 0, :, :]
                o = gated[:, 0:C, :].rearrange("p o (g k) -> p g k o", k=16)[:, bass.ds(g, 1), :, :]
                o = o.rearrange("p a (u s) o -> p (a u) s o", s=S)
                dve.tensor_tensor(o, v, sg[:, s, :].rearrange("p (u s o) -> p u s o", u=4, s=S),
                                  ALU.mult).then_inc(p_a.used, 1)

            groups_ahead(dve, scale_group(dve, p_a, C), gate_a)
            for n, q in enumerate((1, 3)):
                dve.wait_ge(e_turn, q + 1)
                dve.tensor_copy(gated_t[:, 4 * q:4 * q + 4, :].rearrange("p a b -> p (a b)"),
                                bank(q)).then_inc(e_copy_v, 1)
            dve.wait_ge(e_prod, 1)
            t_view = bank(4, 4).rearrange("p (d j) -> p j d", j=P)
            norm_dve(dve, n_o, lambda q: t_view[:, q * QT:(q + 1) * QT, :], lambda q: None, centre=True)

            def gate_o(g, s, early):
                dve.wait_ge(p_o.masked, g + 1)
                v = bank(2 + 2 * s, 2).rearrange("p (u h n) -> p u h n", u=2, h=2)[:, :, 0, :]
                w = sg[:, s, :].rearrange("p (u n) -> p u n", u=2)
                dve.tensor_tensor(w, v, w, ALU.mult).then_inc(p_o.used, 1)

            groups_ahead(dve, scale_group(dve, p_o, D2), gate_o)

            def x_added(q):
                dve.wait_ge(p_o.added, 2 * (q + 1))

            norm_dve(dve, n_b, x_q, x_added)

            def scale_b(g, s, early):
                if not early:
                    dve.wait_ge(p_b.turned, g - 1)
                src = centred[:, :].rearrange("p (s g t c) -> p g s t c", s=S, t=GROUP, c=C)
                r = rstd[:, :].rearrange("p (s g t) -> p g s t", s=S, t=GROUP)
                src = src[:, bass.ds(g, 1), :, :, :].rearrange("p a s t c -> p (a s) t c")
                r = r[:, bass.ds(g, 1), :, :].rearrange("p a s t -> p (a s) t")
                dve.tensor_tensor(xn[:, s, :, :].rearrange("p t (s c) -> p s t c", s=S), src,
                                  r.unsqueeze(3).to_broadcast([P, S, GROUP, C]), ALU.mult)\
                   .then_inc(p_b.scaled, 1)

            def stats_b(g, s, early):
                dve.wait_ge(p_b.projected, g + 1)
                dve.bn_stats(bst[:, bass.ds(g, 1), :].rearrange("p a n -> p (a n)"), bank(2 + s)).then_inc(p_b.used, 1)

            groups_ahead(dve, scale_b, stats_b)
            dve.wait_ge(p_b.used, GROUPS)
            dve.bn_aggr(mv[:, :], bst[:, :, :].rearrange("p g n -> p (g n)")).then_inc(bn_dve, 1)
            dve.wait_ge(bn_pe, 1)
            chain(dve, dve.tensor_copy(bn[:, 0:1], bank(4)[:, 0:1]))
            chain(dve, dve.tensor_tensor(bn[:, 1:2], mv[:, 0:1], bn[:, 0:1], ALU.subtract))
            chain(dve, dve.tensor_tensor(bn[:, 1:2], bn[:, 1:2], bn[:, 1:2], ALU.mult))
            dve.tensor_tensor(bn[:, 2:3], mv[:, 1:2], bn[:, 1:2], ALU.add).then_inc(bn_dve, 1)
            dve.wait_ge(bn_pe, 2)
            dve.tensor_scalar(bn[:, 3:4], bank(4)[:, 0:1], EPS_LN, None, ALU.add).then_inc(bn_var, 1)
            dve.wait_ge(bn_act, 1)
            chain(dve, dve.reciprocal(bn[:, 5:6], bn[:, 4:5]))
            chain(dve, dve.tensor_tensor(bn[:, 6:7], bn[:, 5:6], bn[:, 5:6], ALU.mult))
            chain(dve, dve.scalar_tensor_tensor(bn[:, 6:7], bn[:, 6:7], -0.5, bn[:, 3:4], ALU.mult, ALU.mult))
            chain(dve, dve.scalar_tensor_tensor(bn[:, 7:8], bn[:, 6:7], 1.5, bn[:, 5:6], ALU.add, ALU.mult))
            chain(dve, dve.tensor_tensor(bn[:, 8:9], bn[:, 7:8], gb[:, 0:1], ALU.mult))
            dve.tensor_scalar(diag[:, :], ident[:, :], bn[:, 8:9], None, ALU.mult).then_inc(bn_dve, 1)
            chain(dve, dve.tensor_tensor(bn[:, 10:11], bn[:, 0:1], bn[:, 8:9], ALU.mult))
            dve.tensor_tensor(bn[:, 9:10], gb[:, 1:2], bn[:, 10:11], ALU.subtract).then_inc(bn_done, 1)
            dve.wait_ge(bn_pe, 3)
            dve.tensor_copy(w_bs[:, :], bank(4)[:, 0:P]).then_inc(bn_dve, 1)

            for st in range(2):
                dve.wait_ge(s_state[st], CHUNK)
            keep_ends(dve, ends_kept)
            for st in range(2):
                dve.wait_ge(s_state[st], 2 * CHUNK)
            dve.tensor_tensor(dif[:, 0:P], y_cm[:, 2 * CHUNK - 1, :], ends[:, 1:P + 1], ALU.subtract)
            chain(dve, dve.tensor_tensor(dif[:, P:2 * P], y_cm[:, CHUNK - 1, :], ends[:, P + 1:2 * P + 1],
                                         ALU.subtract))
            dve.tensor_reduce(dmax[:, :], dif[:, :], AX.X, ALU.max, apply_absolute_value=True)\
               .then_inc(ends_kept, 1)
            dve.wait_ge(flag_turned, 1)
            chain(dve, dve.tensor_reduce(flag[:, 0:1], bank(6)[0:1, 0:P], AX.X, ALU.max))
            chain(dve, dve.tensor_scalar(flag[:, 1:2], flag[:, 0:1], SAME, None, ALU.is_gt))
            dve.tensor_copy(flag_i[:, :], flag[:, 1:2]).then_inc(flag_set, 1)
            dve.wait_ge(flag_set, 1)
            again = dve.value_load(flag_i[0:1, 0:1], min_val=0, max_val=1)
            with dve.If(again > 0):
                keep_ends(dve, ends_again)
                with dve.Fori(1, NCHUNKS - 2) as n:
                    for st in range(2):
                        dve.wait_ge(r_state[st], n * CHUNK)
                    keep_ends(dve, ends_again)

            def add_y(g, b):
                dve.wait_ge(y_turn, g + 1)
                v = x[:, :, :].rearrange("p (s g t) c -> p g s t c", s=S, t=GROUP)[:, bass.ds(g, 1), :, :, :]
                v = v.rearrange("p a s t c -> p (a s) t c")
                dve.tensor_tensor(v, v, bank(4 + b).rearrange("p (t s c) -> p s t c", t=GROUP, s=S),
                                  ALU.add).then_inc(y_added, 1)

            with dve.Fori(0, GROUPS // 4) as it:
                for b in range(4):
                    add_y(4 * it + b, b)

            norm_dve(dve, n_c, x_q, lambda q: dve.wait_ge(y_added, GROUPS))

            def gate_c(g, s, early):
                for h in range(2):
                    dve.wait_ge(p_c.masked, 2 * g + h + 1)
                    v = bank(2 + 2 * h, 2).rearrange("p (u h s o) -> p u h s o", u=2, h=2, s=S)[:, :, 1, :, :]
                    o = gated[:, :, :].rearrange("p o (g k) -> p g k o", k=8)[:, bass.ds(2 * g + h, 1), :, :]
                    o = o.rearrange("p a (u s) o -> p (a u) s o", s=S)
                    dve.tensor_tensor(o, v, sg[:, h, :].rearrange("p (u s o) -> p u s o", u=2, s=S),
                                      ALU.mult).then_inc(p_c.used, 1)

            groups_ahead(dve, scale_group(dve, p_c, C), gate_c)
            for q in range(8):
                dve.wait_ge(f_turn, q + 1)
                dve.tensor_copy(gated_t[:, C + 4 * q:C + 4 * q + 4, :].rearrange("p a b -> p (a b)"),
                                bank(2 + q % 2)).then_inc(f_copy_v, 1)
            norm_dve(dve, n_z, prod_q, lambda q: dve.wait_ge(f_kept, 8))

            def gate_z(g, s, early):
                dve.wait_ge(p_z.projected, g + 1)
                if not early:
                    dve.wait_ge(p_z.added, g - 1)
                v = out_gate[:, :, :].rearrange("p (g t) c -> p g (t c)", t=16)[:, bass.ds(g, 1), :]
                dve.tensor_tensor(sg[:, s, :], bank(2 + s), v.rearrange("p a n -> p (a n)"),
                                  ALU.mult).then_inc(p_z.used, 1)

            groups_ahead(dve, scale_group(dve, p_z, C), gate_z)

            def z_added(q):
                dve.wait_ge(p_z.added, 2 * (q + 1))

            norm_dve(dve, n_d, x_q, z_added)
            groups(dve, scale_group(dve, p_d, C), nothing)
            dve.wait_ge(d_logits, 1)
            lp = bank(2, 2).rearrange("p (j e) -> p j e", e=EXPERTS)

            def per_tok(n):
                return bcast(red[:, n, :], EXPERTS)

            def first_of(dst, vals, top, pos):
                chain(dve, dve.tensor_tensor(eq[:, :, :], vals, per_tok(top), ALU.is_equal))
                chain(dve, dve.tensor_tensor(eq[:, :, :], eq[:, :, :],
                                             rank[:, :].unsqueeze(1).to_broadcast([P, P, EXPERTS]), ALU.mult))
                chain(dve, dve.tensor_reduce(red[:, pos, :], eq[:, :, :], AX.X, ALU.max))
                chain(dve, dve.tensor_tensor(dst, eq[:, :, :], per_tok(pos), ALU.is_equal))

            chain(dve, dve.tensor_reduce(red[:, 0, :], lp, AX.X, ALU.max))
            dve.tensor_tensor(lg[:, :, :], lp, per_tok(0), ALU.subtract).then_inc(d_shift, 1)
            dve.wait_ge(d_exp, 1)
            chain(dve, dve.tensor_reduce(red[:, 1, :], pr[:, :, :], AX.X, ALU.add))
            chain(dve, dve.reciprocal(red[:, 2, :], red[:, 1, :]))
            chain(dve, dve.tensor_tensor(pr[:, :, :], pr[:, :, :], per_tok(2), ALU.mult))
            chain(dve, dve.tensor_reduce(red[:, 3, :], pr[:, :, :], AX.X, ALU.max))
            first_of(sel1[:, :, :], pr[:, :, :], 3, 4)
            chain(dve, dve.scalar_tensor_tensor(lg[:, :, :], sel1[:, :, :], -2.0, pr[:, :, :], ALU.mult, ALU.add))
            chain(dve, dve.tensor_reduce(red[:, 5, :], lg[:, :, :], AX.X, ALU.max))
            first_of(sel2[:, :, :], lg[:, :, :], 5, 4)
            chain(dve, dve.tensor_tensor(red[:, 6, :], red[:, 3, :], red[:, 5, :], ALU.add))
            chain(dve, dve.reciprocal(red[:, 7, :], red[:, 6, :]))
            chain(dve, dve.tensor_tensor(sel1[:, :, :], sel1[:, :, :], sel2[:, :, :], ALU.add))
            chain(dve, dve.tensor_tensor(pr[:, :, :], pr[:, :, :], sel1[:, :, :], ALU.mult))
            chain(dve, dve.tensor_tensor(wgt[:, :, :], pr[:, :, :], per_tok(7), ALU.mult))

            def weigh(u, s, early):
                dve.wait_ge(p_d.projected, u + 1)
                if not early:
                    dve.wait_ge(p_d.added, u - 1)
                w = wgt[:, :, :].rearrange("p (u s) e -> p u (s e)", s=S)[:, bass.ds(u, 1), :]
                w = w.rearrange("p a n -> p (a n)")
                dve.tensor_tensor(mixed[:, s, :, :, :].rearrange("p s e c -> p (s e) c"),
                                  bank(4 + 2 * s, 2).rearrange("p (n c) -> p n c", c=C),
                                  w.unsqueeze(2).to_broadcast([P, S * EXPERTS, C]), ALU.mult)\
                   .then_inc(weighed, 1)
                dve.wait_ge(weighed, u + 1)
                m = mixed[:, s, :, :, :]
                h = EXPERTS // 2
                dve.tensor_tensor(m[:, :, 0:h, :], m[:, :, 0:h, :], m[:, :, h:EXPERTS, :],
                                  ALU.add).then_inc(p_d.used, 1)

            weigh(0, 0, True)
            weigh(1, 1, True)
            with dve.Fori(1, TILES // 2) as it:
                weigh(2 * it, 0, False)
                weigh(2 * it + 1, 1, False)



_INS = ["x", "L0_conv_mask", "L0_conv_ln1_w", "L0_conv_ln1_b", "L0_conv_pi_w", "L0_conv_pi_b", "L0_conv_gi_w",
        "L0_conv_gi_b", "L0_conv_ln2_w", "L0_conv_ln2_b", "L0_conv_po_w", "L0_conv_po_b", "L0_conv_go_w",
        "L0_conv_go_b", "L0_ffn_W", "L0_ffn_V", "L0_ffn_gamma", "L0_ffn_beta", "L1_conv_mask", "L1_conv_ln_in_w",
        "L1_conv_ln_in_b", "L1_conv_w_ap", "L1_conv_b_ap", "L1_conv_w_ag", "L1_conv_b_ag", "L1_conv_w_bp",
        "L1_conv_b_bp", "L1_conv_w_bg", "L1_conv_b_bg", "L1_conv_ln_out_w", "L1_conv_ln_out_b", "L1_conv_w_z",
        "L1_conv_b_z", "L1_conv_w_g", "L1_conv_b_g", "L1_ffn_router_w", "L1_ffn_router_b", "L1_ffn_expert_w",
        "L1_ffn_expert_b"]


def kernel(**inputs):
    import numpy as _np
    import concourse.bacc as _bacc
    from concourse import mybir as _mybir
    from concourse.bass_utils import run_bass_kernel_spmd as _run

    nc = _bacc.Bacc("TRN2", target_bir_lowering=False, num_devices=1)
    arrays, args = {}, {}
    for name in _INS:
        v = _np.ascontiguousarray(inputs[name])
        arrays[f"in_{name}_dram"] = v
        args[name] = nc.dram_tensor(f"in_{name}_dram", v.shape, _mybir.dt.from_np(v.dtype),
                                    kind="ExternalInput").ap()
    out = nc.dram_tensor("out_0_dram", (1, P, P, C), _mybir.dt.float32, kind="ExternalOutput").ap()
    build(nc, args, out)
    r = _run(nc, [arrays], core_ids=[0])
    return r.results[0]["out_0_dram"]
```

```python
from contextlib import ExitStack

import concourse.bass as bass
from concourse import mybir

ALU = mybir.AluOpType
ACT = mybir.ActivationFunctionType
AX = mybir.AxisListType
F32 = mybir.dt.float32
BF16 = mybir.dt.bfloat16
I32 = mybir.dt.int32

P = 128
C = 32
D2 = C // 2
S = P // C
TILES = P // S
GROUP = 4
GROUPS = TILES // GROUP
BANK = 512
EXPERTS = 8
CHUNK = 16
NCHUNKS = P * P // CHUNK
EPS_LN = 1e-5
EPS_C = 1e-6
SAME = 2.0 ** -22

RAW = {"A": (0, 64), "C": (64, 192), "G": (192, 224), "Z": (224, 256), "R": (256, 264),
       "E": (264, 520), "W": (520, 552), "V": (552, 584), "gamma": (584, 585), "beta": (585, 586)}
NRAW = 586
RAW_O = (520, 584)
NROW = 584
LN_OF = {"A": 0, "C": 1, "G": 1, "Z": 2, "R": None, "E": None}


def build(nc, a, out):
    ctx = ExitStack()
    with ctx:
        def sb(name, shape, dt=F32):
            return ctx.enter_context(nc.sbuf_tensor(name, shape, dt))

        def sem(name):
            return ctx.enter_context(nc.semaphore(name))

        x = sb("x", [P, P, C])
        centred = sb("centred", [P, P * C])
        squares = sb("squares", [P, P * C])
        gated = sb("gated", [P, 2 * C, P])
        gated_t = sb("gated_t", [P, 2 * C, P])
        prod = sb("prod", [P, C * P])
        out_gate = sb("out_gate", [P, P, C])
        xn = sb("xn", [P, 2, GROUP, P])
        xt = sb("xt", [P, 2, GROUP, P])
        sg = sb("sg", [P, 2, BANK])
        mask_a = sb("mask_a", [P, P])
        mask_c = sb("mask_c", [P, P])
        sums = sb("sums", [P, P])
        mean = sb("mean", [P, P])
        var = sb("var", [P, P])
        sd = sb("sd", [P, P])
        rstd = sb("rstd", [P, P])
        newton = sb("newton", [P, P])
        rstd2 = sb("rstd2", [P, P])
        x_cm = gated[:, 0:C, :]
        y_cm = gated_t[:, 0:C, :]
        ends = sb("ends", [P, 2 * P + 1])
        xd = gated[:, 0:C, :]
        ident = sb("ident", [P, P])
        blk4 = sb("blk4", [P, S])
        blk8 = sb("blk8", [P, 2 * S])
        rep32 = sb("rep32", [C, P])
        rep16 = sb("rep16", [D2, P])
        avg4 = sb("avg4", [P, P])
        raw = sb("raw", [C + 1, NRAW])
        rep_w = sb("rep_w", [P, NRAW + 2 * C])
        raw_s = sb("raw_s", [C, NRAW])
        raw_o = sb("raw_o", [D2 + 1, 2 * C])
        raw_os = sb("raw_os", [D2, 2 * C])
        lnv = sb("lnv", [C, 8])
        lhs_b = sb("lhs_b", [C + 1, 5, P])
        w_a = sb("w_a", [P, 2, S, C])
        w_o = sb("w_o", [P, 2, 2 * S, C])
        w_c = sb("w_c", [P, 2, S, 2 * C])
        w_g = sb("w_g", [P, S, C])
        w_z = sb("w_z", [P, S, C])
        w_r = sb("w_r", [P, S, EXPERTS])
        w_e = sb("w_e", [P, S, EXPERTS * C])
        w_b = sb("w_b", [P, S, C])
        v_b = sb("v_b", [P, S, C])
        w_bt = sb("w_bt", [P, P])
        w_bs = sb("w_bs", [P, P])
        v_t = sb("v_t", [P, P])
        v_next = sb("v_next", [P, P])
        v_wrap = sb("v_wrap", [P, P])
        ones_b = sb("ones_b", [P, P], BF16)
        b_full = sb("b_full", [P, NROW])
        b_hi = sb("b_hi", [P, NROW], BF16)
        b_mid = sb("b_mid", [P, NROW], BF16)
        b_rest = sb("b_rest", [P, NROW])
        b_rest2 = sb("b_rest2", [P, NROW])
        rows = sb("rows", [P, NROW], BF16)
        rows_a = sb("rows_a", [P, 2, S, C], BF16)
        bst = sb("bst", [P, GROUPS, 6])
        mv = sb("mv", [P, 2])
        bn = sb("bn", [P, 12])
        diag = sb("diag", [P, P])
        dif = sb("dif", [P, 2 * P])
        dmax = sb("dmax", [P, 1])
        flag = sb("flag", [1, 2], F32)
        flag_i = sb("flag_i", [1, 1], I32)
        E8 = EXPERTS
        rank = sb("rank", [P, E8])
        lg, pr, eq, sel1, sel2, wgt = (
            gated_t[:, 8 * n:8 * n + 8, :].rearrange("p a b -> p (a b)").rearrange("p (j e) -> p j e", e=E8)
            for n in range(6))
        red = sb("red", [P, 8, P])
        mixed = prod[:, 0:2 * S * E8 * C].rearrange("p (b s e c) -> p b s e c", b=2, s=S, e=E8)

        ps = ctx.enter_context(nc.psum_tensor("ps", [P, 8 * BANK], F32))

        def bank(b, n=1):
            return ps[:, b * BANK:(b + n) * BANK]

        ld_x = [sem(f"ld_x{n}") for n in range(4)]
        ld_m = sem("ld_m")
        ld_mc = sem("ld_mc")
        ld_a = sem("ld_a")
        ld_w = sem("ld_w")
        stored = sem("stored")
        pool_step = sem("pool_step")
        consts = sem("consts")
        cleared = sem("cleared")
        a_scaled = sem("a_scaled")
        a_repeated = sem("a_repeated")
        a_built = sem("a_built")
        w_scaled = sem("w_scaled")
        w_repeated = sem("w_repeated")
        w_kept = sem("w_kept")
        o_built = sem("o_built")
        wv_built = sem("wv_built")
        wv_turned = sem("wv_turned")
        wv_kept = sem("wv_kept")
        rest_built = sem("rest_built")
        dve_step = sem("dve_step")

        halved = sem("halved")
        weighed = sem("weighed")
        bn_pe = sem("bn_pe")
        bn_dve = sem("bn_dve")
        e_turn = sem("e_turn")
        e_copy_a = sem("e_copy_a")
        e_copy_v = sem("e_copy_v")
        e_prod = sem("e_prod")
        f_turn = sem("f_turn")
        f_copy_a = sem("f_copy_a")
        f_copy_v = sem("f_copy_v")
        f_prod = sem("f_prod")
        f_kept = sem("f_kept")
        s_step = [sem(f"s_step{st}") for st in range(2)]
        s_state = [sem(f"s_state{st}") for st in range(2)]
        r_step = [sem(f"r_step{st}") for st in range(2)]
        r_state = [sem(f"r_state{st}") for st in range(2)]
        ends_kept = sem("ends_kept")
        ends_again = sem("ends_again")
        flag_turned = sem("flag_turned")
        flag_set = sem("flag_set")
        y_turn = sem("y_turn")
        y_added = sem("y_added")
        d_logits = sem("d_logits")
        d_shift = sem("d_shift")
        d_exp = sem("d_exp")
        y_final = sem("y_final")
        halves = sem("halves")
        gate_ready = sem("gate_ready")
        gate_kept = sem("gate_kept")
        bn_act = sem("bn_act")
        bn_done = sem("bn_done")
        bn_var = sem("bn_var")

        block = ctx.enter_context(nc.Block())
        steps = [0]

        def chain(eng, ins):
            steps[0] += 1
            ins.then_inc(dve_step, 1)
            eng.wait_ge(dve_step, steps[0])

        class Norm:
            def __init__(self, name, chans, scale, eps):
                self.chans, self.scale, self.eps = chans, scale, eps
                self.meaned = sem(name + "_meaned")
                self.centred = sem(name + "_centred")
                self.squared = sem(name + "_squared")
                self.varied = sem(name + "_varied")
                self.rooted = sem(name + "_rooted")
                self.done = sem(name + "_done")

        QUARTERS = 4
        QT = P // QUARTERS

        def tok(t, q, chans):
            v = t.rearrange("p (j c) -> p j c", c=chans)
            return v[:, q * QT:(q + 1) * QT, :]

        def bcast(v, n):
            return v.unsqueeze(2).to_broadcast([P, v.shape[1], n])

        def norm_dve(dve, nm, src, ready, centre=False, meanwhile=None):
            cbuf = centred[:, 0:P * nm.chans]
            sbuf = squares[:, 0:P * nm.chans]

            def second(q):
                dve.wait_ge(nm.squared, q + 1)
                dve.tensor_reduce(var[:, q * QT:(q + 1) * QT], tok(sbuf, q, nm.chans), AX.X,
                                  ALU.add).then_inc(nm.varied, 1)

            for q in range(QUARTERS):
                ready(q)
                cols = slice(q * QT, (q + 1) * QT)
                chain(dve, dve.tensor_reduce(sums[:, cols], src(q), AX.X, ALU.add))
                ins = dve.tensor_scalar(mean[:, cols], sums[:, cols], 1.0 / nm.chans, None, ALU.mult)
                ins.then_inc(nm.meaned, 1)
                if centre:
                    dve.wait_ge(nm.meaned, q + 1)
                    dve.tensor_tensor(tok(cbuf, q, nm.chans), src(q), bcast(mean[:, cols], nm.chans),
                                      ALU.subtract).then_inc(nm.centred, 1)
                if q:
                    second(q - 1)
            second(QUARTERS - 1)
            dve.wait_ge(nm.varied, QUARTERS)
            dve.tensor_scalar(sd[:, :], var[:, :], nm.scale / nm.chans, nm.eps, ALU.mult,
                              ALU.add).then_inc(nm.varied, 1)
            if meanwhile:
                meanwhile()
            dve.wait_ge(nm.rooted, 1)
            chain(dve, dve.reciprocal(rstd2[:, :], var[:, :]))
            chain(dve, dve.tensor_tensor(newton[:, :], rstd2[:, :], rstd2[:, :], ALU.mult))
            chain(dve, dve.scalar_tensor_tensor(newton[:, :], newton[:, :], -0.5, sd[:, :], ALU.mult, ALU.mult))
            dve.scalar_tensor_tensor(rstd[:, :], newton[:, :], 1.5, rstd2[:, :], ALU.add,
                                     ALU.mult).then_inc(nm.done, 1)
            dve.wait_ge(nm.done, 1)

        def norm_pool(pool, nm, src):
            cbuf = centred[:, 0:P * nm.chans]
            for q in range(QUARTERS):
                pool.wait_ge(nm.meaned, q + 1)
                pool.tensor_tensor(tok(cbuf, q, nm.chans), src(q),
                                   bcast(mean[:, q * QT:(q + 1) * QT], nm.chans),
                                   ALU.subtract).then_inc(nm.centred, 1)

        def norm_act(act, nm, meanwhile=None):
            n = QT * nm.chans
            for q in range(QUARTERS):
                act.wait_ge(nm.centred, q + 1)
                act.activation(squares[:, q * n:(q + 1) * n], centred[:, q * n:(q + 1) * n],
                               ACT.Square).then_inc(nm.squared, 1)
            if meanwhile:
                meanwhile()
            act.wait_ge(nm.varied, QUARTERS + 1)
            act.activation(var[:, :], sd[:, :], ACT.Sqrt).then_inc(nm.rooted, 1)

        def quarter(t, q):
            return t[:, q * QT:(q + 1) * QT]

        def take_mean(dve, nm, src, q, ready, centre=False):
            ready(q)
            chain(dve, dve.tensor_reduce(quarter(sums, q), src(q), AX.X, ALU.add))
            dve.tensor_scalar(quarter(mean, q), quarter(sums, q), 1.0 / nm.chans, None,
                              ALU.mult).then_inc(nm.meaned, 1)
            if centre:
                dve.wait_ge(nm.meaned, q + 1)
                dve.tensor_tensor(tok(centred[:, 0:P * nm.chans], q, nm.chans), src(q),
                                  bcast(quarter(mean, q), nm.chans), ALU.subtract).then_inc(nm.centred, 1)

        def take_var(dve, nm, q):
            dve.wait_ge(nm.squared, q + 1)
            chain(dve, dve.tensor_reduce(quarter(var, q), tok(squares[:, 0:P * nm.chans], q, nm.chans), AX.X,
                                         ALU.add))
            dve.tensor_scalar(quarter(sd, q), quarter(var, q), nm.scale / nm.chans, nm.eps, ALU.mult,
                              ALU.add).then_inc(nm.varied, 1)

        def take_rstd(dve, nm, q):
            dve.wait_ge(nm.rooted, q + 1)
            r2, nw = quarter(rstd2, q), quarter(newton, q)
            chain(dve, dve.reciprocal(r2, quarter(var, q)))
            chain(dve, dve.tensor_tensor(nw, r2, r2, ALU.mult))
            chain(dve, dve.scalar_tensor_tensor(nw, nw, -0.5, quarter(sd, q), ALU.mult, ALU.mult))
            chain(dve, dve.scalar_tensor_tensor(quarter(rstd, q), nw, 1.5, r2, ALU.add, ALU.mult))

        def fused_dve(dve, nm, src, ready, scale, gate, centre=False, meanwhile=None):
            def m(q):
                if not centre:
                    take_mean(dve, nm, src, q, ready)

            if centre:
                for q in range(QUARTERS):
                    take_mean(dve, nm, src, q, ready, True)
            m(0)
            m(1)
            take_var(dve, nm, 0)
            if meanwhile:
                meanwhile()
            take_rstd(dve, nm, 0)
            scale(0, 0, True)
            scale(1, 1, True)
            take_var(dve, nm, 1)
            m(2)
            take_rstd(dve, nm, 1)
            scale(2, 0, False)
            m(3)
            take_var(dve, nm, 2)
            gate(0, 0, True)
            scale(3, 1, False)
            take_var(dve, nm, 3)
            gate(1, 1, True)
            take_rstd(dve, nm, 2)
            take_rstd(dve, nm, 3)
            with dve.Fori(2, GROUPS // 2) as it:
                for b in range(2):
                    scale(2 * it + b, b, False)
                    gate(2 * it + b - 2, b, False)
            gate(GROUPS - 2, 0, False)
            gate(GROUPS - 1, 1, False)

        def fused_pool(pool, nm, src, work, centre=False):
            def sub(q):
                if not centre and q < QUARTERS:
                    pool.wait_ge(nm.meaned, q + 1)
                    pool.tensor_tensor(tok(centred[:, 0:P * nm.chans], q, nm.chans), src(q),
                                       bcast(quarter(mean, q), nm.chans), ALU.subtract).then_inc(nm.centred, 1)

            for q in range(QUARTERS):
                sub(q)
            with pool.Fori(0, GROUPS // 2) as it:
                work(2 * it, 0, False)
                work(2 * it + 1, 1, False)

        def fused_act(act, nm, copy, gate, meanwhile=None):
            n = QT * nm.chans

            def square(q):
                if q < QUARTERS:
                    act.wait_ge(nm.centred, q + 1)
                    act.activation(squares[:, q * n:(q + 1) * n], centred[:, q * n:(q + 1) * n],
                                   ACT.Square).then_inc(nm.squared, 1)

            def root(q):
                if q < QUARTERS:
                    act.wait_ge(nm.varied, q + 1)
                    act.activation(quarter(var, q), quarter(sd, q), ACT.Sqrt).then_inc(nm.rooted, 1)

            square(0)
            if meanwhile:
                meanwhile()
            square(1)
            root(0)
            copy(0, 0, True)
            copy(1, 1, True)
            root(1)
            square(2)
            gate(0, 0, True)
            copy(2, 0, False)
            square(3)
            gate(1, 1, True)
            copy(3, 1, False)
            root(2)
            root(3)
            gate(2, 0, False)
            for g in range(4, GROUPS):
                copy(g, g % 2, False)
                gate(g - 1, (g - 1) % 2, False)
            gate(GROUPS - 1, 1, False)

        both = dict(scale=1.0 + EPS_LN, eps=EPS_LN * EPS_C)
        n_a = Norm("na", C, **both)
        n_o = Norm("no", D2, 1.0, EPS_LN)
        n_b = Norm("nb", C, 1.0, EPS_LN)
        n_c = Norm("nc", C, **both)
        n_z = Norm("nz", C, 1.0, EPS_LN)
        n_d = Norm("nd", C, 1.0, EPS_LN)

        def x_q(q):
            return x[:, q * QT:(q + 1) * QT, :]

        def prod_q(q):
            return prod[:, :].rearrange("p (c j) -> p j c", j=P)[:, q * QT:(q + 1) * QT, :]

        class Proj:
            def __init__(self, name):
                self.scaled = sem(name + "_scaled")
                self.turned = sem(name + "_turned")
                self.copied = sem(name + "_copied")
                self.projected = sem(name + "_projected")
                self.gates = sem(name + "_gates")
                self.masked = sem(name + "_masked")
                self.used = sem(name + "_used")
                self.added = sem(name + "_added")

        p_a, p_o, p_b, p_c, p_z, p_d = (Proj(n) for n in ("pa", "po", "pb", "pc", "pz", "pd"))

        def groups(eng, head, tail, last=True):
            head(0, 0, True)
            head(1, 1, True)
            tail(0, 0, True)
            with eng.Fori(1, GROUPS // 2) as it:
                head(2 * it, 0, False)
                tail(2 * it - 1, 1, False)
                head(2 * it + 1, 1, False)
                tail(2 * it, 0, False)
            tail(GROUPS - 1, 1, False)

        def groups_straight(eng, head, tail):
            for g in range(GROUPS):
                head(g, g % 2, g < 2)
                if g:
                    tail(g - 1, (g - 1) % 2, g - 1 < 2)
            tail(GROUPS - 1, 1, False)

        def groups_ahead(eng, head, tail):
            head(0, 0, True)
            head(1, 1, True)
            for g in (2, 3):
                head(g, g % 2, False)
                tail(g - 2, g % 2, True)
            with eng.Fori(2, GROUPS // 2) as it:
                head(2 * it, 0, False)
                tail(2 * it - 2, 0, False)
                head(2 * it + 1, 1, False)
                tail(2 * it - 1, 1, False)
            tail(GROUPS - 2, 0, False)
            tail(GROUPS - 1, 1, False)

        def nothing(g, s, early):
            pass

        def scale_group(dve, pj, width):
            ntok = 16

            def f(g, s, early):
                if not early:
                    dve.wait_ge(pj.turned, g - 1)
                src = centred[:, 0:P * width].rearrange("p (g t c) -> p g t c", t=ntok, c=width)
                r = rstd[:, :].rearrange("p (g t) -> p g t", t=ntok)
                dst = xn[:, s, :, :].rearrange("p a b -> p (a b)")[:, 0:ntok * width]
                rg = r[:, bass.ds(g, 1), :].rearrange("p a t -> p (a t)")
                dve.tensor_tensor(dst.rearrange("p (t c) -> p t c", c=width),
                                  src[:, bass.ds(g, 1), :, :].rearrange("p a t c -> p (a t) c"),
                                  bcast(rg, width), ALU.mult).then_inc(pj.scaled, 1)
            return f

        def turn_group(pe, pj, tiles=GROUP):
            def f(g, s, early):
                pe.wait_ge(pj.scaled, g + 1)
                if not early:
                    pe.wait_ge(pj.copied, g - 1)
                for t in range(tiles):
                    ins = pe.transpose(bank(s)[:, t * P:(t + 1) * P], xn[:, s, t, :], ident[:, :])
                ins.then_inc(pj.turned, 1)
            return f

        def copy_group(act, pj, tiles=GROUP):
            def f(g, s, early):
                act.wait_ge(pj.turned, g + 1)
                if not early:
                    act.wait_ge(pj.projected, g - 1)
                act.activation(xt[:, s, 0:tiles, :].rearrange("p a b -> p (a b)"),
                               bank(s)[:, 0:tiles * P], ACT.Copy).then_inc(pj.copied, 1)
            return f

        def row(v):
            return v.rearrange("(a n) -> a n", a=1)

        def col(v):
            return v.rearrange("(n a) -> n a", a=1)

        def weights_a():
            return [(lnv[:, 0:1], col(a["L0_conv_ln1_w"])),
                    (raw[0:C, 0:C], a["L0_conv_pi_w"]),
                    (raw[0:C, C:2 * C], a["L0_conv_gi_w"]),
                    (lnv[:, 1:2], col(a["L0_conv_ln1_b"])),
                    (raw[C:C + 1, 0:C], row(a["L0_conv_pi_b"])),
                    (raw[C:C + 1, C:2 * C], row(a["L0_conv_gi_b"]))]

        def weights():
            w = [(raw_o[0:D2, 0:C], a["L0_conv_po_w"]),
                 (raw_o[0:D2, C:2 * C], a["L0_conv_go_w"]),
                 (raw_o[D2:D2 + 1, 0:C], row(a["L0_conv_po_b"])),
                 (raw_o[D2:D2 + 1, C:2 * C], row(a["L0_conv_go_b"])),
                 (lnv[0:D2, 6:7], col(a["L0_conv_ln2_w"])),
                 (lnv[0:D2, 7:8], col(a["L0_conv_ln2_b"]))]
            for n, k in enumerate(("ag", "bg", "ap", "bp", "g", "z")):
                w.append((raw[0:C, 64 + 32 * n:96 + 32 * n], a["L1_conv_w_" + k]))
                w.append((raw[C:C + 1, 64 + 32 * n:96 + 32 * n], row(a["L1_conv_b_" + k])))
            for n, k in ((1, "L1_conv_ln_in_"), (2, "L1_conv_ln_out_")):
                w.append((lnv[:, 2 * n:2 * n + 1], col(a[k + "w"])))
                w.append((lnv[:, 2 * n + 1:2 * n + 2], col(a[k + "b"])))
            w.append((raw[0:C, 256:264], a["L1_ffn_router_w"]))
            w.append((raw[C:C + 1, 256:264], row(a["L1_ffn_router_b"])))
            w.append((raw[0:C, 264:520].rearrange("d (e c) -> d e c", e=EXPERTS),
                      a["L1_ffn_expert_w"].rearrange("e d c -> d e c")))
            w.append((raw[C:C + 1, 264:520], row(a["L1_ffn_expert_b"].rearrange("e c -> (e c)"))))
            w.append((raw[0:C, 520:552], a["L0_ffn_W"]))
            w.append((raw[0:C, 552:584], a["L0_ffn_V"]))
            w.append((raw[0:C, 584:585], col(a["L0_ffn_gamma"])))
            w.append((raw[0:C, 585:586], col(a["L0_ffn_beta"])))
            return w

        @block.sync
        def _(sp):
            for q in range(QUARTERS):
                sp.dma_start(x_q(q), a["x"][0, :, q * QT:(q + 1) * QT, :]).then_inc(ld_x[q], 16)
            sp.dma_start(mask_a[:, :], a["L0_conv_mask"][0]).then_inc(ld_m, 16)
            for dst, src in weights():
                sp.dma_start(dst, src).then_inc(ld_w, 16)
            sp.dma_start(mask_c[:, :], a["L1_conv_mask"][0]).then_inc(ld_mc, 16)
            for g in range(GROUPS):
                sp.wait_ge(p_d.added, 4 * (g + 1))
                sp.dma_start(out[0, :, 16 * g:16 * g + 16, :], x[:, 16 * g:16 * g + 16, :]).then_inc(stored, 16)
            sp.wait_ge(stored, 16 * GROUPS)

        def split_rows(eng, chained, lo, hi):
            c = slice(lo, hi)
            chained(eng, eng.tensor_copy(b_hi[:, c], b_full[:, c]))
            chained(eng, eng.tensor_tensor(b_rest[:, c], b_full[:, c], b_hi[:, c], ALU.subtract))
            chained(eng, eng.tensor_copy(b_mid[:, c], b_rest[:, c]))
            chained(eng, eng.tensor_tensor(b_rest2[:, c], b_rest[:, c], b_mid[:, c], ALU.subtract))
            chained(eng, eng.tensor_copy(rows[0:1, c], b_hi[0:1, c]))
            chained(eng, eng.tensor_copy(rows[32:33, c], b_mid[32:33, c]))
            chained(eng, eng.tensor_copy(rows[64:65, c], b_rest2[64:65, c]))

        def block_diag(eng, dst, src, blk, nb, cols):
            return eng.tensor_tensor(dst, src.unsqueeze(1).to_broadcast([P, nb, cols]),
                                     blk[:, :].unsqueeze(2).to_broadcast([P, nb, cols]), ALU.mult)

        @block.gpsimd
        def _(pool):
            psteps = [0]

            def then(eng, ins):
                psteps[0] += 1
                ins.then_inc(pool_step, 1)
                eng.wait_ge(pool_step, psteps[0])

            def select(t, w, op, fill, base, mult, pattern):
                v = t[:, :].rearrange("p (a b) -> p a b", b=w) if w else t[:, :]
                return pool.affine_select(out=v, in_=v, compare_op=op, fill=fill, base=base,
                                          pattern=pattern, channel_multiplier=mult)

            pool.memset(blk4[:, :], 1.0)
            pool.memset(blk8[:, :], 1.0)
            pool.memset(ident[:, :], 0.0)
            pool.memset(rep32[:, :], 0.0)
            then(pool, pool.memset(rep16[:, :], 0.0))
            select(blk4, 0, ALU.is_ge, 0.0, 0, 1, [[-C, S]])
            then(pool, select(blk8, 0, ALU.is_ge, 0.0, 0, 1, [[-D2, 2 * S]]))
            select(blk4, 0, ALU.is_ge, 0.0, C - 1, -1, [[C, S]])
            select(blk8, 0, ALU.is_ge, 0.0, D2 - 1, -1, [[D2, 2 * S]])
            select(ident, 0, ALU.not_equal, 1.0, 0, 1, [[-1, P]])
            select(rep32, C, ALU.not_equal, 1.0, 0, 1, [[0, P // C], [-1, C]])
            select(rep16, D2, ALU.not_equal, 1.0, 0, 1, [[0, P // D2], [-1, D2]]).then_inc(consts, 1)
            pool.wait_ge(consts, 1)

            for e in range(EXPERTS):
                pool.memset(rank[:, e:e + 1], float(EXPERTS - e))
            pool.wait_ge(ld_m, 16)

            def mask_it(pj, msk, n, half=1):
                def f(g, s, early):
                    pool.wait_ge(pj.gates, g + 1)
                    m = msk[:, :].rearrange("p (g t) -> p g t", t=16)[:, bass.ds(g, 1), :]
                    v = sg[:, s, :].rearrange("p (t o) -> p t o", o=n)
                    pool.tensor_tensor(v, v, bcast(m.rearrange("p a t -> p (a t)"), n),
                                       ALU.mult).then_inc(pj.masked, 1)
                return f

            fused_pool(pool, n_a, x_q, mask_it(p_a, mask_a, C))
            pool.wait_ge(w_kept, 1)
            for h in range(2):
                block_diag(pool, w_o[:, h, :, :], rep_w[:, NRAW + C * h:NRAW + C * (h + 1)], blk8, 2 * S, C)
            split_rows(pool, then, *RAW_O)
            pool.drain().then_inc(o_built, 1)

            def add_out(pj):
                def f(g, s, early):
                    pool.wait_ge(pj.used, g + 1)
                    v = x[:, :, :].rearrange("p (g t) c -> p g (t c)", t=16)[:, bass.ds(g, 1), :]
                    v = v.rearrange("p a n -> p (a n)")
                    pool.tensor_tensor(v, v, sg[:, s, :], ALU.add).then_inc(pj.added, 1)
                return f

            groups(pool, mask_it(p_o, mask_a, C), add_out(p_o))

            block_diag(pool, w_b[:, :, :], rep_w[:, 520:552], blk4, S, C)
            block_diag(pool, v_b[:, :, :], rep_w[:, 552:584], blk4, S, C).then_inc(wv_built, 1)
            norm_pool(pool, n_b, x_q)
            split_rows(pool, then, 64, 520)
            for h in range(2):
                block_diag(pool, w_c[:, h, :, :], rep_w[:, 64 + 64 * h:128 + 64 * h], blk4, S, 2 * C)
            block_diag(pool, w_g[:, :, :], rep_w[:, 192:224], blk4, S, C)
            block_diag(pool, w_z[:, :, :], rep_w[:, 224:256], blk4, S, C)
            block_diag(pool, w_r[:, :, :], rep_w[:, 256:264], blk4, S, EXPERTS)
            then(pool, block_diag(pool, w_e[:, :, :], rep_w[:, 264:520], blk4, S, EXPERTS * C))
            pool.drain().then_inc(rest_built, 1)
            pool.wait_ge(ld_mc, 16)


            def mask_c_half(h):
                def f(g, s, early):
                    pool.wait_ge(p_c.gates, 2 * g + h + 1)
                    m = mask_c[:, :].rearrange("p (g t) -> p g t", t=8)[:, bass.ds(2 * g + h, 1), :]
                    v = sg[:, h, :].rearrange("p (t o) -> p t o", o=2 * C)
                    pool.tensor_tensor(v, v, bcast(m.rearrange("p a t -> p (a t)"), 2 * C),
                                       ALU.mult).then_inc(p_c.masked, 1)
                return f

            def mask_both(g, s, early):
                mask_c_half(0)(g, s, early)
                mask_c_half(1)(g, s, early)

            fused_pool(pool, n_c, x_q, mask_both)
            fused_pool(pool, n_z, prod_q, add_out(p_z))

            fused_pool(pool, n_d, x_q, nothing)

            def reduce_experts(u, s):
                pool.wait_ge(p_d.used, u + 1)
                m = mixed[:, s, :, :, :]
                n = EXPERTS // 2
                for lvl in range(2):
                    n //= 2
                    pool.tensor_tensor(m[:, :, 0:n, :], m[:, :, 0:n, :], m[:, :, n:2 * n, :],
                                       ALU.add).then_inc(halved, 1)
                    pool.wait_ge(halved, 2 * u + lvl + 1)
                v = x[:, :, :].rearrange("p (u t) c -> p u t c", t=S)[:, bass.ds(u, 1), :, :]
                v = v.rearrange("p a t c -> p (a t) c")
                pool.tensor_tensor(v, v, m[:, :, 0, :], ALU.add).then_inc(p_d.added, 1)

            with pool.Fori(0, TILES // 2) as it:
                reduce_experts(2 * it, 0)
                reduce_experts(2 * it + 1, 1)


        def flat(t, J):
            return t[:, bass.ds(J, 1), :].rearrange("p a i -> p (a i)") if not isinstance(J, int) else t[:, J, :]

        def sweep_pe(pe, stepped, state, base):
            def summed(st, k, b):
                return bank(2 + 2 * st + b)[:, 0:P]

            def step(st, k, b):
                J = CHUNK * st + k
                pe.matmul(summed(st, k, b), w_bs[:, :], flat(x_cm, J), start=True, stop=False,
                          skip_group_check=True)
                pe.wait_ge(state[st], base + k)
                pe.matmul(summed(st, k, b), v_t[:, :], flat(y_cm, J - 1), start=False, stop=True,
                          skip_group_check=True).then_inc(stepped[st], 1)

            pe.matmul(summed(0, 0, 0), w_bs[:, :], x_cm[:, 0, :], start=True, stop=False,
                      skip_group_check=True)
            pe.matmul(summed(0, 0, 0), v_next[:, :], ends[:, 1:P + 1], start=False, stop=False,
                      skip_group_check=True)
            pe.matmul(summed(0, 0, 0), v_wrap[:, :], ends[:, 0:P], start=False, stop=True,
                      skip_group_check=True).then_inc(stepped[0], 1)
            pe.matmul(summed(1, 0, 0), w_bs[:, :], x_cm[:, CHUNK, :], start=True, stop=False,
                      skip_group_check=True)
            pe.matmul(summed(1, 0, 0), v_t[:, :], ends[:, P + 1:2 * P + 1], start=False, stop=True,
                      skip_group_check=True).then_inc(stepped[1], 1)
            step(0, 1, 1)
            step(1, 1, 1)
            with pe.Fori(1, CHUNK // 2) as it:
                for b in range(2):
                    for st in range(2):
                        step(st, 2 * it + b, b)

        def sweep_act(act, stepped, state, base):
            for k in range(CHUNK):
                for st in range(2):
                    act.wait_ge(stepped[st], base + k + 1)
                    act.activation(y_cm[:, CHUNK * st + k, :], bank(2 + 2 * st + k % 2)[:, 0:P],
                                   ACT.Sigmoid, bias=bn[:, 9:10]).then_inc(state[st], 1)

        def keep_ends(dve, signal):
            dve.tensor_copy(ends[:, 1:P + 1], y_cm[:, 2 * CHUNK - 1, :])
            dve.tensor_copy(ends[:, P + 1:2 * P + 1], y_cm[:, CHUNK - 1, :]).then_inc(signal, 1)

        @block.tensor
        def _(pe):
            def repeat(dst, src, lhs, signal=None):
                ins = pe.matmul(dst, lhs, src, start=True, stop=True, skip_group_check=True)
                if signal:
                    ins.then_inc(signal, 1)

            pe.wait_ge(consts, 1)
            pe.wait_ge(a_scaled, 1)
            repeat(bank(6)[:, 0:64], raw_s[:, 0:64], rep32[:, :])
            repeat(bank(6)[:, 64:128], raw[:, 0:64], lhs_b[:, 0, :], a_repeated)
            repeat(bank(7)[:, 0:P], rep32[:, :], rep32[:, :], a_repeated)
            pe.wait_ge(a_built, 1)

            def bias_into(b, key, start=True):
                lo, hi = RAW_O if key == "O" else RAW[key]
                r = rows[:, lo:hi]
                n = hi - lo
                if key == "A":
                    v = rows_a[:, :, :, :].rearrange("p h s o -> p (h s o)").unsqueeze(1)
                    pe.matmul(b.rearrange("p (t n) -> p t n", t=2), ones_b[:, :],
                              v.to_broadcast([P, 2, 2 * S * C]), start=True, stop=False,
                              skip_group_check=True)
                elif key in ("O", "C"):
                    w = n // 2
                    k = BANK // n
                    v = r.rearrange("p (h o) -> p h o", h=2).unsqueeze(2).to_broadcast([P, 2, k, w])
                    pe.matmul(b.rearrange("p (h s o) -> p h s o", h=2, s=k), ones_b[:, :], v, start=True,
                              stop=False, skip_group_check=True)
                else:
                    k = BANK // n
                    pe.matmul(b.rearrange("p (k o) -> p k o", k=k), ones_b[:, :],
                              r.unsqueeze(1).to_broadcast([P, k, n]), start=True, stop=False,
                              skip_group_check=True)

            def project(pj, key, mms, per, used_gap):
                def f(g, s, early):
                    pe.wait_ge(pj.copied, g + 1)
                    if not early:
                        pe.wait_ge(pj.used, g - 1)
                    for h in range(2):
                        b = bank(2 + 2 * s + h)
                        bias_into(b, key)
                        for t in range(per):
                            n = BANK // per
                            ins = pe.matmul(b[:, t * n:(t + 1) * n], xt[:, s, per * h + t, :], mms,
                                            start=False, stop=(t == per - 1), skip_group_check=True)
                    ins.then_inc(pj.projected, 1)
                return f

            groups(pe, turn_group(pe, p_a), project(p_a, "A", w_a[:, :, :, :].rearrange("p h s c -> p (h s c)"), 2, 0))
            pe.wait_ge(p_a.used, GROUPS)
            for q in range(4):
                for t in range(4):
                    ins = pe.transpose(bank(q)[:, t * P:(t + 1) * P], gated[:, 4 * q + t, :], ident[:, :])
                ins.then_inc(e_turn, 1)
            for d in range(8):
                b = bank(6 + d // 4)
                ins = pe.matmul(b[:, (d % 4) * P:(d % 4 + 1) * P], gated[:, 16 + d, :], gated[:, 24 + d, :],
                                start=True, stop=True, skip_group_check=True)
            pe.wait_ge(e_copy_a, 2)
            pe.wait_ge(e_copy_v, 2)
            for d in range(8):
                b = bank(4 + d // 4)
                ins = pe.matmul(b[:, (d % 4) * P:(d % 4 + 1) * P], gated_t[:, d, :], gated_t[:, 8 + d, :],
                                start=True, stop=True, skip_group_check=True)
            ins.then_inc(e_prod, 1)
            pe.wait_ge(w_scaled, 1)
            repeat(bank(0), raw_s[:, 0:BANK], rep32[:, :])
            repeat(bank(1)[:, 0:NRAW - BANK], raw_s[:, BANK:NRAW], rep32[:, :])
            repeat(bank(1)[:, NRAW - BANK:NRAW - BANK + 2 * C], raw_os[:, :], rep16[:, :])
            for key in ("C", "G", "Z", "R"):
                lo, hi = RAW[key]
                ln = LN_OF[key]
                repeat(bank(2)[:, lo:hi], raw[:, lo:hi], lhs_b[:, 4 if ln is None else ln, :])
            repeat(bank(3)[:, 0:256], raw[:, 264:520], lhs_b[:, 4, :])
            repeat(bank(3)[:, 256:256 + 2 * C], raw_o[:, :], lhs_b[0:D2 + 1, 3, :], w_repeated)
            pe.wait_ge(w_kept, 1)
            pe.wait_ge(o_built, 1)
            groups(pe, turn_group(pe, p_o, 2), project(p_o, "O", w_o[:, :, :, :].rearrange("p h s c -> p (h s c)"), 1, 0))

            pe.wait_ge(wv_built, 1)
            pe.transpose(bank(6)[:, 0:P], w_b[:, :, :].rearrange("p s c -> p (s c)"), ident[:, :])
            pe.transpose(bank(6)[:, P:2 * P], v_b[:, :, :].rearrange("p s c -> p (s c)"),
                         ident[:, :]).then_inc(wv_turned, 1)
            pe.wait_ge(wv_kept, 1)

            def wx(g, s, early):
                pe.wait_ge(p_b.copied, g + 1)
                if not early:
                    pe.wait_ge(p_b.used, g - 1)
                v = x_cm.rearrange("p (g t) i -> p g (t i)", t=GROUP)[:, bass.ds(g, 1), :]
                pe.matmul(bank(2 + s), w_bt[:, :], v.rearrange("p a n -> p (a n)"), start=True,
                          stop=True).then_inc(p_b.projected, 1)

            groups(pe, turn_group(pe, p_b), wx)
            pe.wait_ge(bn_dve, 1)
            pe.matmul(bank(4)[:, 0:1], avg4[:, :], mv[:, 0:1], start=True, stop=True).then_inc(bn_pe, 1)
            pe.wait_ge(bn_dve, 2)
            pe.matmul(bank(4)[:, 0:1], avg4[:, :], bn[:, 2:3], start=True, stop=True).then_inc(bn_pe, 1)
            pe.wait_ge(bn_dve, 3)
            pe.matmul(bank(4)[:, 0:P], w_b[:, :, :].rearrange("p s c -> p (s c)"), diag[:, :],
                      start=True, stop=True).then_inc(bn_pe, 1)
            pe.wait_ge(bn_dve, 4)

            sweep_pe(pe, s_step, s_state, 0)
            pe.wait_ge(ends_kept, 1)
            sweep_pe(pe, s_step, s_state, CHUNK)
            pe.wait_ge(ends_kept, 2)
            pe.transpose(bank(6)[0:1, 0:P], dmax[:, :], ident[:, :]).then_inc(flag_turned, 1)
            pe.wait_ge(flag_set, 1)
            again = pe.value_load(flag_i[0:1, 0:1], min_val=0, max_val=1)
            with pe.If(again > 0):
                with pe.Fori(0, NCHUNKS - 2) as n:
                    pe.wait_ge(ends_again, n + 1)
                    sweep_pe(pe, r_step, r_state, n * CHUNK)
            pe.wait_ge(y_final, 1)
            for g in range(GROUPS):
                if g >= 4:
                    pe.wait_ge(y_added, g - 3)
                for t in range(4):
                    ins = pe.transpose(bank(4 + g % 4)[:, t * P:(t + 1) * P], y_cm[:, 4 * g + t, :], ident[:, :])
                ins.then_inc(y_turn, 1)

            pe.wait_ge(rest_built, 1)

            def project_c(g, s, early):
                pe.wait_ge(p_c.copied, g + 1)
                bias_into(bank(6 + s), "G")
                for t in range(GROUP):
                    ins = pe.matmul(bank(6 + s)[:, t * P:(t + 1) * P], xt[:, s, t, :],
                                    w_g[:, :, :].rearrange("p s c -> p (s c)"), start=False,
                                    stop=(t == 3), skip_group_check=True)
                ins.then_inc(gate_ready, 1)
                for h in range(2):
                    if not (early and s == 0):
                        pe.wait_ge(p_c.used, 2 * g + h - 1)
                    for t in range(2):
                        b = bank(2 + 2 * h + t)
                        bias_into(b, "C")
                        ins = pe.matmul(b, xt[:, s, 2 * h + t, :],
                                        w_c[:, :, :, :].rearrange("p h s c -> p (h s c)"),
                                        start=False, stop=True, skip_group_check=True)
                    ins.then_inc(halves, 1)
            groups(pe, turn_group(pe, p_c), project_c)
            pe.wait_ge(p_c.used, 2 * GROUPS)
            def c_products(q):
                b = bank(4 + q % 2)
                pe.wait_ge(f_copy_a, q + 1)
                pe.wait_ge(f_copy_v, q + 1)
                if q >= 2:
                    pe.wait_ge(f_kept, q - 1)
                for t in range(4):
                    ins = pe.matmul(b[:, t * P:(t + 1) * P], gated_t[:, 4 * q + t, :],
                                    gated_t[:, C + 4 * q + t, :], start=True, stop=True, skip_group_check=True)
                ins.then_inc(f_prod, 1)

            for q in range(8):
                if q >= 2:
                    pe.wait_ge(f_copy_a, q - 1)
                    pe.wait_ge(f_copy_v, q - 1)
                for t in range(4):
                    pe.transpose(bank(q % 2)[:, t * P:(t + 1) * P], gated[:, 4 * q + t, :], ident[:, :])
                for t in range(4):
                    ins = pe.transpose(bank(2 + q % 2)[:, t * P:(t + 1) * P], gated[:, C + 4 * q + t, :],
                                       ident[:, :])
                ins.then_inc(f_turn, 1)
                if q:
                    c_products(q - 1)
            c_products(7)

            def project_z(g, s, early):
                pe.wait_ge(p_z.copied, g + 1)
                if not early:
                    pe.wait_ge(p_z.used, g - 1)
                bias_into(bank(2 + s), "Z")
                for t in range(GROUP):
                    ins = pe.matmul(bank(2 + s)[:, t * P:(t + 1) * P], xt[:, s, t, :],
                                    w_z[:, :, :].rearrange("p s c -> p (s c)"), start=False,
                                    stop=(t == 3), skip_group_check=True)
                ins.then_inc(p_z.projected, 1)

            groups(pe, turn_group(pe, p_z), project_z)

            pe.wait_ge(p_z.used, GROUPS)
            for b in range(2):
                bias_into(bank(2 + b), "R")

            def router(g):
                pe.wait_ge(p_d.copied, g + 1)
                for t in range(GROUP):
                    u = GROUP * g + t
                    b = bank(2 + u // 16)
                    n = S * EXPERTS
                    ins = pe.matmul(b[:, (u % 16) * n:(u % 16 + 1) * n], xd[:, u, :],
                                    w_r[:, :, :].rearrange("p s e -> p (s e)"), start=False, stop=True,
                                    skip_group_check=True)
                if g == GROUPS - 1:
                    ins.then_inc(d_logits, 1)

            turn = turn_group(pe, p_d)
            for g in range(GROUPS):
                turn(g, g % 2, g < 2)
                if g:
                    router(g - 1)
            router(GROUPS - 1)
            for u in range(TILES):
                s = u % 2
                if u >= 2:
                    pe.wait_ge(weighed, u - 1)
                for h in range(2):
                    b = bank(4 + 2 * s + h)
                    bias_into(b, "E")
                    ins = pe.matmul(b, xd[:, u, :],
                                    w_e[:, :, :].rearrange("p s n -> p (s n)")[:, h * BANK:(h + 1) * BANK],
                                    start=False, stop=True, skip_group_check=True)
                ins.then_inc(p_d.projected, 1)


        @block.scalar
        def _(act):
            for dst, src in weights_a():
                act.dma_start(dst, src).then_inc(ld_a, 16)

            def gates(pj, nbank):
                def f(g, s, early):
                    act.wait_ge(pj.projected, g + 1)
                    if not early:
                        act.wait_ge(gates_free[pj], g - 1)
                    v = bank(2 + 2 * s, 2).rearrange("p (t h n) -> p t h n", h=2, n=nbank)[:, :, 1, :]
                    act.activation(sg[:, s, :].rearrange("p (t n) -> p t n", n=nbank), v,
                                   ACT.Sigmoid).then_inc(pj.gates, 1)
                return f

            gates_free = {p_a: p_a.used, p_o: p_o.added}

            fused_act(act, n_a, copy_group(act, p_a), gates(p_a, P))
            for n, q in enumerate((0, 2)):
                act.wait_ge(e_turn, q + 1)
                act.activation(gated_t[:, 4 * q:4 * q + 4, :].rearrange("p a b -> p (a b)"), bank(q),
                               ACT.Copy).then_inc(e_copy_a, 1)
            def keep_weights():
                act.wait_ge(w_repeated, 1)
                act.activation(rep_w[:, :], bank(0, 2)[:, 0:NRAW + 2 * C], ACT.Copy)
                act.activation(b_full[:, 64:264], bank(2)[:, 64:264], ACT.Copy)
                act.activation(b_full[:, 264:NROW], bank(3)[:, 0:NROW - 264], ACT.Copy).then_inc(w_kept, 1)

            fused_act(act, n_o, copy_group(act, p_o, 2), gates(p_o, 2 * P), keep_weights)

            def keep_wv():
                act.wait_ge(wv_turned, 1)
                act.activation(w_bt[:, :], bank(6)[:, 0:P], ACT.Copy)
                act.activation(v_t[:, :], bank(6)[:, P:2 * P], ACT.Copy)
                act.activation(v_next[:, C:P], bank(6)[:, P:2 * P - C], ACT.Copy)
                act.activation(v_wrap[P - C:P, 0:C], bank(6)[P - C:P, 2 * P - C:2 * P],
                               ACT.Copy).then_inc(wv_kept, 1)

            norm_act(act, n_b, keep_wv)

            def copy_b(g, s, early):
                act.wait_ge(p_b.turned, g + 1)
                v = x_cm.rearrange("p (g t) i -> p g (t i)", t=GROUP)[:, bass.ds(g, 1), :]
                act.activation(v.rearrange("p a n -> p (a n)"), bank(s), ACT.Copy).then_inc(p_b.copied, 1)

            groups_straight(act, copy_b, nothing)
            act.wait_ge(bn_var, 1)
            act.activation(bn[:, 4:5], bn[:, 3:4], ACT.Sqrt).then_inc(bn_act, 1)
            act.wait_ge(bn_done, 1)
            sweep_act(act, s_step, s_state, 0)
            act.wait_ge(ends_kept, 1)
            sweep_act(act, s_step, s_state, CHUNK)
            act.wait_ge(flag_set, 1)
            again = act.value_load(flag_i[0:1, 0:1], min_val=0, max_val=1)
            with act.If(again > 0):
                with act.Fori(0, NCHUNKS - 2) as n:
                    act.wait_ge(ends_again, n + 1)
                    sweep_act(act, r_step, r_state, n * CHUNK)
            act.drain().then_inc(y_final, 1)

            def copy_c(g, s, early):
                act.wait_ge(p_c.turned, g + 1)
                if not early:
                    act.wait_ge(halves, 2 * g - 2)
                act.activation(xt[:, s, :, :].rearrange("p a b -> p (a b)"), bank(s),
                               ACT.Copy).then_inc(p_c.copied, 1)

            def gates_c(g, s, early):
                act.wait_ge(gate_ready, g + 1)
                v = out_gate[:, :, :].rearrange("p (g t) c -> p g (t c)", t=16)[:, bass.ds(g, 1), :]
                act.activation(v.rearrange("p a n -> p (a n)"), bank(6 + s), ACT.Sigmoid)\
                   .then_inc(gate_kept, 1)
                for h in range(2):
                    act.wait_ge(halves, 2 * g + h + 1)
                    if not (early and s == 0):
                        act.wait_ge(p_c.used, 2 * g + h - 1)
                    v = bank(2 + 2 * h, 2).rearrange("p (t h n) -> p t h n", h=2, n=2 * P)[:, :, 0, :]
                    act.activation(sg[:, h, :].rearrange("p (t n) -> p t n", n=2 * P), v,
                                   ACT.Sigmoid).then_inc(p_c.gates, 1)

            fused_act(act, n_c, copy_c, gates_c)

            def keep(q):
                act.wait_ge(f_prod, q + 1)
                act.activation(prod[:, 4 * P * q:4 * P * (q + 1)], bank(4 + q % 2),
                               ACT.Copy).then_inc(f_kept, 1)

            for q in range(8):
                act.wait_ge(f_turn, q + 1)
                act.activation(gated_t[:, 4 * q:4 * q + 4, :].rearrange("p a b -> p (a b)"), bank(q % 2),
                               ACT.Copy).then_inc(f_copy_a, 1)
                if q:
                    keep(q - 1)
            keep(7)
            fused_act(act, n_z, copy_group(act, p_z), nothing)


            def copy_d(g, s, early):
                act.wait_ge(p_d.turned, g + 1)
                v = xd.rearrange("p (g t) i -> p g (t i)", t=GROUP)[:, bass.ds(g, 1), :]
                act.activation(v.rearrange("p a n -> p (a n)"), bank(s), ACT.Copy).then_inc(p_d.copied, 1)

            fused_act(act, n_d, copy_d, nothing)
            act.wait_ge(d_shift, 1)
            act.activation(pr[:, :, :], lg[:, :, :], ACT.Exp).then_inc(d_exp, 1)


        @block.vector
        def _(dve):
            dve.memset(ones_b[:, :], 1.0)
            dve.memset(rows[:, :], 0.0)
            dve.memset(v_next[:, :], 0.0)
            dve.memset(v_wrap[:, :], 0.0)
            dve.memset(ends[:, :], 0.0)
            dve.memset(lhs_b[0:C, 4, :], 0.0)
            dve.memset(lhs_b[C:C + 1, :, :], 1.0)
            chain(dve, dve.memset(lhs_b[0:D2 + 1, 3, :], 1.0))

            def ln_weights(lo, hi, n):
                dve.tensor_copy(lhs_b[0:C, n, :], lnv[:, 2 * n + 1:2 * n + 2].to_broadcast([C, P]))
                return dve.tensor_scalar(raw_s[:, lo:hi], raw[0:C, lo:hi], lnv[:, 2 * n:2 * n + 1], None,
                                         ALU.mult)

            def x_ready(q):
                dve.wait_ge(ld_x[q], 16)
                if q == 1:
                    dve.wait_ge(ld_a, 16 * len(weights_a()))
                    ln_weights(0, 64, 0).then_inc(a_scaled, 1)

            def build_a():
                dve.wait_ge(a_repeated, 2)
                dve.wait_ge(consts, 1)
                for h in range(2):
                    block_diag(dve, w_a[:, h, :, :], bank(6)[:, C * h:C * (h + 1)], blk4, S, C)
                dve.tensor_scalar(avg4[:, :], bank(7)[:, 0:P], 1.0 / S, None, ALU.mult)
                chain(dve, dve.tensor_copy(b_full[:, 0:64], bank(6)[:, 64:128]))
                split_rows(dve, chain, 0, 64)
                dve.tensor_copy(rows_a[:, :, :, :], rows[:, 0:64].rearrange("p (h o) -> p h o", h=2)
                                .unsqueeze(2).to_broadcast([P, 2, S, C])).then_inc(a_built, 1)


            def gate_a(g, s, early):
                dve.wait_ge(p_a.masked, g + 1)
                v = bank(2 + 2 * s, 2).rearrange("p (u h s o) -> p u h s o", u=4, h=2, s=S)[:, :, 0, :, :]
                o = gated[:, 0:C, :].rearrange("p o (g k) -> p g k o", k=16)[:, bass.ds(g, 1), :, :]
                o = o.rearrange("p a (u s) o -> p (a u) s o", s=S)
                dve.tensor_tensor(o, v, sg[:, s, :].rearrange("p (u s o) -> p u s o", u=4, s=S),
                                  ALU.mult).then_inc(p_a.used, 1)

            fused_dve(dve, n_a, x_q, x_ready, scale_group(dve, p_a, C), gate_a, meanwhile=build_a)
            for n, q in enumerate((1, 3)):
                dve.wait_ge(e_turn, q + 1)
                dve.tensor_copy(gated_t[:, 4 * q:4 * q + 4, :].rearrange("p a b -> p (a b)"),
                                bank(q)).then_inc(e_copy_v, 1)
            dve.wait_ge(ld_w, 16 * len(weights()))
            dve.tensor_copy(raw_s[:, 256:NRAW], raw[0:C, 256:NRAW])
            dve.tensor_copy(lhs_b[0:D2, 3, :], lnv[0:D2, 7:8].to_broadcast([D2, P]))
            dve.tensor_scalar(raw_os[:, :], raw_o[0:D2, :], lnv[0:D2, 6:7], None, ALU.mult)
            ln_weights(64, 224, 1)
            ln_weights(224, 256, 2).then_inc(w_scaled, 1)
            dve.wait_ge(e_prod, 1)
            t_view = bank(4, 4).rearrange("p (d j) -> p j d", j=P)

            def gate_o(g, s, early):
                dve.wait_ge(p_o.masked, g + 1)
                v = bank(2 + 2 * s, 2).rearrange("p (u h n) -> p u h n", u=2, h=2)[:, :, 0, :]
                w = sg[:, s, :].rearrange("p (u n) -> p u n", u=2)
                dve.tensor_tensor(w, v, w, ALU.mult).then_inc(p_o.used, 1)

            fused_dve(dve, n_o, lambda q: t_view[:, q * QT:(q + 1) * QT, :], lambda q: None,
                      scale_group(dve, p_o, D2), gate_o, centre=True)

            def x_added(q):
                dve.wait_ge(p_o.added, 2 * (q + 1))

            norm_dve(dve, n_b, x_q, x_added)

            def scale_b(g, s, early):
                if not early:
                    dve.wait_ge(p_b.turned, g - 1)
                src = centred[:, :].rearrange("p (s g t c) -> p g s t c", s=S, t=GROUP, c=C)
                r = rstd[:, :].rearrange("p (s g t) -> p g s t", s=S, t=GROUP)
                src = src[:, bass.ds(g, 1), :, :, :].rearrange("p a s t c -> p (a s) t c")
                r = r[:, bass.ds(g, 1), :, :].rearrange("p a s t -> p (a s) t")
                dve.tensor_tensor(xn[:, s, :, :].rearrange("p t (s c) -> p s t c", s=S), src,
                                  r.unsqueeze(3).to_broadcast([P, S, GROUP, C]), ALU.mult)\
                   .then_inc(p_b.scaled, 1)

            def stats_b(g, s, early):
                dve.wait_ge(p_b.projected, g + 1)
                dve.bn_stats(bst[:, bass.ds(g, 1), :].rearrange("p a n -> p (a n)"), bank(2 + s)).then_inc(p_b.used, 1)

            groups_ahead(dve, scale_b, stats_b)
            dve.wait_ge(w_kept, 1)
            dve.wait_ge(p_b.used, GROUPS)
            dve.bn_aggr(mv[:, :], bst[:, :, :].rearrange("p g n -> p (g n)")).then_inc(bn_dve, 1)
            dve.wait_ge(bn_pe, 1)
            chain(dve, dve.tensor_copy(bn[:, 0:1], bank(4)[:, 0:1]))
            chain(dve, dve.tensor_tensor(bn[:, 1:2], mv[:, 0:1], bn[:, 0:1], ALU.subtract))
            chain(dve, dve.tensor_tensor(bn[:, 1:2], bn[:, 1:2], bn[:, 1:2], ALU.mult))
            dve.tensor_tensor(bn[:, 2:3], mv[:, 1:2], bn[:, 1:2], ALU.add).then_inc(bn_dve, 1)
            dve.wait_ge(bn_pe, 2)
            dve.tensor_scalar(bn[:, 3:4], bank(4)[:, 0:1], EPS_LN, None, ALU.add).then_inc(bn_var, 1)
            dve.wait_ge(bn_act, 1)
            chain(dve, dve.reciprocal(bn[:, 5:6], bn[:, 4:5]))
            chain(dve, dve.tensor_tensor(bn[:, 6:7], bn[:, 5:6], bn[:, 5:6], ALU.mult))
            chain(dve, dve.scalar_tensor_tensor(bn[:, 6:7], bn[:, 6:7], -0.5, bn[:, 3:4], ALU.mult, ALU.mult))
            chain(dve, dve.scalar_tensor_tensor(bn[:, 7:8], bn[:, 6:7], 1.5, bn[:, 5:6], ALU.add, ALU.mult))
            chain(dve, dve.tensor_tensor(bn[:, 8:9], bn[:, 7:8], rep_w[:, 584:585], ALU.mult))
            dve.tensor_scalar(diag[:, :], ident[:, :], bn[:, 8:9], None, ALU.mult).then_inc(bn_dve, 1)
            chain(dve, dve.tensor_tensor(bn[:, 10:11], bn[:, 0:1], bn[:, 8:9], ALU.mult))
            dve.tensor_tensor(bn[:, 9:10], rep_w[:, 585:586], bn[:, 10:11], ALU.subtract).then_inc(bn_done, 1)
            dve.wait_ge(bn_pe, 3)
            dve.tensor_copy(w_bs[:, :], bank(4)[:, 0:P]).then_inc(bn_dve, 1)

            for st in range(2):
                dve.wait_ge(s_state[st], CHUNK)
            keep_ends(dve, ends_kept)
            for st in range(2):
                dve.wait_ge(s_state[st], 2 * CHUNK)
            dve.tensor_tensor(dif[:, 0:P], y_cm[:, 2 * CHUNK - 1, :], ends[:, 1:P + 1], ALU.subtract)
            chain(dve, dve.tensor_tensor(dif[:, P:2 * P], y_cm[:, CHUNK - 1, :], ends[:, P + 1:2 * P + 1],
                                         ALU.subtract))
            dve.tensor_reduce(dmax[:, :], dif[:, :], AX.X, ALU.max, apply_absolute_value=True)\
               .then_inc(ends_kept, 1)
            dve.wait_ge(flag_turned, 1)
            chain(dve, dve.tensor_reduce(flag[:, 0:1], bank(6)[0:1, 0:P], AX.X, ALU.max))
            chain(dve, dve.tensor_scalar(flag[:, 1:2], flag[:, 0:1], SAME, None, ALU.is_gt))
            dve.tensor_copy(flag_i[:, :], flag[:, 1:2]).then_inc(flag_set, 1)
            dve.wait_ge(flag_set, 1)
            again = dve.value_load(flag_i[0:1, 0:1], min_val=0, max_val=1)
            with dve.If(again > 0):
                keep_ends(dve, ends_again)
                with dve.Fori(1, NCHUNKS - 2) as n:
                    for st in range(2):
                        dve.wait_ge(r_state[st], n * CHUNK)
                    keep_ends(dve, ends_again)

            def add_y(g, b):
                dve.wait_ge(y_turn, g + 1)
                v = x[:, :, :].rearrange("p (s g t) c -> p g s t c", s=S, t=GROUP)[:, bass.ds(g, 1), :, :, :]
                v = v.rearrange("p a s t c -> p (a s) t c")
                dve.tensor_tensor(v, v, bank(4 + b).rearrange("p (t s c) -> p s t c", t=GROUP, s=S),
                                  ALU.add).then_inc(y_added, 1)

            with dve.Fori(0, GROUPS // 4) as it:
                for b in range(4):
                    add_y(4 * it + b, b)


            def gate_c(g, s, early):
                for h in range(2):
                    dve.wait_ge(p_c.masked, 2 * g + h + 1)
                    v = bank(2 + 2 * h, 2).rearrange("p (u h s o) -> p u h s o", u=2, h=2, s=S)[:, :, 1, :, :]
                    o = gated[:, :, :].rearrange("p o (g k) -> p g k o", k=8)[:, bass.ds(2 * g + h, 1), :, :]
                    o = o.rearrange("p a (u s) o -> p (a u) s o", s=S)
                    dve.tensor_tensor(o, v, sg[:, h, :].rearrange("p (u s o) -> p u s o", u=2, s=S),
                                      ALU.mult).then_inc(p_c.used, 1)

            fused_dve(dve, n_c, x_q, lambda q: dve.wait_ge(y_added, GROUPS), scale_group(dve, p_c, C), gate_c)
            for q in range(8):
                dve.wait_ge(f_turn, q + 1)
                dve.tensor_copy(gated_t[:, C + 4 * q:C + 4 * q + 4, :].rearrange("p a b -> p (a b)"),
                                bank(2 + q % 2)).then_inc(f_copy_v, 1)

            def gate_z(g, s, early):
                dve.wait_ge(p_z.projected, g + 1)
                if not early:
                    dve.wait_ge(p_z.added, g - 1)
                v = out_gate[:, :, :].rearrange("p (g t) c -> p g (t c)", t=16)[:, bass.ds(g, 1), :]
                dve.tensor_tensor(sg[:, s, :], bank(2 + s), v.rearrange("p a n -> p (a n)"),
                                  ALU.mult).then_inc(p_z.used, 1)

            fused_dve(dve, n_z, prod_q, lambda q: dve.wait_ge(f_kept, 8), scale_group(dve, p_z, C), gate_z)

            def z_added(q):
                dve.wait_ge(p_z.added, 2 * (q + 1))

            fused_dve(dve, n_d, x_q, z_added, scale_group(dve, p_d, C), nothing)
            dve.wait_ge(d_logits, 1)
            lp = bank(2, 2).rearrange("p (j e) -> p j e", e=EXPERTS)

            def per_tok(n):
                return bcast(red[:, n, :], EXPERTS)

            def first_of(dst, vals, top, pos):
                ranks = rank[:, :].unsqueeze(1).to_broadcast([P, P, EXPERTS])
                if top is None:
                    chain(dve, dve.tensor_scalar(eq[:, :, :], vals, 0.0, None, ALU.is_equal))
                else:
                    chain(dve, dve.tensor_tensor(eq[:, :, :], vals, per_tok(top), ALU.is_equal))
                chain(dve, dve.tensor_tensor(eq[:, :, :], eq[:, :, :], ranks, ALU.mult))
                chain(dve, dve.tensor_reduce(red[:, pos, :], eq[:, :, :], AX.X, ALU.max))
                chain(dve, dve.tensor_tensor(dst, eq[:, :, :], per_tok(pos), ALU.is_equal))

            chain(dve, dve.tensor_reduce(red[:, 0, :], lp, AX.X, ALU.max))
            ins = dve.tensor_tensor(lg[:, :, :], lp, per_tok(0), ALU.subtract)
            ins.then_inc(d_shift, 1)
            dve.wait_ge(d_shift, 1)
            first_of(sel1[:, :, :], lg[:, :, :], None, 4)
            dve.wait_ge(d_exp, 1)
            chain(dve, dve.scalar_tensor_tensor(lg[:, :, :], sel1[:, :, :], -2.0, pr[:, :, :], ALU.mult, ALU.add))
            chain(dve, dve.tensor_reduce(red[:, 5, :], lg[:, :, :], AX.X, ALU.max))
            first_of(sel2[:, :, :], lg[:, :, :], 5, 4)
            chain(dve, dve.tensor_scalar(red[:, 6, :], red[:, 5, :], 1.0, None, ALU.add))
            chain(dve, dve.reciprocal(red[:, 7, :], red[:, 6, :]))
            chain(dve, dve.tensor_tensor(sel2[:, :, :], sel2[:, :, :], pr[:, :, :], ALU.mult))
            chain(dve, dve.tensor_tensor(sel1[:, :, :], sel1[:, :, :], sel2[:, :, :], ALU.add))
            chain(dve, dve.tensor_tensor(wgt[:, :, :], sel1[:, :, :], per_tok(7), ALU.mult))

            def weigh(u, s, early):
                dve.wait_ge(p_d.projected, u + 1)
                if not early:
                    dve.wait_ge(p_d.added, u - 1)
                w = wgt[:, :, :].rearrange("p (u s) e -> p u (s e)", s=S)[:, bass.ds(u, 1), :]
                w = w.rearrange("p a n -> p (a n)")
                dve.tensor_tensor(mixed[:, s, :, :, :].rearrange("p s e c -> p (s e) c"),
                                  bank(4 + 2 * s, 2).rearrange("p (n c) -> p n c", c=C),
                                  w.unsqueeze(2).to_broadcast([P, S * EXPERTS, C]), ALU.mult)\
                   .then_inc(weighed, 1)
                dve.wait_ge(weighed, u + 1)
                m = mixed[:, s, :, :, :]
                h = EXPERTS // 2
                dve.tensor_tensor(m[:, :, 0:h, :], m[:, :, 0:h, :], m[:, :, h:EXPERTS, :],
                                  ALU.add).then_inc(p_d.used, 1)

            weigh(0, 0, True)
            weigh(1, 1, True)
            with dve.Fori(1, TILES // 2) as it:
                weigh(2 * it, 0, False)
                weigh(2 * it + 1, 1, False)



_INS = ["x", "L0_conv_mask", "L0_conv_ln1_w", "L0_conv_ln1_b", "L0_conv_pi_w", "L0_conv_pi_b", "L0_conv_gi_w",
        "L0_conv_gi_b", "L0_conv_ln2_w", "L0_conv_ln2_b", "L0_conv_po_w", "L0_conv_po_b", "L0_conv_go_w",
        "L0_conv_go_b", "L0_ffn_W", "L0_ffn_V", "L0_ffn_gamma", "L0_ffn_beta", "L1_conv_mask", "L1_conv_ln_in_w",
        "L1_conv_ln_in_b", "L1_conv_w_ap", "L1_conv_b_ap", "L1_conv_w_ag", "L1_conv_b_ag", "L1_conv_w_bp",
        "L1_conv_b_bp", "L1_conv_w_bg", "L1_conv_b_bg", "L1_conv_ln_out_w", "L1_conv_ln_out_b", "L1_conv_w_z",
        "L1_conv_b_z", "L1_conv_w_g", "L1_conv_b_g", "L1_ffn_router_w", "L1_ffn_router_b", "L1_ffn_expert_w",
        "L1_ffn_expert_b"]


def kernel(**inputs):
    import numpy as _np
    import concourse.bacc as _bacc
    from concourse import mybir as _mybir
    from concourse.bass_utils import run_bass_kernel_spmd as _run

    nc = _bacc.Bacc("TRN2", target_bir_lowering=False, num_devices=1)
    arrays, args = {}, {}
    for name in _INS:
        v = _np.ascontiguousarray(inputs[name])
        arrays[f"in_{name}_dram"] = v
        args[name] = nc.dram_tensor(f"in_{name}_dram", v.shape, _mybir.dt.from_np(v.dtype),
                                    kind="ExternalInput").ap()
    out = nc.dram_tensor("out_0_dram", (1, P, P, C), _mybir.dt.float32, kind="ExternalOutput").ap()
    build(nc, args, out)
    r = _run(nc, [arrays], core_ids=[0])
    return r.results[0]["out_0_dram"]
```

```python
from contextlib import ExitStack

import concourse.bass as bass
from concourse import mybir

ALU = mybir.AluOpType
ACT = mybir.ActivationFunctionType
AX = mybir.AxisListType
F32 = mybir.dt.float32
BF16 = mybir.dt.bfloat16
I32 = mybir.dt.int32

P = 128
C = 32
D2 = C // 2
S = P // C
TILES = P // S
GROUP = 4
GROUPS = TILES // GROUP
BANK = 512
EXPERTS = 8
CHUNK = 16
NCHUNKS = P * P // CHUNK
FIRST = 4
SWEPT = CHUNK - FIRST
EPS_LN = 1e-5
EPS_C = 1e-6
STEPS = 16
POOL_SLOTS = 1
SAME = 2.0 ** -22

RAW = {"A": (0, 64), "C": (64, 192), "G": (192, 224), "Z": (224, 256), "R": (256, 264),
       "E": (264, 520), "W": (520, 552), "V": (552, 584), "gamma": (584, 585), "beta": (585, 586)}
NRAW = 586
RAW_O = (520, 584)
NROW = 584
LN_OF = {"A": 0, "C": 1, "G": 1, "Z": 2, "R": None, "E": None}


def build(nc, a, out):
    ctx = ExitStack()
    with ctx:
        def sb(name, shape, dt=F32):
            return ctx.enter_context(nc.sbuf_tensor(name, shape, dt))

        def sem(name):
            return ctx.enter_context(nc.semaphore(name))

        x = sb("x", [P, P, C])
        centred = sb("centred", [P, P * C])
        squares = sb("squares", [P, P * C])
        gated = sb("gated", [P, 2 * C, P])
        gated_t = sb("gated_t", [P, 2 * C, P])
        prod = sb("prod", [P, C * P])
        out_gate = sb("out_gate", [P, P, C])
        xn = sb("xn", [P, 2, GROUP, P])
        xt = sb("xt", [P, 2, GROUP, P])
        sg = sb("sg", [P, 2, BANK])
        mask_a = sb("mask_a", [P, P])
        mask_c = sb("mask_c", [P, P])
        sums = sb("sums", [P, P])
        mean = sb("mean", [P, P])
        var = sb("var", [P, P])
        sd = sb("sd", [P, P])
        rstd = sb("rstd", [P, P])
        newton = sb("newton", [P, P])
        rstd2 = sb("rstd2", [P, P])
        x_cm = gated[:, 0:C, :]
        y_cm = gated_t[:, 0:C, :]
        ends = sb("ends", [P, 2 * P + 1])
        xd = gated[:, 0:C, :]
        ident = sb("ident", [P, P])
        blk4 = sb("blk4", [P, S])
        blk8 = sb("blk8", [P, 2 * S])
        rep32 = sb("rep32", [C, P])
        rep16 = sb("rep16", [D2, P])
        avg4 = sb("avg4", [P, P])
        raw = sb("raw", [C + 1, NRAW])
        rep_w = sb("rep_w", [P, NRAW + 2 * C])
        raw_s = sb("raw_s", [C, NRAW])
        raw_o = sb("raw_o", [D2 + 1, 2 * C])
        raw_os = sb("raw_os", [D2, 2 * C])
        lnv = sb("lnv", [C, 8])
        lhs_b = sb("lhs_b", [C + 1, 5, P])
        w_a = sb("w_a", [P, 2, S, C])
        w_o = sb("w_o", [P, 2, 2 * S, C])
        w_c = sb("w_c", [P, 2, S, 2 * C])
        w_g = sb("w_g", [P, S, C])
        w_z = sb("w_z", [P, S, C])
        w_r = sb("w_r", [P, S, EXPERTS])
        w_e = sb("w_e", [P, S, EXPERTS * C])
        w_b = sb("w_b", [P, S, C])
        v_b = sb("v_b", [P, S, C])
        w_bt = sb("w_bt", [P, P])
        w_bs = sb("w_bs", [P, P])
        v_t = sb("v_t", [P, P])
        v_next = sb("v_next", [P, P])
        v_wrap = sb("v_wrap", [P, P])
        ones_b = sb("ones_b", [P, P], BF16)
        b_full = sb("b_full", [P, NROW])
        b_hi = sb("b_hi", [P, NROW], BF16)
        b_mid = sb("b_mid", [P, NROW], BF16)
        b_rest = sb("b_rest", [P, NROW])
        b_rest2 = sb("b_rest2", [P, NROW])
        rows = sb("rows", [P, NROW], BF16)
        rows_a = sb("rows_a", [P, 2, S, C], BF16)
        bst = sb("bst", [P, GROUPS, 6])
        mv = sb("mv", [P, 2])
        bn = sb("bn", [P, 12])
        diag = sb("diag", [P, P])
        dif = sb("dif", [P, 2 * P])
        dmax = sb("dmax", [P, 1])
        flag = sb("flag", [1, 2], F32)
        flag_i = sb("flag_i", [1, 1], I32)
        E8 = EXPERTS
        rank = sb("rank", [P, E8])
        lg, pr, eq, sel1, sel2, wgt = (
            gated_t[:, 8 * n:8 * n + 8, :].rearrange("p a b -> p (a b)").rearrange("p (j e) -> p j e", e=E8)
            for n in range(6))
        red = sb("red", [P, 8, P])
        mixed = prod[:, 0:2 * S * E8 * C].rearrange("p (b s e c) -> p b s e c", b=2, s=S, e=E8)

        ps = ctx.enter_context(nc.psum_tensor("ps", [P, 8 * BANK], F32))

        def bank(b, n=1):
            return ps[:, b * BANK:(b + n) * BANK]

        ld_x = [sem(f"ld_x{n}") for n in range(4)]
        ld_m = sem("ld_m")
        ld_mc = sem("ld_mc")
        ld_a = sem("ld_a")
        ld_w = sem("ld_w")
        stored = sem("stored")
        pool_step = sem("pool_step")
        consts = sem("consts")
        a_scaled = sem("a_scaled")
        a_repeated = sem("a_repeated")
        a_built = sem("a_built")
        w_scaled = sem("w_scaled")
        w_repeated = sem("w_repeated")
        w_kept = sem("w_kept")
        o_built = sem("o_built")
        wv_built = sem("wv_built")
        wv_turned = sem("wv_turned")
        wv_kept = sem("wv_kept")
        rest_built = sem("rest_built")
        dve_step = sem("dve_step")

        halved = sem("halved")
        weighed = sem("weighed")
        bn_pe = sem("bn_pe")
        bn_dve = sem("bn_dve")
        e_turn = sem("e_turn")
        e_copy_a = sem("e_copy_a")
        e_copy_v = sem("e_copy_v")
        e_prod = sem("e_prod")
        f_turn = sem("f_turn")
        f_copy_a = sem("f_copy_a")
        f_copy_v = sem("f_copy_v")
        f_prod = sem("f_prod")
        f_kept = sem("f_kept")
        s_step = [sem(f"s_step{st}") for st in range(2)]
        s_state = [sem(f"s_state{st}") for st in range(2)]
        r_step = [sem(f"r_step{st}") for st in range(2)]
        r_state = [sem(f"r_state{st}") for st in range(2)]
        ends_kept = sem("ends_kept")
        ends_again = sem("ends_again")
        flag_turned = sem("flag_turned")
        flag_set = sem("flag_set")
        y_turn = sem("y_turn")
        y_added = sem("y_added")
        d_logits = sem("d_logits")
        chosen = sem("chosen")
        d_exp = sem("d_exp")
        y_again = sem("y_again")
        halves = sem("halves")
        gate_ready = sem("gate_ready")
        gate_kept = sem("gate_kept")
        bn_act = sem("bn_act")
        bn_done = sem("bn_done")
        bn_var = sem("bn_var")

        block = ctx.enter_context(nc.Block())
        steps = [0]

        def chain(eng, ins):
            steps[0] += 1
            ins.then_inc(dve_step, 1)
            eng.wait_ge(dve_step, steps[0])

        class Norm:
            def __init__(self, name, chans, scale, eps):
                self.chans, self.scale, self.eps = chans, scale, eps
                self.meaned = sem(name + "_meaned")
                self.centred = sem(name + "_centred")
                self.squared = sem(name + "_squared")
                self.varied = sem(name + "_varied")
                self.rooted = sem(name + "_rooted")
                self.done = sem(name + "_done")

        QUARTERS = 4
        QT = P // QUARTERS

        def tok(t, q, chans):
            v = t.rearrange("p (j c) -> p j c", c=chans)
            return v[:, q * QT:(q + 1) * QT, :]

        def bcast(v, n):
            return v.unsqueeze(2).to_broadcast([P, v.shape[1], n])

        def norm_dve(dve, nm, src, ready):
            cbuf = centred[:, 0:P * nm.chans]
            sbuf = squares[:, 0:P * nm.chans]

            def second(q):
                dve.wait_ge(nm.squared, q + 1)
                dve.tensor_reduce(var[:, q * QT:(q + 1) * QT], tok(sbuf, q, nm.chans), AX.X,
                                  ALU.add).then_inc(nm.varied, 1)

            for q in range(QUARTERS):
                ready(q)
                cols = slice(q * QT, (q + 1) * QT)
                chain(dve, dve.tensor_reduce(sums[:, cols], src(q), AX.X, ALU.add))
                ins = dve.tensor_scalar(mean[:, cols], sums[:, cols], 1.0 / nm.chans, None, ALU.mult)
                ins.then_inc(nm.meaned, 1)
                if q == 2:
                    second(0)
            second(1)
            dve.wait_ge(nm.meaned, QUARTERS)
            dve.wait_ge(nm.centred, QUARTERS - 1)
            q = QUARTERS - 1
            dve.tensor_tensor(tok(cbuf, q, nm.chans), src(q), bcast(mean[:, q * QT:(q + 1) * QT], nm.chans),
                              ALU.subtract).then_inc(nm.centred, 1)
            second(2)
            second(3)
            dve.wait_ge(nm.varied, QUARTERS)
            dve.tensor_scalar(sd[:, :], var[:, :], nm.scale / nm.chans, nm.eps, ALU.mult,
                              ALU.add).then_inc(nm.varied, 1)
            dve.wait_ge(nm.rooted, 1)
            chain(dve, dve.reciprocal(rstd2[:, :], var[:, :]))
            chain(dve, dve.tensor_tensor(newton[:, :], rstd2[:, :], rstd2[:, :], ALU.mult))
            chain(dve, dve.scalar_tensor_tensor(newton[:, :], newton[:, :], -0.5, sd[:, :], ALU.mult, ALU.mult))
            dve.scalar_tensor_tensor(rstd[:, :], newton[:, :], 1.5, rstd2[:, :], ALU.add,
                                     ALU.mult).then_inc(nm.done, 1)
            dve.wait_ge(nm.done, 1)

        def norm_pool(pool, nm, src):
            cbuf = centred[:, 0:P * nm.chans]
            for q in range(QUARTERS - 1):
                pool.wait_ge(nm.meaned, q + 1)
                pool.tensor_tensor(tok(cbuf, q, nm.chans), src(q),
                                   bcast(mean[:, q * QT:(q + 1) * QT], nm.chans),
                                   ALU.subtract).then_inc(nm.centred, 1)

        def norm_act(act, nm, meanwhile=None):
            n = QT * nm.chans
            for q in range(QUARTERS):
                act.wait_ge(nm.centred, q + 1)
                act.activation(squares[:, q * n:(q + 1) * n], centred[:, q * n:(q + 1) * n],
                               ACT.Square).then_inc(nm.squared, 1)
            if meanwhile:
                meanwhile()
            act.wait_ge(nm.varied, QUARTERS + 1)
            act.activation(var[:, :], sd[:, :], ACT.Sqrt).then_inc(nm.rooted, 1)

        PIECES = ((0, 32), (32, 64), (64, 96), (96, 128))
        LAST = len(PIECES) - 1

        def piece(t, p):
            lo, hi = PIECES[p]
            return t[:, lo:hi]

        def tokens(t, p, chans):
            lo, hi = PIECES[p]
            return t.rearrange("p (j c) -> p j c", c=chans)[:, lo:hi, :]

        def take_mean(dve, nm, src, p, ready, centre=False):
            ready(p)
            chain(dve, dve.tensor_reduce(piece(sums, p), piece(src, p), AX.X, ALU.add))
            dve.tensor_scalar(piece(mean, p), piece(sums, p), 1.0 / nm.chans, None,
                              ALU.mult).then_inc(nm.meaned, 1)
            if centre:
                dve.wait_ge(nm.meaned, p + 1)
                take_centre(dve, nm, src, p)

        def take_centre(eng, nm, src, p):
            eng.tensor_tensor(tokens(centred[:, 0:P * nm.chans], p, nm.chans), piece(src, p),
                              bcast(piece(mean, p), nm.chans), ALU.subtract).then_inc(nm.centred, 1)

        def pool_centre(pool, nm, src, p):
            pool.wait_ge(nm.meaned, p + 1)
            take_centre(pool, nm, src, p)

        def take_square(act, nm, p):
            act.wait_ge(nm.centred, p + 1)
            lo, hi = PIECES[p]
            act.activation(squares[:, lo * nm.chans:hi * nm.chans], centred[:, lo * nm.chans:hi * nm.chans],
                           ACT.Square).then_inc(nm.squared, 1)

        def take_var(dve, nm, p):
            dve.wait_ge(nm.squared, p + 1)
            chain(dve, dve.tensor_reduce(piece(var, p), tokens(squares[:, 0:P * nm.chans], p, nm.chans), AX.X,
                                         ALU.add))
            dve.tensor_scalar(piece(sd, p), piece(var, p), nm.scale / nm.chans, nm.eps, ALU.mult,
                              ALU.add).then_inc(nm.varied, 1)

        def take_root(act, nm, p):
            act.wait_ge(nm.varied, p + 1)
            act.activation(piece(var, p), piece(sd, p), ACT.Sqrt).then_inc(nm.rooted, 1)

        def take_rstd(dve, nm, p):
            dve.wait_ge(nm.rooted, p + 1)
            r2, nw = piece(rstd2, p), piece(newton, p)
            chain(dve, dve.reciprocal(r2, piece(var, p)))
            chain(dve, dve.tensor_tensor(nw, r2, r2, ALU.mult))
            chain(dve, dve.scalar_tensor_tensor(nw, nw, -0.5, piece(sd, p), ALU.mult, ALU.mult))
            dve.scalar_tensor_tensor(piece(rstd, p), nw, 1.5, r2, ALU.add, ALU.mult).then_inc(nm.done, 1)

        def fused_dve(dve, nm, src, ready, scale, gate, centre=False, meanwhile=None, late=None):
            def mean_of(p):
                take_mean(dve, nm, src, p, ready, centre or p == 0)

            def rstd_of(p):
                take_rstd(dve, nm, p)
                dve.wait_ge(nm.done, p + 1)

            mean_of(0)
            mean_of(1)
            if centre:
                mean_of(2)
                mean_of(3)
            if meanwhile:
                meanwhile()
            take_var(dve, nm, 0)
            rstd_of(0)
            scale(0, 0, True)
            scale(1, 1, True)
            take_var(dve, nm, 1)
            if centre:
                take_var(dve, nm, 2)
                take_var(dve, nm, 3)
                rstd_of(1)
                scale(2, 0, False)
                rstd_of(2)
                rstd_of(3)
                gate(0, 0, True)
                scale(3, 1, False)
                gate(1, 1, True)
            else:
                mean_of(2)
                rstd_of(1)
                scale(2, 0, False)
                mean_of(3)
                take_var(dve, nm, 2)
                gate(0, 0, True)
                scale(3, 1, False)
                take_var(dve, nm, 3)
                gate(1, 1, True)
                rstd_of(2)
                rstd_of(3)
            with dve.Fori(2, GROUPS // 2) as it:
                for b in range(2):
                    scale(2 * it + b, b, False)
                    gate(2 * it + b - 2, b, False)
            if late:
                late()
            gate(GROUPS - 2, 0, False)
            gate(GROUPS - 1, 1, False)

        def fused_pool(pool, nm, src, work):
            pool.wait_ge(nm.centred, 1)
            for p in range(1, len(PIECES)):
                pool_centre(pool, nm, src, p)
            with pool.Fori(0, GROUPS // 2) as it:
                work(2 * it, 0, False)
                work(2 * it + 1, 1, False)

        def fused_act(act, nm, copy, gate, centre=False):
            take_square(act, nm, 0)
            if centre:
                take_square(act, nm, 1)
                take_square(act, nm, 2)
                take_square(act, nm, 3)
                take_root(act, nm, 0)
            else:
                take_root(act, nm, 0)
                take_square(act, nm, 1)
            copy(0, 0, True)
            copy(1, 1, True)
            take_root(act, nm, 1)
            if centre:
                take_root(act, nm, 2)
                take_root(act, nm, 3)
            else:
                take_square(act, nm, 2)
            gate(0, 0, True)
            copy(2, 0, False)
            if not centre:
                take_square(act, nm, 3)
            gate(1, 1, True)
            copy(3, 1, False)
            if not centre:
                take_root(act, nm, 2)
                take_root(act, nm, 3)
            gate(2, 0, False)
            for g in range(4, GROUPS):
                copy(g, g % 2, False)
                gate(g - 1, (g - 1) % 2, False)
            gate(GROUPS - 1, 1, False)

        both = dict(scale=1.0 + EPS_LN, eps=EPS_LN * EPS_C)
        n_a = Norm("na", C, **both)
        n_o = Norm("no", D2, 1.0, EPS_LN)
        n_b = Norm("nb", C, 1.0, EPS_LN)
        n_c = Norm("nc", C, **both)
        n_z = Norm("nz", C, 1.0, EPS_LN)
        n_d = Norm("nd", C, 1.0, EPS_LN)

        def x_q(q):
            return x[:, q * QT:(q + 1) * QT, :]

        prod_t = prod[:, :].rearrange("p (c j) -> p j c", j=P)

        class Proj:
            def __init__(self, name):
                self.scaled = sem(name + "_scaled")
                self.turned = sem(name + "_turned")
                self.copied = sem(name + "_copied")
                self.projected = sem(name + "_projected")
                self.gates = sem(name + "_gates")
                self.masked = sem(name + "_masked")
                self.used = sem(name + "_used")
                self.added = sem(name + "_added")

        p_a, p_o, p_b, p_c, p_z, p_d = (Proj(n) for n in ("pa", "po", "pb", "pc", "pz", "pd"))

        def groups(eng, head, tail, last=True):
            head(0, 0, True)
            head(1, 1, True)
            tail(0, 0, True)
            with eng.Fori(1, GROUPS // 2) as it:
                head(2 * it, 0, False)
                tail(2 * it - 1, 1, False)
                head(2 * it + 1, 1, False)
                tail(2 * it, 0, False)
            tail(GROUPS - 1, 1, False)

        def groups_straight(eng, head, tail):
            for g in range(GROUPS):
                head(g, g % 2, g < 2)
                if g:
                    tail(g - 1, (g - 1) % 2, g - 1 < 2)
            tail(GROUPS - 1, 1, False)

        def groups_ahead(eng, head, tail):
            head(0, 0, True)
            head(1, 1, True)
            for g in (2, 3):
                head(g, g % 2, False)
                tail(g - 2, g % 2, True)
            with eng.Fori(2, GROUPS // 2) as it:
                head(2 * it, 0, False)
                tail(2 * it - 2, 0, False)
                head(2 * it + 1, 1, False)
                tail(2 * it - 1, 1, False)
            tail(GROUPS - 2, 0, False)
            tail(GROUPS - 1, 1, False)

        def nothing(g, s, early):
            pass

        def scale_group(dve, pj, width):
            ntok = 16

            def f(g, s, early):
                if not early:
                    dve.wait_ge(pj.turned, g - 1)
                src = centred[:, 0:P * width].rearrange("p (g t c) -> p g t c", t=ntok, c=width)
                r = rstd[:, :].rearrange("p (g t) -> p g t", t=ntok)
                dst = xn[:, s, :, :].rearrange("p a b -> p (a b)")[:, 0:ntok * width]
                rg = r[:, bass.ds(g, 1), :].rearrange("p a t -> p (a t)")
                dve.tensor_tensor(dst.rearrange("p (t c) -> p t c", c=width),
                                  src[:, bass.ds(g, 1), :, :].rearrange("p a t c -> p (a t) c"),
                                  bcast(rg, width), ALU.mult).then_inc(pj.scaled, 1)
            return f

        def turn_group(pe, pj, tiles=GROUP):
            def f(g, s, early):
                pe.wait_ge(pj.scaled, g + 1)
                if not early:
                    pe.wait_ge(pj.copied, g - 1)
                for t in range(tiles):
                    ins = pe.transpose(bank(s)[:, t * P:(t + 1) * P], xn[:, s, t, :], ident[:, :])
                ins.then_inc(pj.turned, 1)
            return f

        def copy_group(act, pj, tiles=GROUP):
            def f(g, s, early):
                act.wait_ge(pj.turned, g + 1)
                if not early:
                    act.wait_ge(pj.projected, g - 1)
                act.activation(xt[:, s, 0:tiles, :].rearrange("p a b -> p (a b)"),
                               bank(s)[:, 0:tiles * P], ACT.Copy).then_inc(pj.copied, 1)
            return f

        def row(v):
            return v.rearrange("(a n) -> a n", a=1)

        def col(v):
            return v.rearrange("(n a) -> n a", a=1)

        def weights_a():
            return [(lnv[:, 0:1], col(a["L0_conv_ln1_w"])),
                    (raw[0:C, 0:C], a["L0_conv_pi_w"]),
                    (raw[0:C, C:2 * C], a["L0_conv_gi_w"]),
                    (lnv[:, 1:2], col(a["L0_conv_ln1_b"])),
                    (raw[C:C + 1, 0:C], row(a["L0_conv_pi_b"])),
                    (raw[C:C + 1, C:2 * C], row(a["L0_conv_gi_b"]))]

        def weights():
            w = [(raw_o[0:D2, 0:C], a["L0_conv_po_w"]),
                 (raw_o[0:D2, C:2 * C], a["L0_conv_go_w"]),
                 (raw_o[D2:D2 + 1, 0:C], row(a["L0_conv_po_b"])),
                 (raw_o[D2:D2 + 1, C:2 * C], row(a["L0_conv_go_b"])),
                 (lnv[0:D2, 6:7], col(a["L0_conv_ln2_w"])),
                 (lnv[0:D2, 7:8], col(a["L0_conv_ln2_b"]))]
            for n, k in enumerate(("ag", "bg", "ap", "bp", "g", "z")):
                w.append((raw[0:C, 64 + 32 * n:96 + 32 * n], a["L1_conv_w_" + k]))
                w.append((raw[C:C + 1, 64 + 32 * n:96 + 32 * n], row(a["L1_conv_b_" + k])))
            for n, k in ((1, "L1_conv_ln_in_"), (2, "L1_conv_ln_out_")):
                w.append((lnv[:, 2 * n:2 * n + 1], col(a[k + "w"])))
                w.append((lnv[:, 2 * n + 1:2 * n + 2], col(a[k + "b"])))
            w.append((raw[0:C, 256:264], a["L1_ffn_router_w"]))
            w.append((raw[C:C + 1, 256:264], row(a["L1_ffn_router_b"])))
            w.append((raw[0:C, 264:520].rearrange("d (e c) -> d e c", e=EXPERTS),
                      a["L1_ffn_expert_w"].rearrange("e d c -> d e c")))
            w.append((raw[C:C + 1, 264:520], row(a["L1_ffn_expert_b"].rearrange("e c -> (e c)"))))
            w.append((raw[0:C, 520:552], a["L0_ffn_W"]))
            w.append((raw[0:C, 552:584], a["L0_ffn_V"]))
            w.append((raw[0:C, 584:585], col(a["L0_ffn_gamma"])))
            w.append((raw[0:C, 585:586], col(a["L0_ffn_beta"])))
            return w

        @block.sync
        def _(sp):
            def load_x(q):
                sp.dma_start(x_q(q), a["x"][0, :, q * QT:(q + 1) * QT, :]).then_inc(ld_x[q], 16)

            load_x(0)
            load_x(1)
            for dst, src in weights_a()[3:]:
                sp.dma_start(dst, src).then_inc(ld_a, 16)
            load_x(2)
            load_x(3)
            sp.dma_start(mask_a[:, :], a["L0_conv_mask"][0]).then_inc(ld_m, 16)
            for dst, src in weights():
                sp.dma_start(dst, src).then_inc(ld_w, 16)
            sp.dma_start(mask_c[:, :], a["L1_conv_mask"][0]).then_inc(ld_mc, 16)
            for g in range(GROUPS):
                sp.wait_ge(p_d.added, 4 * (g + 1))
                sp.dma_start(out[0, :, 16 * g:16 * g + 16, :], x[:, 16 * g:16 * g + 16, :]).then_inc(stored, 16)
            sp.wait_ge(stored, 16 * GROUPS)

        def split_rows(eng, chained, lo, hi):
            c = slice(lo, hi)
            chained(eng, eng.tensor_copy(b_hi[:, c], b_full[:, c]))
            chained(eng, eng.tensor_tensor(b_rest[:, c], b_full[:, c], b_hi[:, c], ALU.subtract))
            chained(eng, eng.tensor_copy(b_mid[:, c], b_rest[:, c]))
            chained(eng, eng.tensor_tensor(b_rest2[:, c], b_rest[:, c], b_mid[:, c], ALU.subtract))
            chained(eng, eng.tensor_copy(rows[0:1, c], b_hi[0:1, c]))
            chained(eng, eng.tensor_copy(rows[32:33, c], b_mid[32:33, c]))
            chained(eng, eng.tensor_copy(rows[64:65, c], b_rest2[64:65, c]))

        def block_diag(eng, dst, src, blk, nb, cols):
            return eng.tensor_tensor(dst, src.unsqueeze(1).to_broadcast([P, nb, cols]),
                                     blk[:, :].unsqueeze(2).to_broadcast([P, nb, cols]), ALU.mult)

        @block.gpsimd
        def _(pool):
            psteps = [0]

            def then(eng, ins):
                psteps[0] += 1
                ins.then_inc(pool_step, 1)
                eng.wait_ge(pool_step, psteps[0])

            def select(t, w, op, fill, base, mult, pattern):
                v = t[:, :].rearrange("p (a b) -> p a b", b=w) if w else t[:, :]
                return pool.affine_select(out=v, in_=v, compare_op=op, fill=fill, base=base,
                                          pattern=pattern, channel_multiplier=mult)

            pool.memset(blk4[:, :], 1.0)
            pool.memset(blk8[:, :], 1.0)
            pool.memset(ident[:, :], 0.0)
            pool.memset(rep32[:, :], 0.0)
            then(pool, pool.memset(rep16[:, :], 0.0))
            select(blk4, 0, ALU.is_ge, 0.0, 0, 1, [[-C, S]])
            then(pool, select(blk8, 0, ALU.is_ge, 0.0, 0, 1, [[-D2, 2 * S]]))
            select(blk4, 0, ALU.is_ge, 0.0, C - 1, -1, [[C, S]])
            select(blk8, 0, ALU.is_ge, 0.0, D2 - 1, -1, [[D2, 2 * S]])
            select(ident, 0, ALU.not_equal, 1.0, 0, 1, [[-1, P]])
            select(rep32, C, ALU.not_equal, 1.0, 0, 1, [[0, P // C], [-1, C]])
            select(rep16, D2, ALU.not_equal, 1.0, 0, 1, [[0, P // D2], [-1, D2]]).then_inc(consts, 1)
            pool.wait_ge(consts, 1)

            for e in range(EXPERTS):
                pool.memset(rank[:, e:e + 1], float(EXPERTS - e))
            pool.wait_ge(ld_m, 16)

            def mask_gated(pj, msk, chans, per):
                def f(g, s, early):
                    n = 16 // per
                    for h in range(per):
                        pool.wait_ge(pj.used, per * g + h + 1)
                        m = msk[:, :].rearrange("p (g k) -> p g k", k=n)[:, bass.ds(per * g + h, 1), :]
                        v = gated[:, 0:chans, :].rearrange("p o (g k) -> p g o k", k=n)
                        v = v[:, bass.ds(per * g + h, 1), :, :].rearrange("p a o k -> p (a o) k")
                        pool.tensor_tensor(v, v, m.to_broadcast([P, chans, n]), ALU.mult).then_inc(pj.masked, 1)
                return f

            fused_pool(pool, n_a, x, mask_gated(p_a, mask_a, C, 1))
            pool.wait_ge(w_kept, 1)
            for h in range(2):
                block_diag(pool, w_o[:, h, :, :], rep_w[:, NRAW + C * h:NRAW + C * (h + 1)], blk8, 2 * S, C)
            split_rows(pool, then, *RAW_O)
            pool.drain().then_inc(o_built, 1)
            block_diag(pool, w_b[:, :, :], rep_w[:, 520:552], blk4, S, C)
            block_diag(pool, v_b[:, :, :], rep_w[:, 552:584], blk4, S, C).then_inc(wv_built, 1)

            def add_out(pj):
                def f(g, s, early):
                    pool.wait_ge(pj.used, g + 1)
                    v = x[:, :, :].rearrange("p (g t) c -> p g (t c)", t=16)[:, bass.ds(g, 1), :]
                    v = v.rearrange("p a n -> p (a n)")
                    pool.tensor_tensor(v, v, sg[:, s, :], ALU.add).then_inc(pj.added, 1)
                return f

            def mask_and_add(g, s, early):
                pool.wait_ge(p_o.used, g + 1)
                m = mask_a[:, :].rearrange("p (g t) -> p g t", t=16)[:, bass.ds(g, 1), :]
                v = sg[:, s, :].rearrange("p (t o) -> p t o", o=C)
                pool.tensor_tensor(v, v, bcast(m.rearrange("p a t -> p (a t)"), C),
                                   ALU.mult).then_inc(p_o.masked, 1)
                pool.wait_ge(p_o.masked, g + 1)
                add_out(p_o)(g, s, early)

            with pool.Fori(0, GROUPS // 2) as it:
                mask_and_add(2 * it, 0, False)
                mask_and_add(2 * it + 1, 1, False)

            norm_pool(pool, n_b, x_q)
            split_rows(pool, then, 64, 520)
            for h in range(2):
                block_diag(pool, w_c[:, h, :, :], rep_w[:, 64 + 64 * h:128 + 64 * h], blk4, S, 2 * C)
            block_diag(pool, w_g[:, :, :], rep_w[:, 192:224], blk4, S, C)
            block_diag(pool, w_z[:, :, :], rep_w[:, 224:256], blk4, S, C)
            block_diag(pool, w_r[:, :, :], rep_w[:, 256:264], blk4, S, EXPERTS)
            then(pool, block_diag(pool, w_e[:, :, :], rep_w[:, 264:520], blk4, S, EXPERTS * C))
            pool.drain().then_inc(rest_built, 1)
            pool.wait_ge(ld_mc, 16)


            fused_pool(pool, n_c, x, mask_gated(p_c, mask_c, 2 * C, 2))
            fused_pool(pool, n_z, prod_t, add_out(p_z))

            def scale_d(p):
                pool.wait_ge(n_d.done, p + 1)
                lo, hi = PIECES[p]
                for g in range(lo // 16, hi // 16):
                    scale_group(pool, p_d, C)(g, g % 2, g < 2)

            pool.wait_ge(n_d.centred, 1)
            pool_centre(pool, n_d, x, 1)
            for p in range(len(PIECES)):
                scale_d(p)
                if p + 2 <= LAST:
                    pool_centre(pool, n_d, x, p + 2)

            def reduce_experts(u, s):
                m = mixed[:, s, :, :, :]
                n = EXPERTS // 2
                mine = m[:, S - POOL_SLOTS:S, :, :]
                pool.wait_ge(weighed, u + 1)
                pool.tensor_tensor(mine[:, :, 0:n, :], mine[:, :, 0:n, :], mine[:, :, n:2 * n, :],
                                   ALU.add).then_inc(halved, 1)
                pool.wait_ge(p_d.used, u + 1)
                for lvl in range(2):
                    pool.wait_ge(halved, 3 * u + lvl + 1)
                    n //= 2
                    pool.tensor_tensor(m[:, :, 0:n, :], m[:, :, 0:n, :], m[:, :, n:2 * n, :],
                                       ALU.add).then_inc(halved, 1)
                pool.wait_ge(halved, 3 * u + 3)
                v = x[:, :, :].rearrange("p (u t) c -> p u t c", t=S)[:, bass.ds(u, 1), :, :]
                v = v.rearrange("p a t c -> p (a t) c")
                pool.tensor_tensor(v, v, m[:, :, 0, :], ALU.add).then_inc(p_d.added, 1)

            with pool.Fori(0, TILES // 2) as it:
                reduce_experts(2 * it, 0)
                reduce_experts(2 * it + 1, 1)


        def flat(t, J):
            return t[:, bass.ds(J, 1), :].rearrange("p a i -> p (a i)") if not isinstance(J, int) else t[:, J, :]

        def sweep_pe(pe, stepped, state, base, first=False):
            def summed(st, k, b):
                return bank(2 + 2 * st + b)[:, 0:P]

            def step(k, b):
                for st in range(2):
                    pe.matmul(summed(st, k, b), w_bs[:, :], flat(x_cm, CHUNK * st + k), start=True,
                              stop=False, skip_group_check=True)
                for st in range(2):
                    pe.wait_ge(state[st], base + k)
                    pe.matmul(summed(st, k, b), v_t[:, :], flat(y_cm, CHUNK * st + k - 1), start=False,
                              stop=True, skip_group_check=True).then_inc(stepped[st], 1)

            if first:
                for st in range(2):
                    pe.matmul(summed(st, FIRST, FIRST % 2), w_bs[:, :], x_cm[:, CHUNK * st + FIRST, :],
                              start=True, stop=True, skip_group_check=True).then_inc(stepped[st], 1)
                begin = FIRST + 1
            else:
                pe.matmul(summed(0, 0, 0), w_bs[:, :], x_cm[:, 0, :], start=True, stop=False,
                          skip_group_check=True)
                pe.matmul(summed(0, 0, 0), v_next[:, :], ends[:, 1:P + 1], start=False, stop=False,
                          skip_group_check=True)
                pe.matmul(summed(0, 0, 0), v_wrap[:, :], ends[:, 0:P], start=False, stop=True,
                          skip_group_check=True).then_inc(stepped[0], 1)
                pe.matmul(summed(1, 0, 0), w_bs[:, :], x_cm[:, CHUNK, :], start=True, stop=False,
                          skip_group_check=True)
                pe.matmul(summed(1, 0, 0), v_t[:, :], ends[:, P + 1:2 * P + 1], start=False, stop=True,
                          skip_group_check=True).then_inc(stepped[1], 1)
                begin = 1
            for k in range(begin, begin + 3):
                step(k, k % 2)
            body = (CHUNK - begin - 3) // 2
            with pe.Fori(0, 2) as it:
                for k in range(body):
                    step(body * it + begin + 3 + k, (begin + 3 + k) % 2)

        def sweep_act(act, stepped, state, base, first=0):
            for k in range(first, CHUNK):
                for st in range(2):
                    act.wait_ge(stepped[st], base + k + 1)
                    act.activation(y_cm[:, CHUNK * st + k, :], bank(2 + 2 * st + k % 2)[:, 0:P],
                                   ACT.Sigmoid, bias=bn[:, 9:10]).then_inc(state[st], 1)

        def keep_ends(dve, signal):
            dve.tensor_copy(ends[:, 1:P + 1], y_cm[:, 2 * CHUNK - 1, :])
            dve.tensor_copy(ends[:, P + 1:2 * P + 1], y_cm[:, CHUNK - 1, :]).then_inc(signal, 1)

        def logits_at(q):
            return 0 if isinstance(q, int) and q == 0 else QUARTERS - q

        @block.tensor
        def _(pe):
            def repeat(dst, src, lhs, signal=None):
                ins = pe.matmul(dst, lhs, src, start=True, stop=True, skip_group_check=True)
                if signal:
                    ins.then_inc(signal, 1)

            pe.wait_ge(consts, 1)
            pe.wait_ge(a_scaled, 1)
            repeat(bank(6)[:, 0:64], raw_s[:, 0:64], rep32[:, :])
            repeat(bank(6)[:, 64:128], raw[:, 0:64], lhs_b[:, 0, :], a_repeated)
            repeat(bank(7)[:, 0:P], rep32[:, :], rep32[:, :], a_repeated)
            pe.wait_ge(a_built, 1)

            def bias_into(b, key, start=True):
                lo, hi = RAW_O if key == "O" else RAW[key]
                r = rows[:, lo:hi]
                n = hi - lo
                if key == "A":
                    v = rows_a[:, :, :, :].rearrange("p h s o -> p (h s o)").unsqueeze(1)
                    pe.matmul(b.rearrange("p (t n) -> p t n", t=2), ones_b[:, :],
                              v.to_broadcast([P, 2, 2 * S * C]), start=True, stop=False,
                              skip_group_check=True)
                elif key in ("O", "C"):
                    w = n // 2
                    k = BANK // n
                    v = r.rearrange("p (h o) -> p h o", h=2).unsqueeze(2).to_broadcast([P, 2, k, w])
                    pe.matmul(b.rearrange("p (h s o) -> p h s o", h=2, s=k), ones_b[:, :], v, start=True,
                              stop=False, skip_group_check=True)
                else:
                    k = BANK // n
                    pe.matmul(b.rearrange("p (k o) -> p k o", k=k), ones_b[:, :],
                              r.unsqueeze(1).to_broadcast([P, k, n]), start=True, stop=False,
                              skip_group_check=True)

            def project(pj, key, mms, per):
                def f(g, s, early):
                    pe.wait_ge(pj.copied, g + 1)
                    if not early:
                        pe.wait_ge(pj.used, g - 1)
                    if s == 1 and key == "O":
                        pe.wait_ge(n_o.centred, len(PIECES))
                    for h in range(2):
                        b = bank(2 + 2 * s + h)
                        bias_into(b, key)
                        for t in range(per):
                            n = BANK // per
                            ins = pe.matmul(b[:, t * n:(t + 1) * n], xt[:, s, per * h + t, :], mms,
                                            start=False, stop=(t == per - 1), skip_group_check=True)
                    ins.then_inc(pj.projected, 1)
                return f

            groups(pe, turn_group(pe, p_a),
                   project(p_a, "A", w_a[:, :, :, :].rearrange("p h s c -> p (h s c)"), 2))
            pe.wait_ge(w_scaled, 1)
            pe.wait_ge(p_a.copied, GROUPS)
            repeat(bank(6), raw_s[:, 0:BANK], rep32[:, :])
            repeat(bank(7)[:, 0:NRAW - BANK], raw_s[:, BANK:NRAW], rep32[:, :])
            repeat(bank(7)[:, NRAW - BANK:NRAW - BANK + 2 * C], raw_os[:, :], rep16[:, :])
            repeat(bank(7)[:, 256:256 + 2 * C], raw_o[:, :], lhs_b[0:D2 + 1, 3, :])
            for key in ("C", "G", "Z", "R", "E"):
                lo, hi = RAW[key]
                ln = LN_OF[key]
                repeat(bank(0)[:, lo - 64:hi - 64], raw[:, lo:hi], lhs_b[:, 4 if ln is None else ln, :],
                       w_repeated if key == "E" else None)
            pe.wait_ge(p_a.masked, GROUPS)
            for q in range(4):
                if q == 3:
                    pe.wait_ge(w_kept, 1)
                for t in range(4):
                    ins = pe.transpose(bank((q + 1) % 4)[:, t * P:(t + 1) * P], gated[:, 4 * q + t, :], ident[:, :])
                ins.then_inc(e_turn, 1)
            for d in range(8):
                b = bank(6 + d // 4)
                ins = pe.matmul(b[:, (d % 4) * P:(d % 4 + 1) * P], gated[:, 16 + d, :], gated[:, 24 + d, :],
                                start=True, stop=True, skip_group_check=True)
            pe.wait_ge(e_copy_a, 2)
            pe.wait_ge(e_copy_v, 2)
            for d in range(8):
                b = bank(4 + d // 4)
                ins = pe.matmul(b[:, (d % 4) * P:(d % 4 + 1) * P], gated_t[:, d, :], gated_t[:, 8 + d, :],
                                start=True, stop=True, skip_group_check=True)
            ins.then_inc(e_prod, 1)
            pe.wait_ge(o_built, 1)
            groups(pe, turn_group(pe, p_o, 2),
                   project(p_o, "O", w_o[:, :, :, :].rearrange("p h s c -> p (h s c)"), 1))

            pe.wait_ge(wv_built, 1)
            pe.transpose(bank(6)[:, 0:P], w_b[:, :, :].rearrange("p s c -> p (s c)"), ident[:, :])
            pe.transpose(bank(6)[:, P:2 * P], v_b[:, :, :].rearrange("p s c -> p (s c)"),
                         ident[:, :]).then_inc(wv_turned, 1)
            pe.wait_ge(wv_kept, 1)

            def wx(g, s, early):
                pe.wait_ge(p_b.copied, g + 1)
                if not early:
                    pe.wait_ge(p_b.used, g - 1)
                v = x_cm.rearrange("p (g t) i -> p g (t i)", t=GROUP)[:, bass.ds(g, 1), :]
                pe.matmul(bank(2 + s), w_bt[:, :], v.rearrange("p a n -> p (a n)"), start=True,
                          stop=True).then_inc(p_b.projected, 1)

            groups(pe, turn_group(pe, p_b), wx)
            pe.wait_ge(bn_dve, 1)
            pe.matmul(bank(4)[:, 0:1], avg4[:, :], mv[:, 0:1], start=True, stop=True).then_inc(bn_pe, 1)
            pe.wait_ge(bn_dve, 2)
            pe.matmul(bank(4)[:, 0:1], avg4[:, :], bn[:, 2:3], start=True, stop=True).then_inc(bn_pe, 1)
            pe.wait_ge(bn_dve, 3)
            pe.matmul(bank(4)[:, 0:P], w_b[:, :, :].rearrange("p s c -> p (s c)"), diag[:, :],
                      start=True, stop=True).then_inc(bn_pe, 1)
            pe.wait_ge(bn_dve, 4)

            sweep_pe(pe, s_step, s_state, -FIRST, True)
            pe.wait_ge(ends_kept, 1)
            sweep_pe(pe, s_step, s_state, SWEPT)

            def turn_y(g):
                for t in range(GROUP):
                    ins = pe.transpose(bank(g)[:, t * P:(t + 1) * P], y_cm[:, GROUP * g + t, :], ident[:, :])
                return ins

            for st in range(2):
                pe.wait_ge(s_state[st], SWEPT + CHUNK)
            for g in (0, 1, 2):
                turn_y(g).then_inc(y_turn, 1)
            pe.wait_ge(ends_kept, 2)
            pe.transpose(bank(6)[0:1, 0:P], dmax[:, :], ident[:, :]).then_inc(flag_turned, 1)
            for g in (3, 4, 5, 7):
                turn_y(g).then_inc(y_turn, 1)
            pe.wait_ge(flag_set, 1)
            again = pe.value_load(flag_i[0:1, 0:1], min_val=0, max_val=1)
            with pe.If(again > 0):
                with pe.Fori(0, NCHUNKS - 1) as n:
                    pe.wait_ge(ends_again, n + 1)
                    sweep_pe(pe, r_step, r_state, n * CHUNK)
                for st in range(2):
                    pe.wait_ge(r_state[st], (NCHUNKS - 1) * CHUNK)
                for g in (0, 1, 2, 3, 4, 5, 7):
                    turn_y(g).then_inc(y_again, 1)
            turn_y(6).then_inc(y_turn, 1)

            pe.wait_ge(rest_built, 1)

            def project_c(g, s, early):
                pe.wait_ge(p_c.copied, g + 1)
                bias_into(bank(6 + s), "G")
                for t in range(GROUP):
                    ins = pe.matmul(bank(6 + s)[:, t * P:(t + 1) * P], xt[:, s, t, :],
                                    w_g[:, :, :].rearrange("p s c -> p (s c)"), start=False,
                                    stop=(t == 3), skip_group_check=True)
                ins.then_inc(gate_ready, 1)
                for h in range(2):
                    if not (early and s == 0):
                        pe.wait_ge(p_c.used, 2 * g + h - 1)
                    for t in range(2):
                        b = bank(2 + 2 * h + t)
                        bias_into(b, "C")
                        ins = pe.matmul(b, xt[:, s, 2 * h + t, :],
                                        w_c[:, :, :, :].rearrange("p h s c -> p (h s c)"),
                                        start=False, stop=True, skip_group_check=True)
                    ins.then_inc(halves, 1)
            groups(pe, turn_group(pe, p_c), project_c)
            pe.wait_ge(p_c.masked, 2 * GROUPS)
            def c_products(q):
                b = bank(4 + q % 2)
                pe.wait_ge(f_copy_a, q + 1)
                pe.wait_ge(f_copy_v, q + 1)
                if q >= 2:
                    pe.wait_ge(f_kept, q - 1)
                for t in range(4):
                    ins = pe.matmul(b[:, t * P:(t + 1) * P], gated_t[:, 4 * q + t, :],
                                    gated_t[:, C + 4 * q + t, :], start=True, stop=True, skip_group_check=True)
                ins.then_inc(f_prod, 1)

            for q in range(8):
                if q >= 2:
                    pe.wait_ge(f_copy_a, q - 1)
                    pe.wait_ge(f_copy_v, q - 1)
                for t in range(4):
                    pe.transpose(bank(q % 2)[:, t * P:(t + 1) * P], gated[:, 4 * q + t, :], ident[:, :])
                for t in range(4):
                    ins = pe.transpose(bank(2 + q % 2)[:, t * P:(t + 1) * P], gated[:, C + 4 * q + t, :],
                                       ident[:, :])
                ins.then_inc(f_turn, 1)
                if q:
                    c_products(q - 1)
            c_products(7)

            def project_z(g, s, early):
                pe.wait_ge(p_z.copied, g + 1)
                if not early:
                    pe.wait_ge(p_z.used, g - 1)
                bias_into(bank(2 + s), "Z")
                for t in range(GROUP):
                    ins = pe.matmul(bank(2 + s)[:, t * P:(t + 1) * P], xt[:, s, t, :],
                                    w_z[:, :, :].rearrange("p s c -> p (s c)"), start=False,
                                    stop=(t == 3), skip_group_check=True)
                ins.then_inc(p_z.projected, 1)

            groups(pe, turn_group(pe, p_z), project_z)

            pe.wait_ge(p_z.used, GROUPS)
            for b in range(2):
                bias_into(bank(2 + b), "R")

            def router(g):
                pe.wait_ge(p_d.copied, g + 1)
                if g == GROUPS - 2:
                    pe.wait_ge(chosen, 2)
                for t in range(GROUP):
                    u = GROUP * g + t
                    n = S * EXPERTS
                    at = logits_at(g // 2) * QT * EXPERTS + u % (TILES // QUARTERS) * n
                    ins = pe.matmul(bank(2, 2)[:, at:at + n], xd[:, u, :],
                                    w_r[:, :, :].rearrange("p s e -> p (s e)"), start=False, stop=True,
                                    skip_group_check=True)
                if g % 2:
                    ins.then_inc(d_logits, 1)

            turn = turn_group(pe, p_d)
            def experts(u):
                s = u % 2
                if u >= 2:
                    pe.wait_ge(weighed, u - 1)
                for h in range(2):
                    b = bank(4 + 2 * s + h)
                    bias_into(b, "E")
                    ins = pe.matmul(b, xd[:, u, :],
                                    w_e[:, :, :].rearrange("p s n -> p (s n)")[:, h * BANK:(h + 1) * BANK],
                                    start=False, stop=True, skip_group_check=True)
                ins.then_inc(p_d.projected, 1)

            for g in range(GROUPS):
                turn(g, g % 2, g < 2)
                if g:
                    router(g - 1)
                if g == GROUPS - 3:
                    experts(0)
                    experts(1)
            router(GROUPS - 1)
            for u in range(2, TILES):
                experts(u)


        @block.scalar
        def _(act):
            for dst, src in weights_a()[:3]:
                act.dma_start(dst, src).then_inc(ld_a, 16)

            def gates(pj, nbank):
                def f(g, s, early):
                    act.wait_ge(pj.projected, g + 1)
                    if not early:
                        act.wait_ge(gates_free[pj], g - 1)
                    v = bank(2 + 2 * s, 2).rearrange("p (t h n) -> p t h n", h=2, n=nbank)[:, :, 1, :]
                    act.activation(sg[:, s, :].rearrange("p (t n) -> p t n", n=nbank), v,
                                   ACT.Sigmoid).then_inc(pj.gates, 1)
                return f

            gates_free = {p_a: p_a.used, p_o: p_o.added}

            fused_act(act, n_a, copy_group(act, p_a), gates(p_a, P))
            def keep_weights():
                act.wait_ge(w_repeated, 1)
                act.activation(rep_w[:, :], bank(6, 2)[:, 0:NRAW + 2 * C], ACT.Copy)
                act.activation(b_full[:, 520:584], bank(7)[:, 256:320], ACT.Copy)
                act.activation(b_full[:, 64:520], bank(0)[:, 0:456], ACT.Copy).then_inc(w_kept, 1)

            keep_weights()
            for n, q in enumerate((0, 2)):
                act.wait_ge(e_turn, q + 1)
                act.activation(gated_t[:, 4 * q:4 * q + 4, :].rearrange("p a b -> p (a b)"),
                               bank(q + 1), ACT.Copy).then_inc(e_copy_a, 1)
            fused_act(act, n_o, copy_group(act, p_o, 2), gates(p_o, 2 * P), centre=True)

            def keep_wv():
                act.wait_ge(wv_turned, 1)
                act.activation(w_bt[:, :], bank(6)[:, 0:P], ACT.Copy)
                act.activation(v_t[:, :], bank(6)[:, P:2 * P], ACT.Copy)
                act.activation(v_next[:, C:P], bank(6)[:, P:2 * P - C], ACT.Copy)
                act.activation(v_wrap[P - C:P, 0:C], bank(6)[P - C:P, 2 * P - C:2 * P],
                               ACT.Copy).then_inc(wv_kept, 1)

            norm_act(act, n_b, keep_wv)

            def copy_b(g, s, early):
                act.wait_ge(p_b.turned, g + 1)
                v = x_cm.rearrange("p (g t) i -> p g (t i)", t=GROUP)[:, bass.ds(g, 1), :]
                act.activation(v.rearrange("p a n -> p (a n)"), bank(s), ACT.Copy).then_inc(p_b.copied, 1)

            groups_straight(act, copy_b, nothing)
            act.wait_ge(bn_var, 1)
            act.activation(bn[:, 4:5], bn[:, 3:4], ACT.Sqrt).then_inc(bn_act, 1)
            act.wait_ge(bn_done, 1)
            sweep_act(act, s_step, s_state, -FIRST, FIRST)
            act.wait_ge(ends_kept, 1)
            sweep_act(act, s_step, s_state, SWEPT)
            act.wait_ge(flag_set, 1)
            again = act.value_load(flag_i[0:1, 0:1], min_val=0, max_val=1)
            with act.If(again > 0):
                with act.Fori(0, NCHUNKS - 1) as n:
                    act.wait_ge(ends_again, n + 1)
                    sweep_act(act, r_step, r_state, n * CHUNK)

            def copy_c(g, s, early):
                act.wait_ge(p_c.turned, g + 1)
                if not early:
                    act.wait_ge(halves, 2 * g - 2)
                act.activation(xt[:, s, :, :].rearrange("p a b -> p (a b)"), bank(s),
                               ACT.Copy).then_inc(p_c.copied, 1)

            def gates_c(g, s, early):
                act.wait_ge(gate_ready, g + 1)
                v = out_gate[:, :, :].rearrange("p (g t) c -> p g (t c)", t=16)[:, bass.ds(g, 1), :]
                act.activation(v.rearrange("p a n -> p (a n)"), bank(6 + s), ACT.Sigmoid)\
                   .then_inc(gate_kept, 1)
                for h in range(2):
                    act.wait_ge(halves, 2 * g + h + 1)
                    if not (early and s == 0):
                        act.wait_ge(p_c.used, 2 * g + h - 1)
                    v = bank(2 + 2 * h, 2).rearrange("p (t h n) -> p t h n", h=2, n=2 * P)[:, :, 0, :]
                    act.activation(sg[:, h, :].rearrange("p (t n) -> p t n", n=2 * P), v,
                                   ACT.Sigmoid).then_inc(p_c.gates, 1)

            fused_act(act, n_c, copy_c, gates_c)

            def keep(q):
                act.wait_ge(f_prod, q + 1)
                act.activation(prod[:, 4 * P * q:4 * P * (q + 1)], bank(4 + q % 2),
                               ACT.Copy).then_inc(f_kept, 1)

            for q in range(8):
                act.wait_ge(f_turn, q + 1)
                act.activation(gated_t[:, 4 * q:4 * q + 4, :].rearrange("p a b -> p (a b)"), bank(q % 2),
                               ACT.Copy).then_inc(f_copy_a, 1)
                if q:
                    keep(q - 1)
            keep(7)
            fused_act(act, n_z, copy_group(act, p_z), nothing)


            def copy_d(g, s, early):
                act.wait_ge(p_d.turned, g + 1)
                v = xd.rearrange("p (g t) i -> p g (t i)", t=GROUP)[:, bass.ds(g, 1), :]
                act.activation(v.rearrange("p a n -> p (a n)"), bank(s), ACT.Copy).then_inc(p_d.copied, 1)

            def exp_d(q):
                act.wait_ge(chosen, STEPS * q + 2)
                act.activation(pr[:, q * QT:(q + 1) * QT, :], lg[:, q * QT:(q + 1) * QT, :],
                               ACT.Exp).then_inc(d_exp, 1)

            take_square(act, n_d, 0)
            take_root(act, n_d, 0)
            take_square(act, n_d, 1)
            take_root(act, n_d, 1)
            take_square(act, n_d, 2)
            copy_d(0, 0, True)
            copy_d(1, 1, True)
            take_square(act, n_d, 3)
            take_root(act, n_d, 2)
            copy_d(2, 0, False)
            take_root(act, n_d, 3)
            copy_d(3, 1, False)
            copy_d(4, 0, False)
            exp_d(0)
            for g in range(5, GROUPS):
                copy_d(g, g % 2, False)
            for q in range(1, QUARTERS):
                exp_d(q)


        @block.vector
        def _(dve):
            dve.memset(ones_b[:, :], 1.0)
            dve.memset(rows[:, :], 0.0)
            dve.memset(v_next[:, :], 0.0)
            dve.memset(v_wrap[:, :], 0.0)
            dve.memset(ends[:, :], 0.0)
            dve.memset(lhs_b[0:C, 4, :], 0.0)
            dve.memset(lhs_b[C:C + 1, :, :], 1.0)
            chain(dve, dve.memset(lhs_b[0:D2 + 1, 3, :], 1.0))

            def ln_weights(lo, hi, n):
                dve.tensor_copy(lhs_b[0:C, n, :], lnv[:, 2 * n + 1:2 * n + 2].to_broadcast([C, P]))
                return dve.tensor_scalar(raw_s[:, lo:hi], raw[0:C, lo:hi], lnv[:, 2 * n:2 * n + 1], None,
                                         ALU.mult)

            def x_ready(p):
                dve.wait_ge(ld_x[PIECES[p][0] // QT], 16)
                if p == 1:
                    dve.wait_ge(ld_a, 16 * len(weights_a()))
                    ln_weights(0, 64, 0).then_inc(a_scaled, 1)

            def build_a():
                dve.wait_ge(a_repeated, 2)
                dve.wait_ge(consts, 1)
                for h in range(2):
                    block_diag(dve, w_a[:, h, :, :], bank(6)[:, C * h:C * (h + 1)], blk4, S, C)
                dve.tensor_scalar(avg4[:, :], bank(7)[:, 0:P], 1.0 / S, None, ALU.mult)
                chain(dve, dve.tensor_copy(b_full[:, 0:64], bank(6)[:, 64:128]))
                split_rows(dve, chain, 0, 64)
                dve.tensor_copy(rows_a[:, :, :, :], rows[:, 0:64].rearrange("p (h o) -> p h o", h=2)
                                .unsqueeze(2).to_broadcast([P, 2, S, C])).then_inc(a_built, 1)


            def gate_a(g, s, early):
                dve.wait_ge(p_a.gates, g + 1)
                v = bank(2 + 2 * s, 2).rearrange("p (u h s o) -> p u h s o", u=4, h=2, s=S)[:, :, 0, :, :]
                o = gated[:, 0:C, :].rearrange("p o (g k) -> p g k o", k=16)[:, bass.ds(g, 1), :, :]
                o = o.rearrange("p a (u s) o -> p (a u) s o", s=S)
                dve.tensor_tensor(o, v, sg[:, s, :].rearrange("p (u s o) -> p u s o", u=4, s=S),
                                  ALU.mult).then_inc(p_a.used, 1)

            def scale_rest():
                dve.wait_ge(ld_w, 16 * len(weights()))
                dve.tensor_copy(raw_s[:, 256:NRAW], raw[0:C, 256:NRAW])
                dve.tensor_copy(lhs_b[0:D2, 3, :], lnv[0:D2, 7:8].to_broadcast([D2, P]))
                dve.tensor_scalar(raw_os[:, :], raw_o[0:D2, :], lnv[0:D2, 6:7], None, ALU.mult)
                ln_weights(64, 224, 1)
                ln_weights(224, 256, 2).then_inc(w_scaled, 1)

            fused_dve(dve, n_a, x, x_ready, scale_group(dve, p_a, C), gate_a, meanwhile=build_a,
                      late=scale_rest)
            for n, q in enumerate((1, 3)):
                dve.wait_ge(e_turn, q + 1)
                dve.tensor_copy(gated_t[:, 4 * q:4 * q + 4, :].rearrange("p a b -> p (a b)"),
                                bank((q + 1) % 4)).then_inc(e_copy_v, 1)
            dve.wait_ge(e_prod, 1)
            t_view = bank(4, 4).rearrange("p (d j) -> p j d", j=P)

            def gate_o(g, s, early):
                dve.wait_ge(p_o.gates, g + 1)
                v = bank(2 + 2 * s, 2).rearrange("p (u h n) -> p u h n", u=2, h=2)[:, :, 0, :]
                w = sg[:, s, :].rearrange("p (u n) -> p u n", u=2)
                dve.tensor_tensor(w, v, w, ALU.mult).then_inc(p_o.used, 1)

            fused_dve(dve, n_o, t_view, lambda p: None, scale_group(dve, p_o, D2), gate_o, centre=True)

            def x_added(q):
                dve.wait_ge(p_o.added, 2 * (q + 1))

            norm_dve(dve, n_b, x_q, x_added)

            def scale_b(g, s, early):
                if not early:
                    dve.wait_ge(p_b.turned, g - 1)
                src = centred[:, :].rearrange("p (s g t c) -> p g s t c", s=S, t=GROUP, c=C)
                r = rstd[:, :].rearrange("p (s g t) -> p g s t", s=S, t=GROUP)
                src = src[:, bass.ds(g, 1), :, :, :].rearrange("p a s t c -> p (a s) t c")
                r = r[:, bass.ds(g, 1), :, :].rearrange("p a s t -> p (a s) t")
                dve.tensor_tensor(xn[:, s, :, :].rearrange("p t (s c) -> p s t c", s=S), src,
                                  r.unsqueeze(3).to_broadcast([P, S, GROUP, C]), ALU.mult)\
                   .then_inc(p_b.scaled, 1)

            def stats_b(g, s, early):
                dve.wait_ge(p_b.projected, g + 1)
                dve.bn_stats(bst[:, bass.ds(g, 1), :].rearrange("p a n -> p (a n)"), bank(2 + s)).then_inc(p_b.used, 1)

            groups_ahead(dve, scale_b, stats_b)
            dve.wait_ge(w_kept, 1)
            dve.wait_ge(p_b.used, GROUPS)
            dve.bn_aggr(mv[:, :], bst[:, :, :].rearrange("p g n -> p (g n)")).then_inc(bn_dve, 1)
            dve.wait_ge(bn_pe, 1)
            chain(dve, dve.tensor_copy(bn[:, 0:1], bank(4)[:, 0:1]))
            chain(dve, dve.tensor_tensor(bn[:, 1:2], mv[:, 0:1], bn[:, 0:1], ALU.subtract))
            chain(dve, dve.tensor_tensor(bn[:, 1:2], bn[:, 1:2], bn[:, 1:2], ALU.mult))
            dve.tensor_tensor(bn[:, 2:3], mv[:, 1:2], bn[:, 1:2], ALU.add).then_inc(bn_dve, 1)
            dve.wait_ge(bn_pe, 2)
            dve.tensor_scalar(bn[:, 3:4], bank(4)[:, 0:1], EPS_LN, None, ALU.add).then_inc(bn_var, 1)
            dve.wait_ge(bn_act, 1)
            chain(dve, dve.reciprocal(bn[:, 5:6], bn[:, 4:5]))
            chain(dve, dve.tensor_tensor(bn[:, 6:7], bn[:, 5:6], bn[:, 5:6], ALU.mult))
            chain(dve, dve.scalar_tensor_tensor(bn[:, 6:7], bn[:, 6:7], -0.5, bn[:, 3:4], ALU.mult, ALU.mult))
            chain(dve, dve.scalar_tensor_tensor(bn[:, 7:8], bn[:, 6:7], 1.5, bn[:, 5:6], ALU.add, ALU.mult))
            chain(dve, dve.tensor_tensor(bn[:, 8:9], bn[:, 7:8], rep_w[:, 584:585], ALU.mult))
            dve.tensor_scalar(diag[:, :], ident[:, :], bn[:, 8:9], None, ALU.mult).then_inc(bn_dve, 1)
            chain(dve, dve.tensor_tensor(bn[:, 10:11], bn[:, 0:1], bn[:, 8:9], ALU.mult))
            dve.tensor_tensor(bn[:, 9:10], rep_w[:, 585:586], bn[:, 10:11], ALU.subtract).then_inc(bn_done, 1)
            dve.wait_ge(bn_pe, 3)
            dve.tensor_copy(w_bs[:, :], bank(4)[:, 0:P]).then_inc(bn_dve, 1)

            for st in range(2):
                dve.wait_ge(s_state[st], SWEPT)
            keep_ends(dve, ends_kept)
            for st in range(2):
                dve.wait_ge(s_state[st], SWEPT + CHUNK)
            dve.tensor_tensor(dif[:, 0:P], y_cm[:, 2 * CHUNK - 1, :], ends[:, 1:P + 1], ALU.subtract)
            chain(dve, dve.tensor_tensor(dif[:, P:2 * P], y_cm[:, CHUNK - 1, :], ends[:, P + 1:2 * P + 1],
                                         ALU.subtract))
            dve.tensor_reduce(dmax[:, :], dif[:, :], AX.X, ALU.max, apply_absolute_value=True)\
               .then_inc(ends_kept, 1)
            dve.wait_ge(flag_turned, 1)
            chain(dve, dve.tensor_reduce(flag[:, 0:1], bank(6)[0:1, 0:P], AX.X, ALU.max))
            chain(dve, dve.tensor_scalar(flag[:, 1:2], flag[:, 0:1], SAME, None, ALU.is_gt))
            dve.tensor_copy(flag_i[:, :], flag[:, 1:2]).then_inc(flag_set, 1)
            dve.wait_ge(flag_set, 1)
            again = dve.value_load(flag_i[0:1, 0:1], min_val=0, max_val=1)
            with dve.If(again > 0):
                keep_ends(dve, ends_again)
                with dve.Fori(1, NCHUNKS - 1) as n:
                    for st in range(2):
                        dve.wait_ge(r_state[st], n * CHUNK)
                    keep_ends(dve, ends_again)
                dve.wait_ge(y_again, GROUPS - 1)

            def add_y(q):
                dve.wait_ge(y_turn, GROUPS)
                v = ps[:, :].rearrange("p (k s c) -> p s k c", s=S, c=C)[:, q, :, :]
                dve.tensor_tensor(x_q(q), x_q(q), v, ALU.add).then_inc(y_added, 1)
                dve.wait_ge(y_added, q + 1)

            def y_ready(p):
                if p < 2:
                    add_y(p)

            def gate_c(g, s, early):
                for h in range(2):
                    dve.wait_ge(p_c.gates, 2 * g + h + 1)
                    v = bank(2 + 2 * h, 2).rearrange("p (u h s o) -> p u h s o", u=2, h=2, s=S)[:, :, 1, :, :]
                    o = gated[:, :, :].rearrange("p o (g k) -> p g k o", k=8)[:, bass.ds(2 * g + h, 1), :, :]
                    o = o.rearrange("p a (u s) o -> p (a u) s o", s=S)
                    dve.tensor_tensor(o, v, sg[:, h, :].rearrange("p (u s o) -> p u s o", u=2, s=S),
                                      ALU.mult).then_inc(p_c.used, 1)

            fused_dve(dve, n_c, x, y_ready, scale_group(dve, p_c, C), gate_c,
                      meanwhile=lambda: (add_y(2), add_y(3)))
            for q in range(8):
                dve.wait_ge(f_turn, q + 1)
                dve.tensor_copy(gated_t[:, C + 4 * q:C + 4 * q + 4, :].rearrange("p a b -> p (a b)"),
                                bank(2 + q % 2)).then_inc(f_copy_v, 1)

            def gate_z(g, s, early):
                dve.wait_ge(p_z.projected, g + 1)
                if not early:
                    dve.wait_ge(p_z.added, g - 1)
                v = out_gate[:, :, :].rearrange("p (g t) c -> p g (t c)", t=16)[:, bass.ds(g, 1), :]
                dve.tensor_tensor(sg[:, s, :], bank(2 + s), v.rearrange("p a n -> p (a n)"),
                                  ALU.mult).then_inc(p_z.used, 1)

            fused_dve(dve, n_z, prod_t, lambda p: dve.wait_ge(f_kept, 8), scale_group(dve, p_z, C), gate_z)

            def z_added(p):
                dve.wait_ge(p_z.added, PIECES[p][1] // 16)

            def mean_d(p):
                take_mean(dve, n_d, x, p, z_added, centre=p == 0)

            mean_d(0)
            mean_d(1)
            take_var(dve, n_d, 0)
            take_rstd(dve, n_d, 0)
            mean_d(2)
            take_var(dve, n_d, 1)
            take_rstd(dve, n_d, 1)
            mean_d(3)
            take_var(dve, n_d, 2)
            take_rstd(dve, n_d, 2)
            take_var(dve, n_d, 3)
            take_rstd(dve, n_d, 3)

            def choose(q, n):
                def of(t):
                    return t.rearrange("p (q j) e -> p q j e", q=QUARTERS)[:, bass.ds(q, 1), :, :]\
                        .rearrange("p a j e -> p (a j) e")

                def small(m):
                    return red[:, m, :].rearrange("p (q j) -> p q j", q=QUARTERS)[:, bass.ds(q, 1), :]\
                        .rearrange("p a j -> p (a j)")

                def each(m):
                    return bcast(small(m), EXPERTS)

                logits = bank(2, 2).rearrange("p (q j e) -> p q j e", q=QUARTERS, e=EXPERTS)\
                    [:, bass.ds(logits_at(q), 1), :, :].rearrange("p a j e -> p (a j) e")
                ranks = rank[:, :].unsqueeze(1).to_broadcast([P, QT, EXPERTS])
                if n == 0:
                    dve.wait_ge(d_logits, 1 if isinstance(q, int) and q == 0 else QUARTERS)
                else:
                    dve.wait_ge(chosen, STEPS * q + n)
                if n == 5:
                    dve.wait_ge(d_exp, q + 1)
                if n == 0:
                    ins = dve.tensor_reduce(small(0), logits, AX.X, ALU.max)
                elif n == 1:
                    ins = dve.tensor_tensor(of(lg), logits, each(0), ALU.subtract)
                elif n == 2:
                    ins = dve.scalar_tensor_tensor(of(eq), of(lg), 0.0, ranks, ALU.is_equal, ALU.mult)
                elif n == 3:
                    ins = dve.tensor_reduce(small(1), of(eq), AX.X, ALU.max)
                elif n == 4:
                    ins = dve.tensor_tensor(of(sel1), of(eq), each(1), ALU.is_equal)
                elif n == 5:
                    ins = dve.scalar_tensor_tensor(of(lg), of(sel1), -2.0, of(pr), ALU.mult, ALU.add)
                elif n == 6:
                    ins = dve.tensor_reduce(small(2), of(lg), AX.X, ALU.max)
                elif n == 7:
                    ins = dve.tensor_tensor(of(eq), of(lg), each(2), ALU.is_equal)
                elif n == 8:
                    ins = dve.tensor_tensor(of(eq), of(eq), ranks, ALU.mult)
                elif n == 9:
                    ins = dve.tensor_reduce(small(3), of(eq), AX.X, ALU.max)
                elif n == 10:
                    ins = dve.tensor_tensor(of(sel2), of(eq), each(3), ALU.is_equal)
                elif n == 11:
                    ins = dve.tensor_scalar(small(4), small(2), 1.0, None, ALU.add)
                elif n == 12:
                    ins = dve.reciprocal(small(5), small(4))
                elif n == 13:
                    ins = dve.tensor_tensor(of(sel2), of(sel2), of(pr), ALU.mult)
                elif n == 14:
                    ins = dve.tensor_tensor(of(sel1), of(sel1), of(sel2), ALU.add)
                else:
                    ins = dve.tensor_tensor(of(wgt), of(sel1), each(5), ALU.mult)
                ins.then_inc(chosen, 1)

            def weigh(u, s, early):
                dve.wait_ge(p_d.projected, u + 1)
                if not early:
                    dve.wait_ge(p_d.added, u - 1)
                w = wgt[:, :, :].rearrange("p (u s) e -> p u (s e)", s=S)[:, bass.ds(u, 1), :]
                w = w.rearrange("p a n -> p (a n)")
                dve.tensor_tensor(mixed[:, s, :, :, :].rearrange("p s e c -> p (s e) c"),
                                  bank(4 + 2 * s, 2).rearrange("p (n c) -> p n c", c=C),
                                  w.unsqueeze(2).to_broadcast([P, S * EXPERTS, C]), ALU.mult)\
                   .then_inc(weighed, 1)

            def first_sum(u, s):
                dve.wait_ge(weighed, u + 1)
                m = mixed[:, s, 0:S - POOL_SLOTS, :, :]
                h = EXPERTS // 2
                dve.tensor_tensor(m[:, :, 0:h, :], m[:, :, 0:h, :], m[:, :, h:EXPERTS, :],
                                  ALU.add).then_inc(p_d.used, 1)

            def weigh_quarter(q, first, last):
                for v in range(TILES // QUARTERS):
                    u = TILES // QUARTERS * q + v
                    weigh(u, v % 2, first and v < 2)
                    if not last:
                        choose(q + 1, 2 * v)
                    first_sum(u, v % 2)
                    if not last:
                        choose(q + 1, 2 * v + 1)

            for n in range(STEPS):
                choose(0, n)
            dve.wait_ge(chosen, STEPS)
            weigh_quarter(0, True, False)
            with dve.Fori(1, QUARTERS - 1) as q:
                dve.wait_ge(chosen, STEPS * q + STEPS)
                weigh_quarter(q, False, False)
            dve.wait_ge(chosen, STEPS * QUARTERS)
            weigh_quarter(QUARTERS - 1, False, True)


_INS = ["x", "L0_conv_mask", "L0_conv_ln1_w", "L0_conv_ln1_b", "L0_conv_pi_w", "L0_conv_pi_b", "L0_conv_gi_w",
        "L0_conv_gi_b", "L0_conv_ln2_w", "L0_conv_ln2_b", "L0_conv_po_w", "L0_conv_po_b", "L0_conv_go_w",
        "L0_conv_go_b", "L0_ffn_W", "L0_ffn_V", "L0_ffn_gamma", "L0_ffn_beta", "L1_conv_mask", "L1_conv_ln_in_w",
        "L1_conv_ln_in_b", "L1_conv_w_ap", "L1_conv_b_ap", "L1_conv_w_ag", "L1_conv_b_ag", "L1_conv_w_bp",
        "L1_conv_b_bp", "L1_conv_w_bg", "L1_conv_b_bg", "L1_conv_ln_out_w", "L1_conv_ln_out_b", "L1_conv_w_z",
        "L1_conv_b_z", "L1_conv_w_g", "L1_conv_b_g", "L1_ffn_router_w", "L1_ffn_router_b", "L1_ffn_expert_w",
        "L1_ffn_expert_b"]


def kernel(**inputs):
    import numpy as _np
    import concourse.bacc as _bacc
    from concourse import mybir as _mybir
    from concourse.bass_utils import run_bass_kernel_spmd as _run

    nc = _bacc.Bacc("TRN2", target_bir_lowering=False, num_devices=1)
    arrays, args = {}, {}
    for name in _INS:
        v = _np.ascontiguousarray(inputs[name])
        arrays[f"in_{name}_dram"] = v
        args[name] = nc.dram_tensor(f"in_{name}_dram", v.shape, _mybir.dt.from_np(v.dtype),
                                    kind="ExternalInput").ap()
    out = nc.dram_tensor("out_0_dram", (1, P, P, C), _mybir.dt.float32, kind="ExternalOutput").ap()
    build(nc, args, out)
    r = _run(nc, [arrays], core_ids=[0])
    return r.results[0]["out_0_dram"]
```
